# Optimizing a Trainium2 kernel written in Bass

```python
import numpy as np
import jax
import jax.numpy as jnp

def _softmax(x, axis=-1):
    return jax.nn.softmax(x, axis=axis)

def _gelu(x):
    return jax.nn.gelu(x, approximate=True)

def _silu(x):
    return jax.nn.silu(x)

def _sigmoid(x):
    return jax.nn.sigmoid(x)

def _layernorm(x, axis=-1, eps=1e-05):
    m = jnp.mean(x, axis=axis, keepdims=True)
    v = jnp.var(x, axis=axis, keepdims=True)
    return (x - m) / jnp.sqrt(v + eps)

def _scatter_add(tgt, idx, src, axis=0):
    return tgt.at[idx].add(src)

def _segment_sum(src, seg, n):
    return jax.ops.segment_sum(src, seg, n)
kernel_name = 'mk_decoder_preln_d1_seqx_r8_14d6cb'

def setup_inputs(seed: int=0):
    np.random.seed(seed)
    _w = jnp.asarray

    def _rec_inputs():
        import jax
        import jax.numpy as jnp
        _rk = jax.random.key(seed)
        x = 7.22e-05 + 1 * jax.random.normal(jax.random.fold_in(_rk, 1), (8, 128, 256), jnp.float32)
        _lenS = 128 - jax.random.randint(jax.random.fold_in(_rk, 7), (8,), 0, max(1, 128 // 4) + 1, jnp.int32)
        _lenS2 = 128 - jax.random.randint(jax.random.fold_in(_rk, 8), (8,), 0, max(1, 128 // 4) + 1, jnp.int32)
        _ctx_2048P = jax.random.normal(jax.random.fold_in(_rk, 11), (8, 16, 256), jnp.float32)
        _ctx_2048c = jax.random.dirichlet(jax.random.fold_in(_rk, 511), 0.3 * jnp.ones((16,), jnp.float32), (8, 128))
        _ctx_2048t = jnp.einsum('bsk,bkd->bsd', _ctx_2048c, _ctx_2048P)
        _ctx_2048t = _ctx_2048t * jax.lax.rsqrt(jnp.mean(jnp.square(_ctx_2048t)) + 1e-12) * 0.953939
        ctx_2048 = 4.13588e-05 + 0.999923 * (_ctx_2048t + 0.3 * jax.random.normal(jax.random.fold_in(_rk, 611), (8, 128, 256), jnp.float32))
        return (x, ctx_2048)
    x, ctx_2048 = _rec_inputs()

    def _L0_attn_setup():
        import jax, jax.numpy as jnp
        import numpy as np
        D_MODEL = 256
        N_HEADS = 16
        ROPE_HEADS = 2
        DH = D_MODEL // N_HEADS
        DIM_HEADS = N_HEADS - ROPE_HEADS
        Q_PROJ = D_MODEL // 2
        KV_PROJ = 2 * D_MODEL // 3
        Q_NOPE = DIM_HEADS * DH
        Q_ROPE = ROPE_HEADS * DH
        K_NOPE = DIM_HEADS * DH
        K_ROPE = ROPE_HEADS * DH
        THETA = 10000.0
        LN_EPS = 1e-05
        B, S = (2, 256)

        def _layernorm(x, w, b):
            m = jnp.mean(x, -1, keepdims=True)
            v = jnp.var(x, -1, keepdims=True)
            return (x - m) * jax.lax.rsqrt(v + LN_EPS) * w + b

        def _rope_tables(seq):
            freqs = 1.0 / THETA ** (jnp.arange(0, DH, 2, dtype=jnp.float32) / DH)
            ang = jnp.arange(seq, dtype=jnp.float32)[:, None] * freqs[None, :]
            cos = jnp.concatenate([jnp.cos(ang), jnp.cos(ang)], -1)
            sin = jnp.concatenate([jnp.sin(ang), jnp.sin(ang)], -1)
            return (cos, sin)

        def _apply_rope(x, cos, sin):
            x1, x2 = jnp.split(x, 2, axis=-1)
            rot = jnp.concatenate([-x2, x1], -1)
            return x * cos + rot * sin

        def _reference_tuple_inner(x, W_dq, W_uq, W_qr, W_dkv, W_ukv, W_kr, W_o, q_ln_w, q_ln_b, kv_ln_w, kv_ln_b):
            Bsz, Sq, D = x.shape
            cq = _layernorm(x @ W_dq, q_ln_w, q_ln_b)
            Q = (cq @ W_uq).reshape(Bsz, Sq, DIM_HEADS, DH).transpose(0, 2, 1, 3)
            Qr = (cq @ W_qr).reshape(Bsz, Sq, ROPE_HEADS, DH).transpose(0, 2, 1, 3)
            cos, sin = _rope_tables(Sq)
            Qr = _apply_rope(Qr, cos, sin)
            ckv = _layernorm(x @ W_dkv, kv_ln_w, kv_ln_b)
            KV = ckv @ W_ukv
            Kn = KV[..., :K_NOPE].reshape(Bsz, Sq, DIM_HEADS, DH).transpose(0, 2, 1, 3)
            V = KV[..., K_NOPE:].reshape(Bsz, Sq, N_HEADS, DH).transpose(0, 2, 1, 3)
            Kr = (x @ W_kr).reshape(Bsz, Sq, ROPE_HEADS, DH).transpose(0, 2, 1, 3)
            Kr = _apply_rope(Kr, cos, sin)
            q = jnp.concatenate([Q, Qr], axis=1)
            k = jnp.concatenate([Kn, Kr], axis=1)
            scores = jnp.einsum('bhqd,bhkd->bhqk', q, k) / jnp.sqrt(jnp.float32(DH))
            mask = jnp.tril(jnp.ones((Sq, Sq), bool))
            scores = jnp.where(mask[None, None], scores, -jnp.inf)
            attn = jax.nn.softmax(scores, axis=-1)
            out = jnp.einsum('bhqk,bhkd->bhqd', attn, V)
            out = out.transpose(0, 2, 1, 3).reshape(Bsz, Sq, D)
            out = out @ W_o.T
            return (out, ckv)
        key = jax.random.key(seed)
        ks = jax.random.split(key, 8)
        p = lambda k, shape: 0.01 * jax.random.normal(k, shape, dtype=jnp.float32)
        return {'x': jax.random.normal(ks[0], (B, S, D_MODEL), dtype=jnp.float32), 'W_dq': p(ks[1], (D_MODEL, Q_PROJ)), 'W_uq': p(ks[2], (Q_PROJ, Q_NOPE)), 'W_qr': p(ks[3], (Q_PROJ, Q_ROPE)), 'W_dkv': p(ks[4], (D_MODEL, KV_PROJ)), 'W_ukv': p(ks[5], (KV_PROJ, D_MODEL + K_NOPE)), 'W_kr': p(ks[6], (D_MODEL, K_ROPE)), 'W_o': p(ks[7], (D_MODEL, D_MODEL)), 'q_ln_w': jnp.ones((Q_PROJ,), jnp.float32), 'q_ln_b': jnp.zeros((Q_PROJ,), jnp.float32), 'kv_ln_w': jnp.ones((KV_PROJ,), jnp.float32), 'kv_ln_b': jnp.zeros((KV_PROJ,), jnp.float32)}
    _L0_attn_all = _L0_attn_setup()
    _L0_attn_in = {k: v for k, v in _L0_attn_all.items() if k in ('W_dq', 'W_uq', 'W_qr', 'W_dkv', 'W_ukv', 'W_kr', 'W_o', 'q_ln_w', 'q_ln_b', 'kv_ln_w', 'kv_ln_b')}
    del _L0_attn_all

    def _L0_xattn_setup():
        import jax, jax.numpy as jnp
        import numpy as np
        B, S, DIM, HD = (4, 128, 256, 128)
        H = DIM // HD
        GN_EPS = 0.001

        def _decay_masks(n_heads, seq_len):
            gam = 1.0 - 2.0 ** (-5.0 - jnp.arange(n_heads, dtype=jnp.float32))
            idx = jnp.arange(seq_len, dtype=jnp.float32)
            expo = idx[None, :] - idx[:, None]
            D = jnp.where(expo[None, :, :] <= 0, gam[:, None, None] ** expo[None, :, :], 0.0)
            return D / jnp.sqrt(D.sum(axis=-1))[:, None, :]
        key = jax.random.key(seed)
        ks = jax.random.split(key, 8)
        x = jax.random.normal(ks[0], (B, S, DIM), dtype=jnp.float32)
        k = jax.random.normal(ks[1], (B, S, DIM), dtype=jnp.float32)
        v = jax.random.normal(ks[2], (B, S, DIM), dtype=jnp.float32)
        Wh = jax.random.normal(ks[3], (H, HD, HD), dtype=jnp.float32) / np.sqrt(HD)
        wg_w = jax.random.normal(ks[4], (DIM, DIM), dtype=jnp.float32) / np.sqrt(DIM)
        wo_w = jax.random.normal(ks[5], (DIM, DIM), dtype=jnp.float32) / np.sqrt(DIM)
        gn_gamma = jnp.ones((DIM,), dtype=jnp.float32)
        gn_beta = jnp.zeros((DIM,), dtype=jnp.float32)
        return {'x': x, 'k': k, 'v': v, 'Wh': Wh, 'wg_w': wg_w, 'wo_w': wo_w, 'gn_gamma': gn_gamma, 'gn_beta': gn_beta}
    _L0_xattn_all = _L0_xattn_setup()
    _L0_xattn_in = {k: v for k, v in _L0_xattn_all.items() if k in ('Wh', 'wg_w', 'wo_w', 'gn_gamma', 'gn_beta')}
    del _L0_xattn_all

    def _L0_ffn_setup():
        import jax, jax.numpy as jnp
        import numpy as np
        H = 256
        I = 176
        E = 16
        K = 2
        SI = I * 2

        def _swiglu(gu, inter):
            g, u = (gu[..., :inter], gu[..., inter:])
            return jax.nn.silu(g) * u
        key = jax.random.key(seed)
        ks = jax.random.split(key, 6)
        s = 0.02
        hidden_states = jax.random.normal(ks[0], (1, 128, H), dtype=jnp.float32)
        gate_w = jax.random.normal(ks[1], (E, H), dtype=jnp.float32) * s
        w_gate_up = jax.random.normal(ks[2], (E, H, 2 * I), dtype=jnp.float32) * s
        w_down = jax.random.normal(ks[3], (E, I, H), dtype=jnp.float32) * s
        shared_gate_up = jax.random.normal(ks[4], (H, 2 * SI), dtype=jnp.float32) * s
        shared_down = jax.random.normal(ks[5], (SI, H), dtype=jnp.float32) * s
        return {'hidden_states': hidden_states, 'gate_w': gate_w, 'w_gate_up': w_gate_up, 'w_down': w_down, 'shared_gate_up': shared_gate_up, 'shared_down': shared_down}
    _L0_ffn_all = _L0_ffn_setup()
    _L0_ffn_in = {k: v for k, v in _L0_ffn_all.items() if k in ('gate_w', 'w_gate_up', 'w_down', 'shared_gate_up', 'shared_down')}
    del _L0_ffn_all
    return {'x': x, 'ctx_2048': ctx_2048, 'L0_attn_W_dq': _L0_attn_in['W_dq'], 'L0_attn_W_uq': _L0_attn_in['W_uq'], 'L0_attn_W_qr': _L0_attn_in['W_qr'], 'L0_attn_W_dkv': _L0_attn_in['W_dkv'], 'L0_attn_W_ukv': _L0_attn_in['W_ukv'], 'L0_attn_W_kr': _L0_attn_in['W_kr'], 'L0_attn_W_o': _L0_attn_in['W_o'], 'L0_attn_q_ln_w': _L0_attn_in['q_ln_w'], 'L0_attn_q_ln_b': _L0_attn_in['q_ln_b'], 'L0_attn_kv_ln_w': _L0_attn_in['kv_ln_w'], 'L0_attn_kv_ln_b': _L0_attn_in['kv_ln_b'], 'L0_xattn_Wh': _L0_xattn_in['Wh'], 'L0_xattn_wg_w': _L0_xattn_in['wg_w'], 'L0_xattn_wo_w': _L0_xattn_in['wo_w'], 'L0_xattn_gn_gamma': _L0_xattn_in['gn_gamma'], 'L0_xattn_gn_beta': _L0_xattn_in['gn_beta'], 'L0_ffn_gate_w': _L0_ffn_in['gate_w'], 'L0_ffn_w_gate_up': _L0_ffn_in['w_gate_up'], 'L0_ffn_w_down': _L0_ffn_in['w_down'], 'L0_ffn_shared_gate_up': _L0_ffn_in['shared_gate_up'], 'L0_ffn_shared_down': _L0_ffn_in['shared_down']}

def reference(x, ctx_2048, L0_attn_W_dq, L0_attn_W_uq, L0_attn_W_qr, L0_attn_W_dkv, L0_attn_W_ukv, L0_attn_W_kr, L0_attn_W_o, L0_attn_q_ln_w, L0_attn_q_ln_b, L0_attn_kv_ln_w, L0_attn_kv_ln_b, L0_xattn_Wh, L0_xattn_wg_w, L0_xattn_wo_w, L0_xattn_gn_gamma, L0_xattn_gn_beta, L0_ffn_gate_w, L0_ffn_w_gate_up, L0_ffn_w_down, L0_ffn_shared_gate_up, L0_ffn_shared_down):
    import jax
    import jax.numpy as jnp

    def _L0_attn_ref(x, W_dq, W_uq, W_qr, W_dkv, W_ukv, W_kr, W_o, q_ln_w, q_ln_b, kv_ln_w, kv_ln_b):
        import jax, jax.numpy as jnp
        import numpy as np
        D_MODEL = 256
        N_HEADS = 16
        ROPE_HEADS = 2
        DH = D_MODEL // N_HEADS
        DIM_HEADS = N_HEADS - ROPE_HEADS
        Q_PROJ = D_MODEL // 2
        KV_PROJ = 2 * D_MODEL // 3
        Q_NOPE = DIM_HEADS * DH
        Q_ROPE = ROPE_HEADS * DH
        K_NOPE = DIM_HEADS * DH
        K_ROPE = ROPE_HEADS * DH
        THETA = 10000.0
        LN_EPS = 1e-05
        B, S = (2, 256)

        def _layernorm(x, w, b):
            m = jnp.mean(x, -1, keepdims=True)
            v = jnp.var(x, -1, keepdims=True)
            return (x - m) * jax.lax.rsqrt(v + LN_EPS) * w + b

        def _rope_tables(seq):
            freqs = 1.0 / THETA ** (jnp.arange(0, DH, 2, dtype=jnp.float32) / DH)
            ang = jnp.arange(seq, dtype=jnp.float32)[:, None] * freqs[None, :]
            cos = jnp.concatenate([jnp.cos(ang), jnp.cos(ang)], -1)
            sin = jnp.concatenate([jnp.sin(ang), jnp.sin(ang)], -1)
            return (cos, sin)

        def _apply_rope(x, cos, sin):
            x1, x2 = jnp.split(x, 2, axis=-1)
            rot = jnp.concatenate([-x2, x1], -1)
            return x * cos + rot * sin

        def _reference_tuple_inner(x, W_dq, W_uq, W_qr, W_dkv, W_ukv, W_kr, W_o, q_ln_w, q_ln_b, kv_ln_w, kv_ln_b):
            Bsz, Sq, D = x.shape
            cq = _layernorm(x @ W_dq, q_ln_w, q_ln_b)
            Q = (cq @ W_uq).reshape(Bsz, Sq, DIM_HEADS, DH).transpose(0, 2, 1, 3)
            Qr = (cq @ W_qr).reshape(Bsz, Sq, ROPE_HEADS, DH).transpose(0, 2, 1, 3)
            cos, sin = _rope_tables(Sq)
            Qr = _apply_rope(Qr, cos, sin)
            ckv = _layernorm(x @ W_dkv, kv_ln_w, kv_ln_b)
            KV = ckv @ W_ukv
            Kn = KV[..., :K_NOPE].reshape(Bsz, Sq, DIM_HEADS, DH).transpose(0, 2, 1, 3)
            V = KV[..., K_NOPE:].reshape(Bsz, Sq, N_HEADS, DH).transpose(0, 2, 1, 3)
            Kr = (x @ W_kr).reshape(Bsz, Sq, ROPE_HEADS, DH).transpose(0, 2, 1, 3)
            Kr = _apply_rope(Kr, cos, sin)
            q = jnp.concatenate([Q, Qr], axis=1)
            k = jnp.concatenate([Kn, Kr], axis=1)
            scores = jnp.einsum('bhqd,bhkd->bhqk', q, k) / jnp.sqrt(jnp.float32(DH))
            mask = jnp.tril(jnp.ones((Sq, Sq), bool))
            scores = jnp.where(mask[None, None], scores, -jnp.inf)
            attn = jax.nn.softmax(scores, axis=-1)
            out = jnp.einsum('bhqk,bhkd->bhqd', attn, V)
            out = out.transpose(0, 2, 1, 3).reshape(Bsz, Sq, D)
            out = out @ W_o.T
            return (out, ckv)
        return _reference_tuple_inner(x, W_dq, W_uq, W_qr, W_dkv, W_ukv, W_kr, W_o, q_ln_w, q_ln_b, kv_ln_w, kv_ln_b)[0]

    def _L0_xattn_ref(x, k, v, Wh, wg_w, wo_w, gn_gamma, gn_beta):
        import jax, jax.numpy as jnp
        import numpy as np
        B, S, DIM, HD = (4, 128, 256, 128)
        H = DIM // HD
        GN_EPS = 0.001

        def _decay_masks(n_heads, seq_len):
            gam = 1.0 - 2.0 ** (-5.0 - jnp.arange(n_heads, dtype=jnp.float32))
            idx = jnp.arange(seq_len, dtype=jnp.float32)
            expo = idx[None, :] - idx[:, None]
            D = jnp.where(expo[None, :, :] <= 0, gam[:, None, None] ** expo[None, :, :], 0.0)
            return D / jnp.sqrt(D.sum(axis=-1))[:, None, :]
        b, s, dim = x.shape
        h, hd, _ = Wh.shape
        xh = x.reshape(b, s, h, hd)
        kh = k.reshape(b, s, h, hd)
        vh = v.reshape(b, s, h, hd)
        Q = jnp.einsum('bshd,hde->bshe', xh, Wh)
        K = jnp.einsum('bshd,hde->bshe', kh, Wh)
        V = jnp.einsum('bshd,hde->bshe', vh, Wh)
        scores = jnp.einsum('bshe,bthe->bhst', Q, K) / jnp.sqrt(jnp.float32(hd))
        Dn = _decay_masks(h, s)
        masked = scores * Dn[None, :, :, :]
        A = jnp.maximum(jnp.abs(masked.sum(axis=0)), 1.0)
        O = jnp.einsum('hst,bthe->bshe', A, V).reshape(b, s, dim)
        mu = O.mean(axis=-1, keepdims=True)
        var = O.var(axis=-1, keepdims=True)
        Y = (O - mu) / jnp.sqrt(var + GN_EPS) * gn_gamma + gn_beta
        W = jax.nn.relu(x @ wg_w)
        return W * Y @ wo_w

    def _L0_ffn_ref(hidden_states, gate_w, w_gate_up, w_down, shared_gate_up, shared_down):
        import jax, jax.numpy as jnp
        import numpy as np
        H = 256
        I = 176
        E = 16
        K = 2
        SI = I * 2

        def _swiglu(gu, inter):
            g, u = (gu[..., :inter], gu[..., inter:])
            return jax.nn.silu(g) * u
        orig_shape = hidden_states.shape
        x = hidden_states.reshape(-1, H)
        logits = jnp.einsum('th,eh->te', x, gate_w)
        scores = jax.nn.softmax(logits, axis=-1)
        topk_w, topk_idx = jax.lax.top_k(scores, K)
        combine = jnp.sum(jax.nn.one_hot(topk_idx, E, dtype=x.dtype) * topk_w[..., None], axis=1)
        gu = jnp.einsum('th,ehj->etj', x, w_gate_up)
        h = _swiglu(gu, I)
        y = jnp.einsum('eti,eih,te->th', h, w_down, combine)
        gu_s = x @ shared_gate_up
        y = y + _swiglu(gu_s, SI) @ shared_down
        return y.reshape(orig_shape)
    x = x + _L0_attn_ref(_layernorm(x, axis=-1), L0_attn_W_dq, L0_attn_W_uq, L0_attn_W_qr, L0_attn_W_dkv, L0_attn_W_ukv, L0_attn_W_kr, L0_attn_W_o, L0_attn_q_ln_w, L0_attn_q_ln_b, L0_attn_kv_ln_w, L0_attn_kv_ln_b)
    x = x + _L0_xattn_ref(_layernorm(x, axis=-1), ctx_2048, ctx_2048, L0_xattn_Wh, L0_xattn_wg_w, L0_xattn_wo_w, L0_xattn_gn_gamma, L0_xattn_gn_beta)
    x = x + _L0_ffn_ref(_layernorm(x, axis=-1), L0_ffn_gate_w, L0_ffn_w_gate_up, L0_ffn_w_down, L0_ffn_shared_gate_up, L0_ffn_shared_down)
    return x

_drawn_inputs = setup_inputs


def setup_inputs(seed=0):
    import zlib

    import numpy as np

    out = dict(_drawn_inputs(seed))
    spreads = {'L0_attn_q_ln_w': (1.0, 0.6),
     'L0_attn_q_ln_b': (0.0, 0.8),
     'L0_attn_kv_ln_w': (1.0, 0.6),
     'L0_attn_kv_ln_b': (0.0, 0.8),
     'L0_xattn_gn_gamma': (1.0, 0.2),
     'L0_xattn_gn_beta': (0.0, 0.1)}
    factors = {'L0_attn_W_dq': 8.0,
     'L0_attn_W_uq': 8.0,
     'L0_attn_W_qr': 8.0,
     'L0_attn_W_dkv': 8.0,
     'L0_attn_W_ukv': 8.0,
     'L0_attn_W_kr': 8.0,
     'L0_attn_W_o': 8.0,
     'L0_ffn_gate_w': 8.0,
     'L0_ffn_w_gate_up': 8.0,
     'L0_ffn_w_down': 8.0,
     'L0_ffn_shared_gate_up': 3.526,
     'L0_ffn_shared_down': 3.541}
    for name, (base, spread) in spreads.items():
        noise = np.random.default_rng([zlib.crc32(name.encode()), seed]).standard_normal(out[name].shape)
        drawn = base * np.exp(spread * noise) if base else spread * noise
        out[name] = jnp.asarray(drawn.astype(out[name].dtype))
    for name, factor in factors.items():
        out[name] = (out[name] * factor).astype(out[name].dtype)
    return out
```

```python
import numpy as np
import concourse.bass as bass
from concourse import mybir
from contextlib import ExitStack

T = 128
B = 8
D = 256
KD = D // 128
H, DH = 16, 16
HN = 14
NOPE = HN * DH
ROPE = (H - HN) * DH
QP = D // 2
KP = 2 * D // 3
KPH = KP // 2
MW = QP + KP + 2 * ROPE
QW = D + ROPE
CH = 4
NC = H // CH
HD = 128
XH = D // HD
E = 16
I = 176
IH = I // 2
SI = 2 * I
SLOTS = 2 * B * T
BLOCKS = (SLOTS + E * (T - 1)) // T
LN_EPS, GN_EPS = 1e-5, 1e-3
MASKED = -1e30

C_ID, C_MASK, C_ROPE, C_HEAD, C_DECAY = 0, 128, 256, 256 + 4 * DH, 256 + 4 * DH + 8
C_TRI = C_DECAY + XH * T
C_THR = C_TRI + 128
C_IOTA = C_THR + B
C_LOW = C_IOTA + E
C_BLK = C_LOW + E * E
C_N = C_BLK + BLOCKS


def constants():
    c = np.zeros((128, C_N), np.float32)
    p = np.arange(128)
    c[:, C_ID:C_ID + 128] = np.eye(128)
    c[:, C_MASK:C_MASK + 128] = np.where(p[None, :] <= p[:, None], 0.0, MASKED)
    freqs = (1.0 / 10000.0 ** (np.arange(0, DH, 2, dtype=np.float32) / DH)).astype(np.float32)
    ang = p.astype(np.float32)[:, None] * freqs[None, :]
    cos, sin = np.cos(ang), np.sin(ang)
    c[:, C_ROPE:C_ROPE + 4 * DH] = np.concatenate([cos, cos, cos, cos, -sin, sin, -sin, sin], 1)
    c[:, C_HEAD:C_HEAD + 8] = p[:, None] // DH == np.arange(8)[None, :]
    for h in range(XH):
        expo = (p[None, :] - p[:, None]).astype(np.float64)
        decay = np.where(expo <= 0, (1.0 - 2.0 ** (-5.0 - h)) ** expo, 0.0)
        decay = decay / np.sqrt(decay.sum(-1))[None, :] / np.sqrt(float(HD))
        c[:, C_DECAY + h * T:C_DECAY + (h + 1) * T] = decay.T
    c[:, C_TRI:C_TRI + 128] = p[:, None] < p[None, :]
    c[:, C_THR:C_THR + B] = 128.0 * np.arange(B)
    c[:, C_IOTA:C_IOTA + E] = np.arange(E)
    c[:, C_LOW:C_LOW + E * E] = (np.arange(E)[None, :] < np.arange(E)[:, None]).reshape(1, -1)
    c[:, C_BLK:C_BLK + BLOCKS] = np.arange(BLOCKS)
    return c


def decoder_layer(nc, x, ctx_in, table, w_m, w_q, w_kv, w_out, ln_q, ln_kv, wh, wg, wo, gn,
                  gate, w_gu, w_dn, s_gu_d, s_dn_d, out):
    f32, bf16, i32 = mybir.dt.float32, mybir.dt.bfloat16, mybir.dt.int32
    ALU, ACT, AX = mybir.AluOpType, mybir.ActivationFunctionType, mybir.AxisListType

    ctx = ExitStack()
    with ctx:
        def sb(name, shape, dt=f32):
            return ctx.enter_context(nc.sbuf_tensor(name, shape, dt))

        def sem(name):
            return ctx.enter_context(nc.semaphore(name))

        slots_x = nc.dram_tensor("slots_x", [BLOCKS * T, D], f32).ap()
        slots_y = nc.dram_tensor("slots_y", [BLOCKS * T, D], f32).ap()

        tab = sb("tab", [128, C_N])
        idf = tab[:, C_ID:C_ID + 128]
        idb = sb("idb", [128, 128], bf16)
        maskb = sb("maskb", [128, 128], bf16)
        trib = sb("trib", [128, 128], bf16)
        onesb = sb("onesb", [128, 128], bf16)
        halfpow = sb("halfpow", [128, 2])
        wm_s = sb("wm_s", [128, KD, MW])
        wq_s = sb("wq_s", [128, QW])
        wkv_s = sb("wkv_s", [KPH, 2, NOPE + D])
        wout_s = sb("wout_s", [128, KD, D])
        lnq_s = sb("lnq_s", [128, 2])
        lnkv_s = sb("lnkv_s", [KPH, 2, 2])
        wh_s = sb("wh_s", [128, XH, HD])
        wg_s = sb("wg_s", [128, KD, D])
        wo_s = sb("wo_s", [128, KD, D])
        gn_s = sb("gn_s", [128, KD, 2])
        gate_s = sb("gate_s", [128, KD, E])
        gu_s = sb("gu_s", [128, KD, E, 2 * I])
        dn_s = sb("dn_s", [IH, 2, E, D])
        sgu_s = sb("sgu_s", [128, KD, 2 * SI])
        x_s = sb("x_s", [128, B, D])
        x1_s = sb("x1_s", [128, B, D])
        qw_s = sb("qw_s", [128, B, 4, T])
        ck_s = sb("ck_s", [128, XH, B, T])
        cv_s = sb("cv_s", [128, B, XH, HD])
        kbd = sb("kbd", [128, 2, 2, 8, T])
        xh = sb("xh", [128, 2, D])
        xT = sb("xT", [128, 2, KD, T])
        lat = sb("lat", [128, 2, QP + KP])
        cqT = sb("cqT", [128, 2, T])
        ckvT = sb("ckvT", [KPH, 2, 2, T])
        qk = sb("qk", [128, 2, 2 * D])
        rope_t = sb("rope_t", [128, 2, 2, 2 * ROPE])
        v_s = sb("v_s", [128, 2, H, DH + 1])
        qkT = sb("qkT", [128, 2, 4, T])
        mx = sb("mx", [128, 2, CH])
        sc_s = sb("sc_s", [128, 2, CH, T])
        pr_s = sb("pr_s", [128, 2, CH, T])
        prT = sb("prT", [128, 2, CH, T])
        rden = sb("rden", [128, 2, H])
        o_s = sb("o_s", [128, 2, D])
        oT = sb("oT", [128, 2, KD, T])
        xb = sb("xb", [128, 2, D])
        xbT = sb("xbT", [128, 2, KD, T])
        zeros = qw_s[:, B - 1, :, :].rearrange("p k t -> p (k t)")[:, 0:D]
        cs = qw_s[:].rearrange("p b k t -> p (b k t)")[:, 0:B * D].rearrange("p (b d) -> p b d", b=B)
        cT = pr_s[:].rearrange("p r h t -> p (r h t)").rearrange("p (h j t) -> p h j t", h=XH, j=4)
        st = sb("st", [128, 2, 6])
        ag = sb("ag", [128, 5, 2, 2])
        ve = sb("ve", [128, 5, 2, 1])
        rs = sb("rs", [128, 5, 2, 1])
        ag2 = sb("ag2", [128, 2, 2, 2])
        ve2 = sb("ve2", [128, 2, 2])
        rs2 = sb("rs2", [128, 2, 2])
        LX, LX1, LO, LX2 = range(4)

        bank = [ctx.enter_context(nc.psum_tensor(f"bank{i}", [128, 512], f32)) for i in range(8)]

        NX = 3
        XPARTS = [(0, 1), (1, 3), (3, 8)]
        s_x = [sem(f"s_x{i}") for i in range(NX)]
        s_tab, s_wm, s_wq, s_wkv, s_lnv, s_wout, s_ctx0, s_ctx1, s_wh, s_wgo, s_gate, s_shw, s_gu, s_dn = [
            sem(n) for n in "s_tab s_wm s_wq s_wkv s_lnv s_wout s_ctx0 s_ctx1 s_wh s_wgo s_gate s_shw s_gu s_dn".split()]
        s_zero, s_zfill = sem("s_zero"), sem("s_zfill")
        c_bf, c_set = sem("c_bf"), sem("c_set")
        p_t1, p_m1, p_t2, p_kv, p_q, p_t3, p_s, p_pt, p_pv, p_t5, p_wo, p_bt, p_bqw, p_sc = [
            sem(n) for n in "p_t1 p_m1 p_t2 p_kv p_q p_t3 p_s p_pt p_pv p_t5 p_wo p_bt p_bqw p_sc".split()]
        p_ct, p_ck, p_cv = sem("p_ct"), sem("p_ck"), sem("p_cv")
        chain = sem("chain")
        v_xv, v_xh, v_q, v_sb, v_x1, v_x1v, v_xb, v_mv, v_lat, v_on = [
            sem(n) for n in "v_xv v_xh v_q v_sb v_x1 v_x1v v_xb v_mv v_lat v_on".split()]
        a_exp, a_kv, a_ot, a_xT, a_qkT, a_prT, a_bt, a_qw, a_lat, a_ct, a_ck, a_cv = [
            sem(n) for n in "a_exp a_kv a_ot a_xT a_qkT a_prT a_bt a_qw a_lat a_ct a_ck a_cv".split()]
        g_x, g_m, g_x1, g_kbd = [sem(n) for n in "g_x g_m g_x1 g_kbd".split()]
        v_at, p_o, v_ov, g_o, v_yh, p_ty, a_ty, v_z, p_xo, v_x2v, g_x2, v_xf, p_tf, a_tf, p_lg = [
            sem(n) for n in "v_at p_o v_ov g_o v_yh p_ty a_ty v_z p_xo v_x2v g_x2 v_xf p_tf a_tf p_lg".split()]
        v_x2 = sem("v_x2")
        v_lg, a_re, v_top, p_rk, v_pos, v_blk = [sem(n) for n in "v_lg a_re v_top p_rk v_pos v_blk".split()]
        d_sc = sem("d_sc")
        p_sg, a_sg, v_sh, p_sT, a_sT, p_sd, v_sd = [sem(n) for n in "p_sg a_sg v_sh p_sT a_sT p_sd v_sd".split()]
        d_xs = [sem("d_xs0"), sem("d_xs1")]
        d_ys = [sem("d_ys0"), sem("d_ys1")]
        p_bT, v_bT, p_gu, a_si, v_h, p_hT, a_hT, p_dn, v_y = [
            sem(n) for n in "p_bT v_bT p_gu a_si v_h p_hT a_hT p_dn v_y".split()]
        d_g = [sem(f"d_g{i}") for i in range(4)]
        v_f1, d_out = sem("v_f1"), sem("d_out")

        def carve(t, cols):
            flat, at = t
            t[1] = at + cols
            return flat[:, at:at + cols]

        scr = [sc_s[:].rearrange("p r h t -> p (r h t)"), 0]
        prr = [pr_s[:].rearrange("p r h t -> p (r h t)"), 0]
        ptr = [prT[:].rearrange("p r h t -> p (r h t)"), 0]
        qtr = [qkT[:].rearrange("p r h t -> p (r h t)"), 0]
        qkr = [qk[:].rearrange("p r t -> p (r t)"), 0]
        aT = carve(scr, XH * T).rearrange("p (h t) -> p h t", h=XH)
        atmp = carve(scr, XH * T).rearrange("p (h t) -> p h t", h=XH)
        yh = xh
        yT = xT
        zT = oT
        xfT = ck_s
        lg = carve(qtr, B * E).rearrange("p (t e) -> p t e", t=B)
        ex = carve(qtr, B * E).rearrange("p (t e) -> p t e", t=B)
        prob = carve(qtr, B * E).rearrange("p (t e) -> p t e", t=B)
        s8 = sb("s8", [128, 8, B])
        oh = carve(qtr, 2 * B * E).rearrange("p (k t e) -> p k t e", k=2, t=B)
        t128 = carve(qtr, 2 * B * E).rearrange("p (k t e) -> p k t e", k=2, t=B)
        mb = sb("mb", [128, B, E], bf16)
        cmp = carve(qkr, E * E).rearrange("p (a b) -> p a b", a=E)
        nb = sb("nb", [128, 3, E])
        posi = sb("posi", [128, 2, B], i32)
        bcmp = carve(qkr, BLOCKS * E)[0:1, :].rearrange("p (a b) -> p a b", a=BLOCKS)
        be = sb("be", [1, 2, BLOCKS])
        bei = sb("bei", [1, BLOCKS], i32)
        spare = kbd[:].rearrange("p a g h t -> p (a g h t)")
        sg = spare[:, 0:2 * SI].rearrange("p (r n) -> p r n", r=2)
        sh = spare[:, 2 * SI:4 * SI].rearrange("p (r n) -> p r n", r=2)
        shT = spare[:, 4 * SI:4 * SI + 6 * T].rearrange("p (r k t) -> p r k t", r=2, k=3)
        bx = xb
        bxT = xbT
        bs = carve(prr, 2 * I).rearrange("p (r n) -> p r n", r=2)
        bh = carve(prr, 2 * I).rearrange("p (r n) -> p r n", r=2)
        bhT = carve(ptr, 4 * T)[0:IH, :].rearrange("p (r k t) -> p r k t", r=2, k=2)
        by = carve(ptr, 2 * D).rearrange("p (r n) -> p r n", r=2)
        yg = spare[:, 4 * SI + 6 * T:4 * SI + 6 * T + 4 * D].rearrange("p (r n) -> p r n", r=4)
        sdn_s = spare[:, 4 * SI + 6 * T + 4 * D:4 * SI + 6 * T + 7 * D].rearrange("p (k n) -> p k n", k=3)

        def xpart(b):
            return [i for i, (lo, hi) in enumerate(XPARTS) if lo <= b < hi][0]

        block = ctx.enter_context(nc.Block())

        @block.sync
        def _(sp):
            xv = x.rearrange("b p d -> p b d")
            cv = ctx_in.rearrange("b p d -> p b d")
            for i, (lo, hi) in enumerate(XPARTS[:1]):
                sp.dma_start(x_s[:, lo:hi, :], xv[:, lo:hi, :]).then_inc(s_x[i], 16)
            sp.dma_start(tab[:], table).then_inc(s_tab, 16)
            sp.dma_start(wm_s[:], w_m.rearrange("(k p) n -> p k n", p=128)).then_inc(s_wm, 16)
            sp.dma_start(cs[:, 0:4, :], cv[:, 0:4, :]).then_inc(s_ctx0, 16)
            sp.dma_start(wh_s[:], wh.rearrange("h p n -> p h n")).then_inc(s_wh, 16)
            sp.dma_start(x_s[:, 1:3, :], xv[:, 1:3, :]).then_inc(s_x[1], 16)
            sp.dma_start(wq_s[:], w_q).then_inc(s_wq, 16)
            sp.dma_start(wkv_s[:], w_kv.rearrange("(k p) n -> p k n", p=KPH)).then_inc(s_wkv, 16)
            sp.dma_start(lnq_s[:], ln_q).then_inc(s_lnv, 16)
            sp.dma_start(lnkv_s[:], ln_kv.rearrange("(k p) n -> p k n", p=KPH)).then_inc(s_lnv, 16)
            sp.dma_start(x_s[:, 3:8, :], xv[:, 3:8, :]).then_inc(s_x[2], 16)
            sp.dma_start(cs[:, 4:8, :], cv[:, 4:8, :]).then_inc(s_ctx1, 16)
            sp.dma_start(wout_s[:], w_out.rearrange("(k p) n -> p k n", p=128)).then_inc(s_wout, 16)
            sp.dma_start(wg_s[:], wg.rearrange("(k p) n -> p k n", p=128)).then_inc(s_wgo, 16)
            sp.dma_start(wo_s[:], wo.rearrange("(k p) n -> p k n", p=128)).then_inc(s_wgo, 16)
            sp.dma_start(gn_s[:], gn.rearrange("(k p) n -> p k n", p=128)).then_inc(s_wgo, 16)
            sp.dma_start(gate_s[:], gate.rearrange("(k p) n -> p k n", p=128)).then_inc(s_gate, 16)
            sp.dma_start(sgu_s[:], s_gu_d.rearrange("(k p) n -> p k n", p=128)).then_inc(s_shw, 16)
            for k in range(KD):
                for e in range(0, E, 4):
                    sp.dma_start(gu_s[:, k, e:e + 4, :],
                                 w_gu[e:e + 4, k * 128:(k + 1) * 128, :].rearrange("e p n -> p e n")).then_inc(s_gu, 16)
            for k in range(2):
                for e in range(0, E, 8):
                    sp.dma_start(dn_s[:, k, e:e + 8, :],
                                 w_dn[e:e + 8, k * IH:(k + 1) * IH, :].rearrange("e p n -> p e n")).then_inc(s_dn, 16)
            sp.wait_ge(s_zero, 1)
            sp.dma_start(slots_x.rearrange("(b p) d -> p b d", p=T),
                         zeros.unsqueeze(1).to_broadcast([T, BLOCKS, D])).then_inc(s_zfill, 16)
            sp.wait_ge(p_s, NC * B)
            sp.dma_start(sdn_s[:, 0:2, :], s_dn_d[0:256, :].rearrange("(k p) n -> p k n", p=128)).then_inc(s_shw, 16)
            sp.dma_start(sdn_s[0:SI - 256, 2, :], s_dn_d[256:SI, :]).then_inc(s_shw, 16)

            sp.wait_ge(d_sc, 16 * 2 * B)

            def load(i, par, first=False):
                if not first:
                    sp.wait_ge(p_bT, i - 1)
                sp.dma_start(bx[:, par, :], slots_x[bass.ts(i, T), :]).then_inc(d_xs[par], 16)

            def store(i, par):
                sp.wait_ge(v_y, i + 1)
                sp.dma_start(slots_y[bass.ts(i, T), :], by[:, par, :]).then_inc(d_ys[par], 16)

            sp.wait_ge(p_bt, B)
            load(0, 0, True)
            load(1, 1, True)
            with sp.Fori(2, BLOCKS - 1, 2) as i:
                load(i, 0)
                store(i - 2, 0)
                load(i + 1, 1)
                store(i - 1, 1)
            load(BLOCKS - 1, 0)
            for i in range(BLOCKS - 3, BLOCKS):
                store(i, i % 2)
            for t in range(B):
                sp.wait_ge(v_f1, 2 * t + 2)
                sp.dma_start(out[t, :, :], x_s[:, t, :]).then_inc(d_out, 16)
            sp.wait_ge(d_out, 16 * B)

        @block.gpsimd
        def _(pool):
            nc.gpsimd.memset(halfpow[:], -0.5).then_inc(c_set, 1)
            nc.gpsimd.memset(v_s[:, :, :, DH:DH + 1], 1.0).then_inc(c_set, 1)
            nc.gpsimd.memset(zeros, 0.0).then_inc(s_zero, 1)
            pool.wait_ge(c_set, 2)

            def rsqrt(kind, b, ready, done):
                pool.wait_ge(ready, b + 1)
                nc.gpsimd.tensor_tensor(rs[:, kind, b % 2, :], ve[:, kind, b % 2, :], halfpow[:, 0:1],
                                        ALU.pow).then_inc(done, 1)

            def rsqrt_latent(b):
                pool.wait_ge(v_mv, b + 1)
                nc.gpsimd.tensor_tensor(rs2[:, b % 2, :], ve2[:, b % 2, :], halfpow[:], ALU.pow).then_inc(g_m, 1)

            def expand(b, g):
                pool.wait_ge(a_qkT, b + 1)
                if b >= 2:
                    pool.wait_ge(p_s, NC * (b - 2) + 2 * (g + 1))
                nc.gpsimd.tensor_tensor(
                    kbd[:, b % 2, g, :, :],
                    qkT[:, b % 2, 2 + g, :].unsqueeze(1).to_broadcast([128, 8, T]),
                    tab[:, C_HEAD:C_HEAD + 8].unsqueeze(2).to_broadcast([128, 8, T]), ALU.mult).then_inc(g_kbd, 1)

            pool.wait_ge(s_tab, 16)
            rsqrt(LX, 0, v_xv, g_x)
            for i in range(-2, B + 1):
                if 0 <= i - 1 < B:
                    rsqrt(LX1, i - 1, v_x1v, g_x1)
                if 0 < i + 3 < B:
                    rsqrt(LX, i + 3, v_xv, g_x)
                if 0 <= i + 1 < B:
                    expand(i + 1, 0)
                if i + 2 < B:
                    rsqrt_latent(i + 2)
                if 0 <= i + 1 < B:
                    expand(i + 1, 1)
            for i in range(B + 2):
                if i < B:
                    rsqrt(LO, i, v_ov, g_o)
                if 0 <= i - 2:
                    rsqrt(LX2, i - 2, v_x2v, g_x2)
            pool.wait_ge(s_zfill, 16)
            pool.wait_ge(v_pos, 1)
            for k in range(2):
                for t in range(B):
                    pool.indirect_dma_start(slots_x[:], bass.IndirectOffsetOnAxis(ap=posi[:, k, t:t + 1], axis=0),
                                            x1_s[:, t, :], None).then_inc(d_sc, 16)
            pool.wait_ge(d_ys[0], 16 * ((BLOCKS + 1) // 2))
            pool.wait_ge(d_ys[1], 16 * (BLOCKS // 2))
            for n in range(2 * B):
                t, k = n // 2, n % 2
                if n >= 4:
                    pool.wait_ge(v_f1, n - 3)
                pool.indirect_dma_start(yg[:, n % 4, :], None, slots_y[:],
                                        bass.IndirectOffsetOnAxis(ap=posi[:, k, t:t + 1], axis=0)).then_inc(d_g[n % 4], 16)

        @block.tensor
        def _(pe):
            mm, tr = nc.tensor.matmul, nc.tensor.transpose

            def front_transpose(b):
                pe.wait_ge(v_xh, b + 1)
                if b >= 1:
                    pe.wait_ge(v_q, b)
                for k in range(KD):
                    last = tr(bank[5][:, k * T:(k + 1) * T], xh[:, b % 2, k * 128:(k + 1) * 128], idf)
                last.then_inc(p_t1, 1)

            def front_project(b):
                pe.wait_ge(a_xT, b + 1)
                for k in range(KD):
                    last = mm(bank[5][:, 0:MW], xT[:, b % 2, k, :], wm_s[:, k, :], start=k == 0, stop=k == KD - 1)
                last.then_inc(p_m1, 1)

            def latent_transpose(b):
                pe.wait_ge(v_lat, b + 1)
                tr(bank[5][:, 0:T], lat[:, b % 2, 0:QP], idf)
                for k in range(2):
                    last = tr(bank[5][0:KPH, (k + 1) * T:(k + 2) * T],
                              lat[:, b % 2, QP + k * KPH:QP + (k + 1) * KPH], idf)
                last.then_inc(p_t2, 1)

            def keys_values(b):
                pe.wait_ge(a_lat, b + 1)
                if b >= 3:
                    pe.wait_ge(a_qw, b - 2)
                for k in range(2):
                    last = mm(bank[4][:, 0:NOPE + D], ckvT[:, b % 2, k, :], wkv_s[:, k, :], start=k == 0, stop=k == 1)
                last.then_inc(p_kv, 1)
                mm(bank[5][:, 0:QW], cqT[:, b % 2, :], wq_s[:], start=True, stop=True).then_inc(p_q, 1)

            def qk_transpose(b):
                pe.wait_ge(v_q, b + 1)
                pe.wait_ge(a_kv, b + 1)
                if b >= 2:
                    pe.wait_ge(a_ot, b - 1)
                for k in range(4):
                    last = tr(bank[6][:, k * T:(k + 1) * T], qk[:, b % 2, k * 128:(k + 1) * 128], idf)
                last.then_inc(p_t3, 1)

            def scores(b, c):
                n, g = NC * b + c, c // 2
                if c == 0:
                    pe.wait_ge(a_qkT, b + 1)
                if c % 2 == 0:
                    pe.wait_ge(g_kbd, 2 * b + g + 1)
                if n >= 2:
                    pe.wait_ge(v_sb, n - 1)
                h0 = (c % 2) * CH
                o = bank[c % 2][:].rearrange("p (h k) -> p h k", h=CH)
                mm(o, qkT[:, b % 2, g, :], kbd[:, b % 2, g, h0:h0 + CH, :], start=True, stop=False)
                mm(o, idb[:], maskb[:].unsqueeze(1).to_broadcast([128, CH, T]), start=False, stop=True).then_inc(p_s, 1)

            def prob_transpose(b, c):
                n = NC * b + c
                pe.wait_ge(a_exp, n + 1)
                if n >= 2:
                    pe.wait_ge(a_prT, n - 1)
                for h in range(CH):
                    last = tr(bank[2 + n % 2][:, h * T:(h + 1) * T], pr_s[:, n % 2, h, :], idf)
                last.then_inc(p_pt, 1)

            def weigh_values(b, c):
                n = NC * b + c
                pe.wait_ge(a_prT, n + 1)
                if c == 0:
                    pe.wait_ge(a_qkT, min(b + 2, B))
                for h in range(CH):
                    hh = c * CH + h
                    last = mm(bank[6][:, hh * (DH + 1):(hh + 1) * (DH + 1)], prT[:, n % 2, h, :],
                              v_s[:, b % 2, hh, :], start=True, stop=True)
                last.then_inc(p_pv, 1)

            def out_transpose(b):
                pe.wait_ge(v_on, b + 1)
                for k in range(KD):
                    last = tr(bank[6][:, k * T:(k + 1) * T], o_s[:, b % 2, k * 128:(k + 1) * 128], idf)
                last.then_inc(p_t5, 1)

            def out_project(b):
                pe.wait_ge(a_ot, b + 1)
                pe.wait_ge(a_kv, min(b + 3, B))
                for k in range(KD):
                    last = mm(bank[4][:, 0:D], oT[:, b % 2, k, :], wout_s[:, k, :], start=k == 0, stop=k == KD - 1)
                last.then_inc(p_wo, 1)

            def cross_transpose(b):
                pe.wait_ge(v_xb, b + 1)
                for k in range(KD):
                    last = tr(bank[4][:, k * T:(k + 1) * T], xb[:, b % 2, k * 128:(k + 1) * 128], idf)
                last.then_inc(p_bt, 1)

            def cross_project(b):
                pe.wait_ge(a_bt, b + 1)
                for h in range(XH):
                    mm(bank[4][:, h * T:(h + 1) * T], wh_s[:, h, :], xbT[:, b % 2, h, :], start=True, stop=True)
                for m in range(KD):
                    for k in range(KD):
                        last = mm(bank[4][:, (XH + m) * T:(XH + m + 1) * T], wg_s[:, k, m * 128:(m + 1) * 128],
                                  xbT[:, b % 2, k, :], start=k == 0, stop=k == KD - 1)
                last.then_inc(p_bqw, 1)

            def cross_scores(b):
                pe.wait_ge(a_qw, b + 1)
                for h in range(XH):
                    last = mm(bank[7][:, h * T:(h + 1) * T], ck_s[:, h, b, :], qw_s[:, b, h, :],
                              start=b == 0 and h == 0, stop=b == B - 1, skip_group_check=True)
                last.then_inc(p_sc, 1)

            def ctx_part(g, step):
                if step == 0:
                    pe.wait_ge((s_ctx0, s_ctx1)[g], 16)
                    for h in range(XH):
                        if g:
                            pe.wait_ge(a_cv, 2 * g)
                        for j in range(4):
                            last = tr(bank[2 + h][:, j * T:(j + 1) * T], cs[:, 4 * g + j, h * HD:(h + 1) * HD], idf)
                        last.then_inc(p_ct, 1)
                if step == 1:
                    pe.wait_ge(s_wh, 16)
                    for h in range(XH):
                        pe.wait_ge(a_ct, XH * g + h + 1)
                        if g:
                            pe.wait_ge(a_ck, XH * g)
                        mm(bank[h][:], wh_s[:, h, :], cT[:, h, :, :], start=True, stop=True).then_inc(p_ck, 1)
                if step == 2:
                    for j in range(4):
                        for h in range(XH):
                            last = mm(bank[2 + j // 2][:, (j % 2) * D + h * HD:(j % 2) * D + (h + 1) * HD],
                                      cT[:, h, j, :], wh_s[:, h, :], start=True, stop=True)
                        if j % 2:
                            last.then_inc(p_cv, 1)

            pe.wait_ge(s_tab, 16)
            for i in range(-2, B + 1):
                a, w, f1, f2 = i, i - 1, i + 1, i + 2
                if i == -1:
                    pe.wait_ge(s_wq, 16)
                    pe.wait_ge(s_wkv, 16)
                if i == 0:
                    pe.wait_ge(c_bf, 3)
                if i == 1:
                    pe.wait_ge(s_wout, 16)
                    pe.wait_ge(s_wgo, 48)
                if 0 <= a < B:
                    scores(a, 0)
                if 0 <= f1 < B:
                    keys_values(f1)
                if 0 <= a < B:
                    scores(a, 1)
                if 0 <= w < B:
                    out_transpose(w)
                if f2 < B:
                    front_transpose(f2)
                if i == -2:
                    ctx_part(0, 0)
                    pe.wait_ge(s_wm, 16)
                if 0 <= a < B:
                    scores(a, 2)
                if 0 <= w < B:
                    out_project(w)
                if 0 <= a < B:
                    scores(a, 3)
                if 0 <= f1 < B:
                    qk_transpose(f1)
                if f2 < B:
                    front_project(f2)
                if i == -2:
                    ctx_part(0, 1)
                    ctx_part(0, 2)
                if i == -1:
                    ctx_part(1, 0)
                    ctx_part(1, 1)
                    ctx_part(1, 2)
                    pe.wait_ge(a_cv, 4)
                if 0 <= a < B:
                    prob_transpose(a, 0)
                    prob_transpose(a, 1)
                if 0 <= w < B:
                    cross_transpose(w)
                if 0 <= a < B:
                    weigh_values(a, 0)
                    weigh_values(a, 1)
                    prob_transpose(a, 2)
                    prob_transpose(a, 3)
                if 0 <= w < B:
                    cross_project(w)
                if f2 < B:
                    latent_transpose(f2)
                if 0 <= a < B:
                    weigh_values(a, 2)
                    weigh_values(a, 3)
                if 0 <= w < B:
                    cross_scores(w)

            def cross_mix(b):
                if b == 0:
                    pe.wait_ge(v_at, 1)
                if b >= 1:
                    pe.wait_ge(v_yh, b)
                for h in range(XH):
                    last = mm(bank[0][:, h * HD:(h + 1) * HD], aT[:, h, :], cv_s[:, b, h, :], start=True, stop=True)
                last.then_inc(p_o, 1)

            def mix_transpose(b):
                pe.wait_ge(v_yh, b + 1)
                if b >= 1:
                    pe.wait_ge(a_ty, b)
                for k in range(KD):
                    last = tr(bank[1][:, k * T:(k + 1) * T], yh[:, b % 2, k * 128:(k + 1) * 128], idf)
                last.then_inc(p_ty, 1)

            def cross_out(b):
                pe.wait_ge(v_z, b + 1)
                if b >= 1:
                    pe.wait_ge(v_x2, b)
                for k in range(KD):
                    last = mm(bank[2][:, 0:D], zT[:, b % 2, k, :], wo_s[:, k, :], start=k == 0, stop=k == KD - 1)
                last.then_inc(p_xo, 1)

            def ffn_transpose(b):
                pe.wait_ge(v_xf, b + 1)
                if b >= 1:
                    pe.wait_ge(a_tf, b)
                for k in range(KD):
                    last = tr(bank[3][:, k * T:(k + 1) * T], x1_s[:, b, k * 128:(k + 1) * 128], idf)
                last.then_inc(p_tf, 1)

            def router(b):
                pe.wait_ge(a_tf, b + 1)
                for k in range(KD):
                    last = mm(bank[4][:, b * E:(b + 1) * E], xfT[:, k, b, :], gate_s[:, k, :],
                              start=k == 0, stop=k == KD - 1)
                last.then_inc(p_lg, 1)

            def shared_up(b):
                pe.wait_ge(a_tf, b + 1)
                if b >= 1:
                    pe.wait_ge(v_sh, b)
                for m in range(2):
                    for k in range(KD):
                        last = mm(bank[5 + m][:, 0:SI], xfT[:, k, b, :], sgu_s[:, k, m * SI:(m + 1) * SI],
                                  start=k == 0, stop=k == KD - 1)
                last.then_inc(p_sg, 1)

            def shared_transpose(b):
                pe.wait_ge(v_sh, b + 1)
                if b >= 1:
                    pe.wait_ge(a_sT, b)
                for k in range(3):
                    r = min(128, SI - k * 128)
                    last = tr(bank[7][0:r, k * T:(k + 1) * T], sh[:, b % 2, k * 128:k * 128 + r], idf)
                last.then_inc(p_sT, 1)

            def shared_down(b):
                pe.wait_ge(a_sT, b + 1)
                if b >= 1:
                    pe.wait_ge(v_sd, b)
                for k in range(3):
                    r = min(128, SI - k * 128)
                    last = mm(bank[3][:, 0:D], shT[0:r, b % 2, k, :], sdn_s[0:r, k, :], start=k == 0, stop=k == 2)
                last.then_inc(p_sd, 1)

            pe.wait_ge(s_gate, 16)
            for i in range(B + 4):
                if i < B:
                    cross_mix(i)
                if 0 <= i - 1 < B:
                    mix_transpose(i - 1)
                if 0 <= i - 2 < B:
                    cross_out(i - 2)
                if 0 <= i - 3 < B:
                    ffn_transpose(i - 3)
                if 0 <= i - 4 < B:
                    router(i - 4)
            pe.wait_ge(s_shw, 48)
            pe.wait_ge(a_tf, B)
            for i in range(B + 1):
                if i < B:
                    shared_up(i)
                if i >= 1:
                    shared_transpose(i - 1)
                if i == 2:
                    pe.wait_ge(v_top, 1)
                    rank = bank[0][:, 0:B * E]
                    for t in range(B - 1):
                        mm(rank[:, (t + 1) * E:].rearrange("p (t e) -> p t e", e=E), onesb[:],
                           mb[:, t:t + 1, :].to_broadcast([128, B - 1 - t, E]), start=t == 0, stop=False,
                           skip_group_check=True)
                    mm(rank, trib[:], mb[:].rearrange("p t e -> p (t e)"), start=False, stop=True, skip_group_check=True)
                    for t in range(B):
                        last = mm(bank[1][:, 0:E], onesb[:], mb[:, t, :], start=t == 0, stop=t == B - 1)
                    last.then_inc(p_rk, 1)
                if i >= 1:
                    shared_down(i - 1)

            pe.wait_ge(s_gu, 16 * 8)
            pe.wait_ge(s_dn, 16 * 4)
            pe.wait_ge(v_blk, 1)
            pe.wait_ge(v_pos, 1)

            def block_transpose(i, par, first=False):
                pe.wait_ge(d_xs[par], (i // 2 if isinstance(i, int) else (i - par) // 2) * 16 + 16)
                if not first:
                    pe.wait_ge(v_bT, i)
                for k in range(KD):
                    last = tr(bank[0][:, k * T:(k + 1) * T], bx[:, par, k * 128:(k + 1) * 128], idf)
                last.then_inc(p_bT, 1)

            def hidden_transpose(i, par):
                pe.wait_ge(v_h, i + 1)
                for k in range(2):
                    last = tr(bank[1][0:IH, k * T:(k + 1) * T], bh[:, par, k * IH:(k + 1) * IH], idf)
                last.then_inc(p_hT, 1)

            def expert_up(i, par, e):
                pe.wait_ge(v_bT, i + 1)
                for k in range(KD):
                    last = mm(bank[2 + par][:, 0:2 * I], bxT[:, par, k, :], gu_s[:, k, bass.ds(e, 1), :],
                              start=k == 0, stop=k == KD - 1)
                last.then_inc(p_gu, 1)

            def expert_down(i, par, e):
                pe.wait_ge(a_hT, i + 1)
                for k in range(2):
                    last = mm(bank[4 + par][:, 0:D], bhT[:, par, k, :], dn_s[:, k, bass.ds(e, 1), :],
                              start=k == 0, stop=k == 1)
                last.then_inc(p_dn, 1)

            def expert_of(i):
                return pe.value_load(bei[0:1, bass.ds(i, 1)], min_val=0, max_val=E - 1)

            def step(i, par, first=False):
                block_transpose(i + 1, 1 - par)
                if not first:
                    hidden_transpose(i - 1, 1 - par)
                expert_up(i, par, expert_of(i))
                if not first:
                    expert_down(i - 1, 1 - par, expert_of(i - 1))

            block_transpose(0, 0, True)
            step(0, 0, True)
            with pe.Fori(1, BLOCKS - 2, 2) as i:
                step(i, 1)
                step(i + 1, 0)
            step(BLOCKS - 2, 1)
            i = BLOCKS - 1
            hidden_transpose(i - 1, 1)
            expert_up(i, 0, expert_of(i))
            expert_down(i - 1, 1, expert_of(i - 1))
            hidden_transpose(i, 0)
            expert_down(i, 0, expert_of(i))

        @block.scalar
        def _(act):
            copy = lambda o, i: nc.scalar.activation(o, i, ACT.Copy)

            def exps(b, c):
                n = NC * b + c
                act.wait_ge(v_sb, n + 1)
                if n >= 2:
                    act.wait_ge(p_pt, n - 1)
                nc.scalar.activation(pr_s[:, n % 2, :, :], sc_s[:, n % 2, :, :], ACT.Exp, scale=DH ** -0.5).then_inc(a_exp, 1)

            def kv_out(b):
                act.wait_ge(p_kv, b + 1)
                if b >= 2:
                    act.wait_ge(p_t3, b - 1)
                    act.wait_ge(p_pv, NC * (b - 1))
                copy(qk[:, b % 2, D:D + NOPE], bank[4][:, 0:NOPE])
                copy(v_s[:, b % 2, :, 0:DH], bank[4][:, NOPE:NOPE + D].rearrange("p (h d) -> p h d", h=H)).then_inc(a_kv, 1)

            def ot_out(b):
                act.wait_ge(p_t5, b + 1)
                if b >= 2:
                    act.wait_ge(p_wo, b - 1)
                copy(oT[:, b % 2, :, :].rearrange("p k t -> p (k t)"), bank[6][:, 0:D]).then_inc(a_ot, 1)

            def xT_out(b):
                act.wait_ge(p_t1, b + 1)
                if b >= 2:
                    act.wait_ge(p_m1, b - 1)
                copy(xT[:, b % 2, :, :].rearrange("p k t -> p (k t)"), bank[5][:, 0:D]).then_inc(a_xT, 1)

            def qkT_out(b):
                act.wait_ge(p_t3, b + 1)
                if b >= 2:
                    act.wait_ge(p_s, NC * (b - 1))
                    act.wait_ge(g_kbd, 2 * (b - 1))
                copy(qkT[:, b % 2, :, :].rearrange("p k t -> p (k t)"), bank[6][:, 0:4 * T]).then_inc(a_qkT, 1)

            def prT_out(b, c):
                n = NC * b + c
                act.wait_ge(p_pt, n + 1)
                if n >= 2:
                    act.wait_ge(p_pv, n - 1)
                copy(prT[:, n % 2, :, :].rearrange("p k t -> p (k t)"), bank[2 + n % 2][:]).then_inc(a_prT, 1)

            def xbT_out(b):
                act.wait_ge(p_bt, b + 1)
                if b >= 2:
                    act.wait_ge(p_bqw, b - 1)
                copy(xbT[:, b % 2, :, :].rearrange("p k t -> p (k t)"), bank[4][:, 0:D]).then_inc(a_bt, 1)

            def qw_out(b):
                act.wait_ge(p_bqw, b + 1)
                if b == B - 1:
                    act.wait_ge(s_zfill, 16)
                copy(qw_s[:, b, :, :].rearrange("p k t -> p (k t)"), bank[4][:]).then_inc(a_qw, 1)

            def latents_out(b):
                act.wait_ge(p_t2, b + 1)
                if b >= 2:
                    act.wait_ge(p_q, b - 1)
                nc.scalar.activation(cqT[:, b % 2, :], bank[5][:, 0:T], ACT.Identity, scale=lnq_s[:, 0:1], bias=lnq_s[:, 1:2])
                for k in range(2):
                    last = nc.scalar.activation(ckvT[:, b % 2, k, :], bank[5][0:KPH, (k + 1) * T:(k + 2) * T],
                                                ACT.Identity, scale=lnkv_s[:, k, 0:1], bias=lnkv_s[:, k, 1:2])
                last.then_inc(a_lat, 1)

            def ctx_out(g):
                for h in range(XH):
                    act.wait_ge(p_ct, XH * g + h + 1)
                    if g:
                        act.wait_ge(p_cv, 2)
                    copy(cT[:, h, :, :].rearrange("p j t -> p (j t)"), bank[2 + h][:]).then_inc(a_ct, 1)
                for h in range(XH):
                    act.wait_ge(p_ck, XH * g + h + 1)
                    copy(ck_s[:, h, 4 * g:4 * g + 4, :].rearrange("p j t -> p (j t)"), bank[h][:]).then_inc(a_ck, 1)
                for j in range(2):
                    act.wait_ge(p_cv, 2 * g + j + 1)
                    copy(cv_s[:, 4 * g + 2 * j:4 * g + 2 * j + 2, :, :].rearrange("p j h t -> p (j h t)"),
                         bank[2 + j][:]).then_inc(a_cv, 1)

            for i in range(-2, B + 1):
                a, w, f1, f2 = i, i - 1, i + 1, i + 2
                if i == -2:
                    act.wait_ge(s_lnv, 32)
                if 0 <= a < B:
                    exps(a, 0)
                if 0 <= f1 < B:
                    kv_out(f1)
                if 0 <= w < B:
                    ot_out(w)
                if f2 < B:
                    xT_out(f2)
                if 0 <= a < B:
                    exps(a, 1)
                    exps(a, 2)
                if 0 <= f1 < B:
                    qkT_out(f1)
                if i == -2:
                    ctx_out(0)
                if i == -1:
                    ctx_out(1)
                if 0 <= a < B:
                    exps(a, 3)
                    prT_out(a, 0)
                    prT_out(a, 1)
                if 0 <= w < B:
                    xbT_out(w)
                if 0 <= a < B:
                    prT_out(a, 2)
                    prT_out(a, 3)
                if 0 <= w < B:
                    qw_out(w)
                if f2 < B:
                    latents_out(f2)

            def yT_out(b):
                act.wait_ge(p_ty, b + 1)
                if b >= 2:
                    act.wait_ge(v_z, b - 1)
                for k in range(KD):
                    last = nc.scalar.activation(yT[:, b % 2, k, :], bank[1][:, k * T:(k + 1) * T], ACT.Identity,
                                                scale=gn_s[:, k, 0:1], bias=gn_s[:, k, 1:2])
                last.then_inc(a_ty, 1)

            def xfT_out(b):
                act.wait_ge(p_tf, b + 1)
                copy(xfT[:, :, b, :], bank[3][:, 0:D].rearrange("p (k t) -> p k t", k=KD)).then_inc(a_tf, 1)

            for i in range(B + 4):
                if 0 <= i - 1 < B:
                    yT_out(i - 1)
                if 0 <= i - 3 < B:
                    xfT_out(i - 3)
            act.wait_ge(v_lg, 1)
            nc.scalar.activation(ex, lg, ACT.Exp).then_inc(a_re, 1)

            for i in range(B + 1):
                if i < B:
                    act.wait_ge(p_sg, i + 1)
                    if i >= 2:
                        act.wait_ge(v_sh, i - 1)
                    nc.scalar.activation(sg[:, i % 2, :], bank[5][:, 0:SI], ACT.Silu).then_inc(a_sg, 1)
                if i >= 1:
                    b = i - 1
                    act.wait_ge(p_sT, b + 1)
                    if b >= 2:
                        act.wait_ge(p_sd, b - 1)
                    copy(shT[:, b % 2, 0:2, :].rearrange("p k t -> p (k t)"), bank[7][:, 0:2 * T])
                    copy(shT[0:SI - 256, b % 2, 2, :], bank[7][0:SI - 256, 2 * T:3 * T]).then_inc(a_sT, 1)

            def silu(i, par, first=False):
                act.wait_ge(p_gu, i + 1)
                if not first:
                    act.wait_ge(v_h, i - 1)
                nc.scalar.activation(bs[:, par, :], bank[2 + par][:, 0:I], ACT.Silu).then_inc(a_si, 1)

            def hT_out(i, par, first=False):
                act.wait_ge(p_hT, i + 1)
                if not first:
                    act.wait_ge(p_dn, i - 1)
                copy(bhT[:, par, :, :].rearrange("p k t -> p (k t)"), bank[1][0:IH, 0:2 * T]).then_inc(a_hT, 1)

            silu(0, 0, True)
            hT_out(0, 0, True)
            silu(1, 1, True)
            hT_out(1, 1, True)
            with act.Fori(2, BLOCKS - 1, 2) as i:
                silu(i, 0)
                hT_out(i, 0)
                silu(i + 1, 1)
                hT_out(i + 1, 1)
            silu(BLOCKS - 1, 0)
            hT_out(BLOCKS - 1, 0)

        @block.vector
        def _(dve):
            V = nc.vector
            count = [0]

            def link(ins):
                count[0] += 1
                ins.then_inc(chain, 1)
                dve.wait_ge(chain, count[0])

            def variance(kind, b, src, eps, done):
                link(V.bn_stats(st[:, 0, :], src))
                link(V.bn_aggr(ag[:, kind, b % 2, :], st[:, 0, :]))
                V.tensor_scalar_add(ve[:, kind, b % 2, :], ag[:, kind, b % 2, 1:2], eps).then_inc(done, 1)

            def normalize(kind, b, o, src):
                return V.tensor_scalar(o, src, ag[:, kind, b % 2, 0:1], rs[:, kind, b % 2, :], ALU.subtract, ALU.mult)

            def x_variance(b):
                dve.wait_ge(s_x[xpart(b)], 16)
                variance(LX, b, x_s[:, b, :], LN_EPS, v_xv)

            def x_normalize(b):
                dve.wait_ge(g_x, b + 1)
                if b >= 2:
                    dve.wait_ge(p_t1, b - 1)
                normalize(LX, b, xh[:, b % 2, :], x_s[:, b, :]).then_inc(v_xh, 1)

            def max_subtract(b, c):
                n = NC * b + c
                s = bank[c % 2][:].rearrange("p (h k) -> p h k", h=CH)
                dve.wait_ge(p_s, n + 1)
                link(V.reduce_max(mx[:, n % 2, :], s, AX.X))
                if n >= 2:
                    dve.wait_ge(a_exp, n - 1)
                V.tensor_tensor(sc_s[:, n % 2, :, :], s, mx[:, n % 2, :].unsqueeze(2).to_broadcast([128, CH, T]),
                                ALU.subtract).then_inc(v_sb, 1)

            def rope(par, which, src, dst, done):
                t = rope_t[:, par, which, :]
                link(V.tensor_tensor(t, src, tab[:, C_ROPE:C_ROPE + 2 * ROPE], ALU.mult))
                V.tensor_tensor(dst, t[:, 0:ROPE], t[:, ROPE:2 * ROPE], ALU.add).then_inc(done, 1)

            def q_out(b):
                dve.wait_ge(p_q, b + 1)
                if b >= 2:
                    dve.wait_ge(p_t3, b - 1)
                link(V.tensor_copy(qk[:, b % 2, 0:NOPE], bank[5][:, 0:NOPE]))
                rope(b % 2, 0, bank[5][:, NOPE:NOPE + 2 * ROPE], qk[:, b % 2, NOPE:D], v_q)

            def latent_variance(b):
                dve.wait_ge(p_m1, b + 1)
                V.bn_stats(st[:, 0, :], bank[5][:, 0:QP])
                link(V.bn_stats(st[:, 1, :], bank[5][:, QP:QP + KP]))
                V.bn_aggr(ag2[:, b % 2, 0, :], st[:, 0, :])
                link(V.bn_aggr(ag2[:, b % 2, 1, :], st[:, 1, :]))
                V.tensor_scalar_add(ve2[:, b % 2, :], ag2[:, b % 2, :, 1], LN_EPS).then_inc(v_mv, 1)

            def latent_normalize(b):
                if b >= 2:
                    dve.wait_ge(p_t2, b - 1)
                    dve.wait_ge(p_t3, b - 1)
                dve.wait_ge(g_m, b + 1)
                for j, (lo, hi) in enumerate(((0, QP), (QP, QP + KP))):
                    V.tensor_scalar(lat[:, b % 2, lo:hi], bank[5][:, lo:hi], ag2[:, b % 2, j, 0:1],
                                    rs2[:, b % 2, j:j + 1], ALU.subtract, ALU.mult)
                rope(b % 2, 1, bank[5][:, QP + KP:MW], qk[:, b % 2, D + NOPE:2 * D], v_lat)

            def out_normalize(b):
                o = bank[6][:, 0:H * (DH + 1)].rearrange("p (h d) -> p h d", h=H)
                dve.wait_ge(p_pv, NC * (b + 1))
                link(V.reciprocal(rden[:, b % 2, :], o[:, :, DH]))
                if b >= 2:
                    dve.wait_ge(p_t5, b - 1)
                V.tensor_tensor(o_s[:, b % 2, :].rearrange("p (h d) -> p h d", h=H), o[:, :, 0:DH],
                                rden[:, b % 2, :].unsqueeze(2).to_broadcast([128, H, DH]), ALU.mult).then_inc(v_on, 1)

            def residual_attention(b):
                dve.wait_ge(p_wo, b + 1)
                V.tensor_tensor(x1_s[:, b, :], bank[4][:, 0:D], x_s[:, b, :], ALU.add).then_inc(v_x1, 1)
                dve.wait_ge(v_x1, b + 1)
                variance(LX1, b, x1_s[:, b, :], LN_EPS, v_x1v)

            def x1_normalize(b):
                dve.wait_ge(g_x1, b + 1)
                if b >= 2:
                    dve.wait_ge(p_bt, b - 1)
                normalize(LX1, b, xb[:, b % 2, :], x1_s[:, b, :]).then_inc(v_xb, 1)

            V.memset(onesb[:], 1.0).then_inc(c_bf, 1)
            x_variance(0)
            dve.wait_ge(s_tab, 16)
            V.tensor_copy(idb[:], idf).then_inc(c_bf, 1)
            V.tensor_copy(maskb[:], tab[:, C_MASK:C_MASK + 128]).then_inc(c_bf, 1)
            V.tensor_copy(trib[:], tab[:, C_TRI:C_TRI + 128]).then_inc(c_bf, 1)
            x_normalize(0)
            for i in range(-2, B + 1):
                a, w, f1, f2, f3 = i, i - 1, i + 1, i + 2, i + 3
                if 0 <= a < B:
                    max_subtract(a, 0)
                if 0 <= f1 < B:
                    q_out(f1)
                if 0 <= a < B:
                    max_subtract(a, 1)
                    max_subtract(a, 2)
                if 0 <= w < B:
                    residual_attention(w)
                if 0 <= a < B:
                    max_subtract(a, 3)
                if 0 <= w < B:
                    x1_normalize(w)
                if 0 < f3 < B:
                    x_variance(f3)
                if f2 < B:
                    latent_variance(f2)
                if 0 < f3 < B:
                    x_normalize(f3)
                if f2 < B:
                    latent_normalize(f2)
                if 0 <= a < B:
                    out_normalize(a)

            dve.wait_ge(p_sc, B)
            link(V.tensor_tensor(atmp, bank[7][:, 0:XH * T].rearrange("p (h t) -> p h t", h=XH),
                                 tab[:, C_DECAY:C_DECAY + XH * T].rearrange("p (h t) -> p h t", h=XH), ALU.mult))
            link(V.scalar_tensor_tensor(aT, atmp, -1.0, atmp, ALU.mult, ALU.max))
            V.tensor_scalar_max(aT, aT, 1.0).then_inc(v_at, 1)

            def mix_variance(b):
                dve.wait_ge(p_o, b + 1)
                variance(LO, b, bank[0][:, 0:D], GN_EPS, v_ov)

            def mix_normalize(b):
                dve.wait_ge(g_o, b + 1)
                if b >= 2:
                    dve.wait_ge(p_ty, b - 1)
                normalize(LO, b, yh[:, b % 2, :], bank[0][:, 0:D]).then_inc(v_yh, 1)

            def gated(b):
                dve.wait_ge(a_ty, b + 1)
                if b >= 2:
                    dve.wait_ge(p_xo, b - 1)
                V.scalar_tensor_tensor(zT[:, b % 2, :, :].rearrange("p k t -> p (k t)"),
                                       qw_s[:, b, XH:XH + KD, :].rearrange("p k t -> p (k t)"), 0.0,
                                       yT[:, b % 2, :, :].rearrange("p k t -> p (k t)"), ALU.max, ALU.mult).then_inc(v_z, 1)

            def residual_cross(b):
                dve.wait_ge(p_xo, b + 1)
                V.tensor_tensor(x_s[:, b, :], bank[2][:, 0:D], x1_s[:, b, :], ALU.add).then_inc(v_x2, 1)
                dve.wait_ge(v_x2, b + 1)
                variance(LX2, b, x_s[:, b, :], LN_EPS, v_x2v)

            def ffn_normalize(b):
                dve.wait_ge(g_x2, b + 1)
                normalize(LX2, b, x1_s[:, b, :], x_s[:, b, :]).then_inc(v_xf, 1)

            for i in range(B + 2):
                if i < B:
                    mix_variance(i)
                    mix_normalize(i)
                if 0 <= i - 1 < B:
                    gated(i - 1)
                if 0 <= i - 2 < B:
                    residual_cross(i - 2)
                    ffn_normalize(i - 2)

            iota = tab[:, C_IOTA:C_IOTA + E].unsqueeze(1).to_broadcast([128, B, E])
            wide = lambda s: s.unsqueeze(2).to_broadcast([128, B, E])
            top_w, top_i = [s8[:, 0, :], s8[:, 1, :]], [s8[:, 2, :], s8[:, 3, :]]
            dve.wait_ge(p_lg, B)
            logits = bank[4][:, 0:B * E].rearrange("p (t e) -> p t e", e=E)
            link(V.reduce_max(s8[:, 4, :], logits, AX.X))
            V.tensor_tensor(lg, logits, wide(s8[:, 4, :]), ALU.subtract).then_inc(v_lg, 1)
            dve.wait_ge(a_re, 1)
            link(V.reduce_sum(s8[:, 5, :], ex, AX.X))
            link(V.reciprocal(s8[:, 6, :], s8[:, 5, :]))
            link(V.tensor_tensor(prob, ex, wide(s8[:, 6, :]), ALU.mult))
            for k in range(2):
                link(V.reduce_max(top_w[k], prob, AX.X))
                link(V.tensor_tensor(t128[:, 0], prob, wide(top_w[k]), ALU.is_lt))
                link(V.scalar_tensor_tensor(t128[:, 1], t128[:, 0], float(E), iota, ALU.mult, ALU.add))
                link(V.tensor_reduce(top_i[k], t128[:, 1], op=ALU.min, axis=AX.X))
                link(V.tensor_tensor(oh[:, k], iota, wide(top_i[k]), ALU.is_equal))
                if k == 0:
                    link(V.scalar_tensor_tensor(prob, oh[:, 0], -2.0, prob, ALU.mult, ALU.add))
            V.tensor_tensor(mb[:], oh[:, 0], oh[:, 1], ALU.add).then_inc(v_top, 1)

            def shared_mul(b):
                dve.wait_ge(a_sg, b + 1)
                if b >= 2:
                    dve.wait_ge(p_sT, b - 1)
                V.tensor_tensor(sh[:, b % 2, :], bank[6][:, 0:SI], sg[:, b % 2, :], ALU.mult).then_inc(v_sh, 1)

            def shared_add(b):
                dve.wait_ge(p_sd, b + 1)
                V.tensor_tensor(x_s[:, b, :], bank[3][:, 0:D], x_s[:, b, :], ALU.add).then_inc(v_sd, 1)

            def places():
                dve.wait_ge(p_rk, 1)
                c = cmp[:, :, 0:B]
                link(V.tensor_tensor(c, bank[1][:, 0:E].unsqueeze(2).to_broadcast([128, E, B]),
                                     tab[:, C_THR:C_THR + B].unsqueeze(1).to_broadcast([128, E, B]), ALU.is_gt))
                link(V.reduce_sum(nb[:, 0, :], c, AX.X))
                link(V.tensor_tensor(cmp, nb[:, 0, :].unsqueeze(1).to_broadcast([128, E, E]),
                                     tab[:, C_LOW:C_LOW + E * E].rearrange("p (a b) -> p a b", a=E), ALU.mult))
                link(V.reduce_sum(nb[:, 1, :], cmp, AX.X))
                link(V.tensor_scalar_mul(nb[:, 2, :], nb[:, 1, :], float(T)))
                link(V.tensor_tensor(t128[:, 0], bank[0][:, 0:B * E].rearrange("p (t e) -> p t e", e=E),
                                     nb[:, 2, :].unsqueeze(1).to_broadcast([128, B, E]), ALU.add))
                for k in range(2):
                    link(V.tensor_tensor(t128[:, 1], t128[:, 0], oh[:, k], ALU.mult))
                    link(V.reduce_sum(s8[:, 4 + k, :], t128[:, 1], AX.X))
                V.tensor_copy(posi[:], s8[:, 4:6, :]).then_inc(v_pos, 1)
                link(V.tensor_tensor(bcmp, nb[0:1, 1, :].unsqueeze(1).to_broadcast([1, BLOCKS, E]),
                                     tab[0:1, C_BLK:C_BLK + BLOCKS].unsqueeze(2).to_broadcast([1, BLOCKS, E]), ALU.is_le))
                link(V.reduce_sum(be[:, 0, :], bcmp, AX.X))
                link(V.tensor_scalar_add(be[:, 1, :], be[:, 0, :], -1.0))
                V.tensor_copy(bei[:], be[:, 1, :]).then_inc(v_blk, 1)

            for i in range(B + 1):
                if i < B:
                    shared_mul(i)
                if i >= 1:
                    shared_add(i - 1)
                if i == 2:
                    places()

            def bT_out(i, par, first=False):
                dve.wait_ge(p_bT, i + 1)
                if not first:
                    dve.wait_ge(p_gu, i - 1)
                V.tensor_copy(bxT[:, par, :, :].rearrange("p k t -> p (k t)"), bank[0][:, 0:D]).then_inc(v_bT, 1)

            def h_mul(i, par, first=False):
                dve.wait_ge(a_si, i + 1)
                if not first:
                    dve.wait_ge(p_hT, i - 1)
                V.tensor_tensor(bh[:, par, :], bank[2 + par][:, I:2 * I], bs[:, par, :], ALU.mult).then_inc(v_h, 1)

            def y_out(i, par, first=False):
                dve.wait_ge(p_dn, i + 1)
                if not first:
                    dve.wait_ge(d_ys[par], ((i - par) // 2) * 16 if not isinstance(i, int) else i // 2 * 16)
                V.tensor_copy(by[:, par, :], bank[4 + par][:, 0:D]).then_inc(v_y, 1)

            dve.wait_ge(p_bqw, B)
            bT_out(0, 0, True)
            bT_out(1, 1, True)
            h_mul(0, 0, True)
            bT_out(2, 0)
            h_mul(1, 1, True)
            y_out(0, 0, True)
            bT_out(3, 1)
            h_mul(2, 0)
            y_out(1, 1, True)
            with dve.Fori(4, BLOCKS - 1, 2) as i:
                bT_out(i, 0)
                h_mul(i - 1, 1)
                y_out(i - 2, 0)
                bT_out(i + 1, 1)
                h_mul(i, 0)
                y_out(i - 1, 1)
            bT_out(BLOCKS - 1, 0)
            h_mul(BLOCKS - 2, 1)
            y_out(BLOCKS - 3, 0)
            h_mul(BLOCKS - 1, 0)
            y_out(BLOCKS - 2, 1)
            y_out(BLOCKS - 1, 0)

            for n in range(2 * B):
                t, k = n // 2, n % 2
                dve.wait_ge(d_g[n % 4], 16 * (n // 4 + 1))
                if k:
                    dve.wait_ge(v_f1, n)
                V.scalar_tensor_tensor(x_s[:, t, :], yg[:, n % 4, :], top_w[k][:, t:t + 1], x_s[:, t, :],
                                       ALU.mult, ALU.add).then_inc(v_f1, 1)


def kernel(**inputs):
    import numpy as _np
    import concourse.bacc as _bacc
    from concourse import mybir as _mybir
    from concourse.bass_utils import run_bass_kernel_spmd as _run

    g = {k: _np.asarray(v) for k, v in inputs.items()}

    def swapped(w):
        return w.reshape(w.shape[0], -1, 2, DH // 2)[:, :, ::-1, :].reshape(w.shape)

    a = "L0_attn_"
    arrays = {
        "x": g["x"],
        "ctx_in": g["ctx_2048"],
        "table": constants(),
        "w_m": _np.concatenate([g[a + "W_dq"], g[a + "W_dkv"], g[a + "W_kr"], swapped(g[a + "W_kr"])], 1),
        "w_q": _np.concatenate([g[a + "W_uq"], g[a + "W_qr"], swapped(g[a + "W_qr"])], 1),
        "w_kv": g[a + "W_ukv"],
        "w_out": g[a + "W_o"].T,
        "ln_q": _np.stack([g[a + "q_ln_w"], g[a + "q_ln_b"]], 1),
        "ln_kv": _np.stack([g[a + "kv_ln_w"], g[a + "kv_ln_b"]], 1),
        "wh": g["L0_xattn_Wh"],
        "wg": g["L0_xattn_wg_w"],
        "wo": g["L0_xattn_wo_w"],
        "gn": _np.stack([g["L0_xattn_gn_gamma"], g["L0_xattn_gn_beta"]], 1),
        "gate": g["L0_ffn_gate_w"].T,
        "w_gu": g["L0_ffn_w_gate_up"],
        "w_dn": g["L0_ffn_w_down"],
        "s_gu_d": g["L0_ffn_shared_gate_up"],
        "s_dn_d": g["L0_ffn_shared_down"],
    }
    nc = _bacc.Bacc("TRN2", target_bir_lowering=False, num_devices=1)
    feed, args = {}, []
    for name, v in arrays.items():
        v = _np.ascontiguousarray(v)
        feed[f"in_{name}"] = v
        args.append(nc.dram_tensor(f"in_{name}", v.shape, _mybir.dt.from_np(v.dtype), kind="ExternalInput").ap())
    args.append(nc.dram_tensor("out_0", (B, T, D), _mybir.dt.float32, kind="ExternalOutput").ap())
    decoder_layer(nc, *args)
    r = _run(nc, [feed], core_ids=[0])
    return r.results[0]["out_0"]
```

```python
import numpy as np
import concourse.bass as bass
from concourse import mybir
from contextlib import ExitStack

T = 128
B = 8
D = 256
KD = D // 128
H, DH = 16, 16
HN = 14
NOPE = HN * DH
ROPE = (H - HN) * DH
QP = D // 2
KP = 2 * D // 3
KPH = KP // 2
MW = QP + KP + 2 * ROPE
QW = D + ROPE
CH = 4
NC = H // CH
HD = 128
XH = D // HD
E = 16
I = 176
IH = I // 2
SI = 2 * I
SLOTS = 2 * B * T
BLOCKS = (SLOTS + E * (T - 1)) // T
LN_EPS, GN_EPS = 1e-5, 1e-3
MASKED = -1e30

DUMMY = SLOTS
RB = 4
PAIRS = B // 2

C_ID, C_ROPE, C_HEAD, C_DECAY = 0, 128, 128 + 4 * DH, 128 + 4 * DH + 8
C_IOTA = C_DECAY + XH * T
C_N = C_IOTA + E
R_THR, R_LOW, R_BLK, R_SLOT, R_TOK, R_DUMMY = (int(v) for v in np.cumsum([0, B, E * E, BLOCKS, T, B]))
R_N = R_DUMMY + BLOCKS


def constants():
    c = np.zeros((128, C_N), np.float32)
    p = np.arange(128)
    c[:, C_ID:C_ID + 128] = np.eye(128)
    freqs = (1.0 / 10000.0 ** (np.arange(0, DH, 2, dtype=np.float32) / DH)).astype(np.float32)
    ang = p.astype(np.float32)[:, None] * freqs[None, :]
    cos, sin = np.cos(ang), np.sin(ang)
    c[:, C_ROPE:C_ROPE + 4 * DH] = np.concatenate([cos, cos, cos, cos, -sin, sin, -sin, sin], 1)
    c[:, C_HEAD:C_HEAD + 8] = p[:, None] // DH == np.arange(8)[None, :]
    for h in range(XH):
        expo = (p[None, :] - p[:, None]).astype(np.float64)
        decay = np.where(expo <= 0, (1.0 - 2.0 ** (-5.0 - h)) ** expo, 0.0)
        decay = decay / np.sqrt(decay.sum(-1))[None, :] / np.sqrt(float(HD))
        c[:, C_DECAY + h * T:C_DECAY + (h + 1) * T] = decay.T
    c[:, C_IOTA:C_IOTA + E] = np.arange(E)
    return c


def routing_constants():
    c = np.zeros((128, R_N), np.float32)
    p = np.arange(128)[:, None]
    c[:, R_THR:R_THR + B] = 128.0 * np.arange(B)
    c[:, R_LOW:R_LOW + E * E] = (np.arange(E)[None, :] < np.arange(E)[:, None]).reshape(1, -1)
    c[:, R_BLK:R_BLK + BLOCKS] = np.arange(BLOCKS)
    c[:, R_SLOT:R_SLOT + T] = np.arange(T)
    c[:, R_TOK:R_TOK + B] = T * np.arange(B) + p + 1
    c[:, R_DUMMY:R_DUMMY + BLOCKS] = DUMMY + T * np.arange(BLOCKS) + p + 1
    return c


def bf16_constants():
    p = np.arange(128)
    c = np.concatenate([np.eye(128), np.where(p[None, :] <= p[:, None], 0.0, MASKED), p[:, None] < p[None, :]], 1)
    return c.astype(mybir.dt.np(mybir.dt.bfloat16))


def decoder_layer(nc, x, ctx_in, table, table_b, table_r, w_m, w_q, w_kv, w_out, ln_q, ln_kv, wh, wg, wo, gn,
                  gate, w_gu, w_dn, s_gu_d, s_dn_d, out):
    f32, bf16, i32 = mybir.dt.float32, mybir.dt.bfloat16, mybir.dt.int32
    ALU, ACT, AX = mybir.AluOpType, mybir.ActivationFunctionType, mybir.AxisListType

    ctx = ExitStack()
    with ctx:
        def sb(name, shape, dt=f32):
            return ctx.enter_context(nc.sbuf_tensor(name, shape, dt))

        def sem(name):
            return ctx.enter_context(nc.semaphore(name))

        ffn_in = nc.dram_tensor("ffn_in", [B * T, D], f32).ap()
        expert_out = nc.dram_tensor("expert_out", [DUMMY + BLOCKS * T, D], f32).ap()

        tab = sb("tab", [128, C_N])
        wm_s = sb("wm_s", [128, KD, MW])
        idf = tab[:, C_ID:C_ID + 128]
        tabr = wm_s[:].rearrange("p k n -> p (k n)")[:, 0:R_N]
        tabb = sb("tabb", [128, 3 * 128], bf16)
        idb, maskb, trib = (tabb[:, i * 128:(i + 1) * 128] for i in range(3))
        onesb = sb("onesb", [128, 128], bf16)
        halfpow = sb("halfpow", [128, 2])
        wq_s = sb("wq_s", [128, QW])
        wkv_s = sb("wkv_s", [KPH, 2, NOPE + D])
        wout_s = sb("wout_s", [128, KD, D])
        lnq_s = sb("lnq_s", [128, 2])
        lnkv_s = sb("lnkv_s", [KPH, 2, 2])
        wh_s = sb("wh_s", [128, XH, HD])
        wg_s = sb("wg_s", [128, KD, D])
        wo_s = sb("wo_s", [128, KD, D])
        gn_s = sb("gn_s", [128, KD, 2])
        gate_s = sb("gate_s", [128, KD, E])
        gu_s = sb("gu_s", [128, KD, E, 2 * I])
        dn_s = sb("dn_s", [IH, 2, E, D])
        sgu_s = sb("sgu_s", [128, KD, 2 * SI])
        x_s = sb("x_s", [128, B, D])
        x1_s = sb("x1_s", [128, B, D])
        qw_s = sb("qw_s", [128, B, 4, T])
        ck_s = sb("ck_s", [128, XH, B, T])
        cv_s = sb("cv_s", [128, B, XH, HD])
        kbd = sb("kbd", [128, 2, 2, 8, T])
        xh = sb("xh", [128, 2, D])
        xT = sb("xT", [128, 2, KD, T])
        lat = sb("lat", [128, 2, QP + KP])
        cqT = sb("cqT", [128, 2, T])
        ckvT = sb("ckvT", [KPH, 2, 2, T])
        qk = sb("qk", [128, 2, 2 * D])
        rope_t = sb("rope_t", [128, 2, 2, 2 * ROPE])
        v_s = sb("v_s", [128, 3, H, DH + 1])
        qkT = sb("qkT", [128, 2, 4, T])
        mx = sb("mx", [128, 2, CH])
        sc_s = sb("sc_s", [128, 2, CH, T])
        pr_s = sb("pr_s", [128, 2, CH, T])
        prT = sb("prT", [128, 2, CH, T])
        rden = sb("rden", [128, 2, H])
        o_s = sb("o_s", [128, 2, D])
        oT = sb("oT", [128, 2, KD, T])
        xb = sb("xb", [128, 2, D])
        xbT = sb("xbT", [128, 2, KD, T])
        cs = qw_s[:].rearrange("p b k t -> p (b k t)")[:, 0:B * D].rearrange("p (b d) -> p b d", b=B)
        cT = pr_s[:].rearrange("p r h t -> p (r h t)").rearrange("p (h j t) -> p h j t", h=XH, j=4)
        st = sb("st", [128, 2, 6])
        ag = sb("ag", [128, 2, 2, 2])
        ve = sb("ve", [128, 2, 2, 1])
        rs = sb("rs", [128, 2, 2, 1])
        agp = sb("agp", [128, 2, 2, 2, 2])
        vep = sb("vep", [128, 2, 2, 2])
        rsp = sb("rsp", [128, 2, 2, 2])
        ag2 = sb("ag2", [128, 2, 2, 2])
        ve2 = sb("ve2", [128, 2, 2])
        rs2 = sb("rs2", [128, 2, 2])
        LX, LX1 = range(2)
        MIX, FFN = range(2)

        bank = [ctx.enter_context(nc.psum_tensor(f"bank{i}", [128, 512], f32)) for i in range(8)]

        NX = 3
        XPARTS = [(0, 1), (1, 3), (3, 8)]
        s_x = [sem(f"s_x{i}") for i in range(NX)]
        s_tab, s_tabb, s_wm, s_wq, s_wkv, s_lnv, s_wout, s_ctx0, s_ctx1, s_wh, s_wgo, s_gate, s_shw, s_gu, s_dn = [
            sem(n) for n in "s_tab s_tabb s_wm s_wq s_wkv s_lnv s_wout s_ctx0 s_ctx1 s_wh s_wgo s_gate s_shw s_gu s_dn".split()]
        s_tabr = sem("s_tabr")
        c_bf, c_set = sem("c_bf"), sem("c_set")
        p_t1, p_m1, p_t2, p_kv, p_q, p_t3, p_s, p_pt, p_pv, p_t5, p_wo, p_bt, p_bqw, p_sc = [
            sem(n) for n in "p_t1 p_m1 p_t2 p_kv p_q p_t3 p_s p_pt p_pv p_t5 p_wo p_bt p_bqw p_sc".split()]
        p_ct, p_ck, p_cv = sem("p_ct"), sem("p_ck"), sem("p_cv")
        chain = sem("chain")
        v_xv, v_xh, v_q, v_sb, v_x1, v_x1v, v_xb, v_mv, v_lat, v_on = [
            sem(n) for n in "v_xv v_xh v_q v_sb v_x1 v_x1v v_xb v_mv v_lat v_on".split()]
        a_exp, a_kv, a_ot, a_xT, a_qkT, a_prT, a_bt, a_qw, a_lat, a_ct, a_ck, a_cv = [
            sem(n) for n in "a_exp a_kv a_ot a_xT a_qkT a_prT a_bt a_qw a_lat a_ct a_ck a_cv".split()]
        g_x, g_m, g_x1, g_kbd = [sem(n) for n in "g_x g_m g_x1 g_kbd".split()]
        v_at, p_o, v_ov, g_o, v_yh, p_ty, a_ty, g_z, p_xo, v_x2v, g_x2, v_xf, p_tf, a_tf, p_lg = [
            sem(n) for n in "v_at p_o v_ov g_o v_yh p_ty a_ty g_z p_xo v_x2v g_x2 v_xf p_tf a_tf p_lg".split()]
        v_x2 = sem("v_x2")
        v_lg, a_re, v_top, p_rk, v_pos, v_blk = [sem(n) for n in "v_lg a_re v_top p_rk v_pos v_blk".split()]
        v_hot, p_tb, v_idx, d_xf = [sem(n) for n in "v_hot p_tb v_idx d_xf".split()]
        p_sg, a_sg, v_sh, p_sT, a_sT, p_sd, v_sd = [sem(n) for n in "p_sg a_sg v_sh p_sT a_sT p_sd v_sd".split()]
        d_bx = [sem(f"d_bx{i}") for i in range(RB)]
        d_by = [sem(f"d_by{i}") for i in range(RB)]
        p_bT, v_bT, p_gu, a_si, v_h, p_hT, a_hT, p_dn, v_y = [
            sem(n) for n in "p_bT v_bT p_gu a_si v_h p_hT a_hT p_dn v_y".split()]
        d_g = [sem(f"d_g{i}") for i in range(4)]
        v_f1, d_out = sem("v_f1"), sem("d_out")

        def carve(t, cols):
            flat, at = t
            t[1] = at + cols
            return flat[:, at:at + cols]

        scr = [sc_s[:].rearrange("p r h t -> p (r h t)"), 0]
        prr = [pr_s[:].rearrange("p r h t -> p (r h t)"), 0]
        ptr = [prT[:].rearrange("p r h t -> p (r h t)"), 0]
        qtr = [qkT[:].rearrange("p r h t -> p (r h t)"), 0]
        qkr = [qk[:].rearrange("p r t -> p (r t)"), 0]
        aT = carve(scr, XH * T).rearrange("p (h t) -> p h t", h=XH)
        atmp = carve(scr, XH * T).rearrange("p (h t) -> p h t", h=XH)
        yh = xh
        yT = xT
        zT = oT
        xfT = ck_s
        lg = carve(qtr, B * E).rearrange("p (t e) -> p t e", t=B)
        ex = carve(qtr, B * E).rearrange("p (t e) -> p t e", t=B)
        prob = carve(qtr, B * E).rearrange("p (t e) -> p t e", t=B)
        s8 = sb("s8", [128, 8, B])
        oh = carve(qtr, 2 * B * E).rearrange("p (k t e) -> p k t e", k=2, t=B)
        t128 = carve(qtr, 2 * B * E).rearrange("p (k t e) -> p k t e", k=2, t=B)
        ohp = carve(qkr, 2 * B * E).rearrange("p (k t e) -> p k t e", k=2, t=B)
        mb = sb("mb", [128, B, E], bf16)
        cmp = carve(qkr, E * E).rearrange("p (a b) -> p a b", a=E)
        nb = sb("nb", [128, 3, E])
        posi = sb("posi", [128, 3, 2 * B], i32)
        posf = sb("posf", [128, 3, 2 * B])
        bcmp = carve(qkr, BLOCKS * E)[0:1, :].rearrange("p (a b) -> p a b", a=BLOCKS)
        be = sb("be", [1, 2, BLOCKS])
        bei = sb("bei", [1, BLOCKS], i32)
        spare = [kbd[:].rearrange("p a g h t -> p (a g h t)"), 0]
        sg = carve(spare, 2 * SI).rearrange("p (r n) -> p r n", r=2)
        sh = carve(spare, 2 * SI).rearrange("p (r n) -> p r n", r=2)
        shT = carve(spare, 6 * T).rearrange("p (r k t) -> p r k t", r=2, k=3)
        sdn_s = carve(spare, 3 * D).rearrange("p (k n) -> p k n", k=3)
        by = carve(spare, RB * D).rearrange("p (r n) -> p r n", r=RB)
        qwr = [qw_s[:].rearrange("p b k t -> p (b k t)"), 0]
        hot = carve(qwr, 2 * B * T).rearrange("p (n t) -> p n t", n=2 * B)
        num = carve(qwr, 2 * B * BLOCKS).rearrange("p (n b) -> p n b", n=2 * B)
        bx = carve(qwr, RB * D).rearrange("p (r n) -> p r n", r=RB)
        yg = cv_s[:].rearrange("p b h e -> p (b h e)").rearrange("p (r k d) -> p r k d", r=4, k=2)
        bxT = xbT
        bs = carve(prr, 2 * I).rearrange("p (r n) -> p r n", r=2)
        bh = carve(prr, 2 * I).rearrange("p (r n) -> p r n", r=2)
        bhT = carve(ptr, 4 * T)[0:IH, :].rearrange("p (r k t) -> p r k t", r=2, k=2)
        idx = ptr[0][:, ptr[1]:].bitcast(i32)[:, 0:2 * BLOCKS].rearrange("p (k b) -> p k b", k=2)
        ids = ptr[0][:, ptr[1] + 64:ptr[1] + 64 + 4 * BLOCKS].rearrange("p (k b) -> p k b", k=4)

        def xpart(b):
            return [i for i, (lo, hi) in enumerate(XPARTS) if lo <= b < hi][0]

        block = ctx.enter_context(nc.Block())

        @block.sync
        def _(sp):
            xv = x.rearrange("b p d -> p b d")
            cv = ctx_in.rearrange("b p d -> p b d")
            for i, (lo, hi) in enumerate(XPARTS[:1]):
                sp.dma_start(x_s[:, lo:hi, :], xv[:, lo:hi, :]).then_inc(s_x[i], 16)
            sp.dma_start(tab[:], table).then_inc(s_tab, 16)
            sp.dma_start(tabb[:], table_b).then_inc(s_tabb, 16)
            sp.dma_start(wm_s[:], w_m.rearrange("(k p) n -> p k n", p=128)).then_inc(s_wm, 16)
            sp.dma_start(cs[:, 0:4, :], cv[:, 0:4, :]).then_inc(s_ctx0, 16)
            sp.dma_start(wh_s[:], wh.rearrange("h p n -> p h n")).then_inc(s_wh, 16)
            sp.dma_start(x_s[:, 1:3, :], xv[:, 1:3, :]).then_inc(s_x[1], 16)
            sp.dma_start(wq_s[:], w_q).then_inc(s_wq, 16)
            sp.dma_start(wkv_s[:], w_kv.rearrange("(k p) n -> p k n", p=KPH)).then_inc(s_wkv, 16)
            sp.dma_start(lnq_s[:], ln_q).then_inc(s_lnv, 16)
            sp.dma_start(lnkv_s[:], ln_kv.rearrange("(k p) n -> p k n", p=KPH)).then_inc(s_lnv, 16)
            sp.dma_start(x_s[:, 3:8, :], xv[:, 3:8, :]).then_inc(s_x[2], 16)
            sp.dma_start(cs[:, 4:8, :], cv[:, 4:8, :]).then_inc(s_ctx1, 16)
            sp.dma_start(wout_s[:], w_out.rearrange("(k p) n -> p k n", p=128)).then_inc(s_wout, 16)
            sp.dma_start(wg_s[:], wg.rearrange("(k p) n -> p k n", p=128)).then_inc(s_wgo, 16)
            sp.dma_start(wo_s[:], wo.rearrange("(k p) n -> p k n", p=128)).then_inc(s_wgo, 16)
            sp.dma_start(gn_s[:], gn.rearrange("(k p) n -> p k n", p=128)).then_inc(s_wgo, 16)
            sp.dma_start(gate_s[:], gate.rearrange("(k p) n -> p k n", p=128)).then_inc(s_gate, 16)
            sp.dma_start(sgu_s[:], s_gu_d.rearrange("(k p) n -> p k n", p=128)).then_inc(s_shw, 16)
            for k in range(KD):
                for e in range(0, E, 4):
                    sp.dma_start(gu_s[:, k, e:e + 4, :],
                                 w_gu[e:e + 4, k * 128:(k + 1) * 128, :].rearrange("e p n -> p e n")).then_inc(s_gu, 16)
            for k in range(2):
                for e in range(0, E, 8):
                    sp.dma_start(dn_s[:, k, e:e + 8, :],
                                 w_dn[e:e + 8, k * IH:(k + 1) * IH, :].rearrange("e p n -> p e n")).then_inc(s_dn, 16)
            sp.wait_ge(p_m1, B)
            sp.dma_start(tabr, table_r).then_inc(s_tabr, 16)
            sp.wait_ge(p_s, NC * B)
            sp.dma_start(sdn_s[:, 0:2, :], s_dn_d[0:256, :].rearrange("(k p) n -> p k n", p=128)).then_inc(s_shw, 16)
            sp.dma_start(sdn_s[0:SI - 256, 2, :], s_dn_d[256:SI, :]).then_inc(s_shw, 16)
            for q in range(PAIRS):
                sp.wait_ge(v_xf, q + 1)
                sp.dma_start(ffn_in[2 * q * T:2 * (q + 1) * T, :].rearrange("(b p) d -> p b d", b=2),
                             x1_s[:, 2 * q:2 * q + 2, :]).then_inc(d_xf, 16)
            for r in range(RB):
                sp.wait_ge(d_by[r], 16 * len(range(r, BLOCKS, RB)))
            for t in range(B):
                if t >= 4:
                    sp.wait_ge(v_f1, 2 * (t - 3))
                sp.dma_start(yg[:, t % 4, :, :],
                             expert_out[0:SLOTS, :].rearrange("(k b p) d -> b p k d", k=2, b=B)[t]).then_inc(d_g[t % 4], 16)
            sp.wait_ge(d_out, 16 * B)

        @block.gpsimd
        def _(pool):
            nc.gpsimd.memset(halfpow[:], -0.5).then_inc(c_set, 1)
            nc.gpsimd.memset(v_s[:, :, :, DH:DH + 1], 1.0).then_inc(c_set, 1)
            pool.wait_ge(c_set, 2)

            def rsqrt(kind, b, ready, done):
                pool.wait_ge(ready, b + 1)
                nc.gpsimd.tensor_tensor(rs[:, kind, b % 2, :], ve[:, kind, b % 2, :], halfpow[:, 0:1],
                                        ALU.pow).then_inc(done, 1)

            def rsqrt_latent(b):
                pool.wait_ge(v_mv, b + 1)
                nc.gpsimd.tensor_tensor(rs2[:, b % 2, :], ve2[:, b % 2, :], halfpow[:], ALU.pow).then_inc(g_m, 1)

            def expand(b, g):
                pool.wait_ge(a_qkT, b + 1)
                if b >= 2:
                    pool.wait_ge(p_s, NC * (b - 2) + 2 * (g + 1))
                nc.gpsimd.tensor_tensor(
                    kbd[:, b % 2, g, :, :],
                    qkT[:, b % 2, 2 + g, :].unsqueeze(1).to_broadcast([128, 8, T]),
                    tab[:, C_HEAD:C_HEAD + 8].unsqueeze(2).to_broadcast([128, 8, T]), ALU.mult).then_inc(g_kbd, 1)

            pool.wait_ge(s_tab, 16)
            rsqrt(LX, 0, v_xv, g_x)
            tiles = lambda b: 0 <= b < B
            for i in range(-2, B + 3):
                if tiles(i - 2):
                    rsqrt(LX1, i - 2, v_x1v, g_x1)
                if tiles(i + 2):
                    rsqrt_latent(i + 2)
                if 0 < i + 3 < B:
                    rsqrt(LX, i + 3, v_xv, g_x)
                if tiles(i + 1):
                    expand(i + 1, 0)
                    expand(i + 1, 1)
            def rsqrt_pair(kind, q, ready, done):
                pool.wait_ge(ready, q + 1)
                nc.gpsimd.tensor_tensor(rsp[:, kind, q % 2, :], vep[:, kind, q % 2, :], halfpow[:], ALU.pow).then_inc(done, 1)

            def gate_mix(q):
                pool.wait_ge(a_ty, q + 1)
                if q >= 1:
                    pool.wait_ge(p_xo, q)
                nc.gpsimd.tensor_tensor(zT[:], qw_s[:, 2 * q:2 * q + 2, XH:XH + KD, :].rearrange("p b k t -> p k b t"),
                                        yT[:], ALU.mult).then_inc(g_z, 1)

            for j in range(PAIRS + 2):
                if j < PAIRS:
                    rsqrt_pair(MIX, j, v_ov, g_o)
                if j >= 2:
                    rsqrt_pair(FFN, j - 2, v_x2v, g_x2)
                if 0 <= j - 1 < PAIRS:
                    gate_mix(j - 1)

            pool.wait_ge(d_xf, 16 * PAIRS)
            pool.wait_ge(v_idx, 1)
            for i in range(BLOCKS + RB + 1):
                if i < BLOCKS:
                    if i >= RB:
                        pool.wait_ge(p_bT, i - RB + 1)
                    pool.indirect_dma_start(bx[:, i % RB, :], None, ffn_in[:],
                                            bass.IndirectOffsetOnAxis(ap=idx[:, 0, i:i + 1], axis=0)).then_inc(d_bx[i % RB], 16)
                k = i - RB - 1
                if k >= 0:
                    pool.wait_ge(v_y, k + 1)
                    pool.indirect_dma_start(expert_out[:], bass.IndirectOffsetOnAxis(ap=idx[:, 1, k:k + 1], axis=0),
                                            by[:, k % RB, :], None).then_inc(d_by[k % RB], 16)

        @block.tensor
        def _(pe):
            mm, tr = nc.tensor.matmul, nc.tensor.transpose

            def front_transpose(b):
                pe.wait_ge(v_xh, b + 1)
                if b >= 5:
                    pe.wait_ge(a_qw, b - 4)
                for k in range(KD):
                    last = tr(bank[5][:, k * T:(k + 1) * T], xh[:, b % 2, k * 128:(k + 1) * 128], idf)
                last.then_inc(p_t1, 1)

            def front_project(b):
                pe.wait_ge(a_xT, b + 1)
                if b >= 1:
                    pe.wait_ge(v_q, b)
                for k in range(KD):
                    last = mm(bank[4][:, 0:MW], xT[:, b % 2, k, :], wm_s[:, k, :], start=k == 0, stop=k == KD - 1)
                last.then_inc(p_m1, 1)

            def latent_transpose(b):
                pe.wait_ge(v_lat, b + 1)
                tr(bank[4][:, 0:T], lat[:, b % 2, 0:QP], idf)
                for k in range(2):
                    last = tr(bank[4][0:KPH, (k + 1) * T:(k + 2) * T],
                              lat[:, b % 2, QP + k * KPH:QP + (k + 1) * KPH], idf)
                last.then_inc(p_t2, 1)

            def keys_values(b):
                pe.wait_ge(a_lat, b + 1)
                if b >= 3:
                    pe.wait_ge(a_ot, b - 2)
                for k in range(2):
                    last = mm(bank[3][:, 0:NOPE + D], ckvT[:, b % 2, k, :], wkv_s[:, k, :], start=k == 0, stop=k == 1)
                last.then_inc(p_kv, 1)
                mm(bank[4][:, 0:QW], cqT[:, b % 2, :], wq_s[:], start=True, stop=True).then_inc(p_q, 1)

            def qk_transpose(b):
                pe.wait_ge(v_q, b + 1)
                pe.wait_ge(a_kv, b + 1)
                pe.wait_ge(a_xT, min(b + 2, B))
                for k in range(4):
                    last = tr(bank[5][:, k * T:(k + 1) * T], qk[:, b % 2, k * 128:(k + 1) * 128], idf)
                last.then_inc(p_t3, 1)

            def scores(n):
                b, c = n // NC, n % NC
                g = c // 2
                if c == 0:
                    pe.wait_ge(a_qkT, b + 1)
                if c % 2 == 0:
                    pe.wait_ge(g_kbd, 2 * b + g + 1)
                if n >= 2:
                    pe.wait_ge(v_sb, n - 1)
                h0 = (c % 2) * CH
                o = bank[n % 2][:].rearrange("p (h k) -> p h k", h=CH)
                mm(o, qkT[:, b % 2, g, :], kbd[:, b % 2, g, h0:h0 + CH, :], start=True, stop=False)
                mm(o, idb, maskb.unsqueeze(1).to_broadcast([128, CH, T]), start=False, stop=True).then_inc(p_s, 1)

            def prob_transpose(n):
                pe.wait_ge(a_exp, n + 1)
                if n >= 1:
                    pe.wait_ge(a_prT, n)
                for h in range(CH):
                    last = tr(bank[2][:, h * T:(h + 1) * T], pr_s[:, n % 2, h, :], idf)
                last.then_inc(p_pt, 1)

            def weigh_values(n):
                b, c = n // NC, n % NC
                pe.wait_ge(a_prT, n + 1)
                if c == 0 and b >= 1:
                    pe.wait_ge(v_on, b)
                for h in range(CH):
                    hh = c * CH + h
                    last = mm(bank[6][:, hh * (DH + 1):(hh + 1) * (DH + 1)], prT[:, n % 2, h, :],
                              v_s[:, b % 3, hh, :], start=True, stop=True)
                last.then_inc(p_pv, 1)

            def out_transpose(b):
                pe.wait_ge(v_on, b + 1)
                if b >= 1:
                    pe.wait_ge(a_bt, b)
                for k in range(KD):
                    last = tr(bank[3][:, k * T:(k + 1) * T], o_s[:, b % 2, k * 128:(k + 1) * 128], idf)
                last.then_inc(p_t5, 1)

            def out_project(b):
                pe.wait_ge(a_ot, b + 1)
                pe.wait_ge(a_kv, min(b + 4, B))
                for k in range(KD):
                    last = mm(bank[3][:, 0:D], oT[:, b % 2, k, :], wout_s[:, k, :], start=k == 0, stop=k == KD - 1)
                last.then_inc(p_wo, 1)

            def cross_transpose(b):
                pe.wait_ge(v_xb, b + 1)
                for k in range(KD):
                    last = tr(bank[3][:, k * T:(k + 1) * T], xb[:, b % 2, k * 128:(k + 1) * 128], idf)
                last.then_inc(p_bt, 1)

            def cross_project(b):
                pe.wait_ge(a_bt, b + 1)
                pe.wait_ge(a_qkT, min(b + 4, B))
                for h in range(XH):
                    mm(bank[5][:, h * T:(h + 1) * T], wh_s[:, h, :], xbT[:, b % 2, h, :], start=True, stop=True)
                for m in range(KD):
                    for k in range(KD):
                        last = mm(bank[5][:, (XH + m) * T:(XH + m + 1) * T], wg_s[:, k, m * 128:(m + 1) * 128],
                                  xbT[:, b % 2, k, :], start=k == 0, stop=k == KD - 1)
                last.then_inc(p_bqw, 1)

            def cross_scores(b):
                pe.wait_ge(a_qw, b + 1)
                for h in range(XH):
                    last = mm(bank[7][:, h * T:(h + 1) * T], ck_s[:, h, b, :], qw_s[:, b, h, :],
                              start=b == 0 and h == 0, stop=b == B - 1, skip_group_check=True)
                last.then_inc(p_sc, 1)

            def ctx_part(g, step):
                if step == 0:
                    pe.wait_ge((s_ctx0, s_ctx1)[g], 16)
                    for h in range(XH):
                        for j in range(4):
                            last = tr(bank[6 + h][:, j * T:(j + 1) * T], cs[:, 4 * g + j, h * HD:(h + 1) * HD], idf)
                        last.then_inc(p_ct, 1)
                if step == 1:
                    pe.wait_ge(s_wh, 16)
                    for h in range(XH):
                        pe.wait_ge(a_ct, XH * g + h + 1)
                        if g:
                            pe.wait_ge(a_cv, 2)
                        mm(bank[h][:], wh_s[:, h, :], cT[:, h, :, :], start=True, stop=True).then_inc(p_ck, 1)
                if step == 2:
                    pe.wait_ge(a_ck, XH * (g + 1))
                    for j in range(4):
                        for h in range(XH):
                            last = mm(bank[1 + j // 2][:, (j % 2) * D + h * HD:(j % 2) * D + (h + 1) * HD],
                                      cT[:, h, j, :], wh_s[:, h, :], start=True, stop=True)
                        if j % 2:
                            last.then_inc(p_cv, 1)

            tiles = lambda b: 0 <= b < B

            def attention(n):
                if 0 <= n < NC * B:
                    scores(n)
                if 0 <= n - 2 < NC * B:
                    prob_transpose(n - 2)
                if 0 <= n - 3 < NC * B:
                    weigh_values(n - 3)

            pe.wait_ge(s_tab, 16)
            for i in range(-2, B + 3):
                if i == -1:
                    pe.wait_ge(s_wq, 16)
                    pe.wait_ge(s_wkv, 16)
                if i == 0:
                    pe.wait_ge(s_tabb, 16)
                    pe.wait_ge(a_cv, 4)
                if i == 2:
                    pe.wait_ge(s_wout, 16)
                    pe.wait_ge(s_wgo, 48)
                attention(NC * i)
                if tiles(i + 1):
                    keys_values(i + 1)
                if tiles(i + 2):
                    front_transpose(i + 2)
                if i == -2:
                    ctx_part(0, 0)
                    pe.wait_ge(s_wm, 16)
                attention(NC * i + 1)
                if tiles(i - 2):
                    out_project(i - 2)
                if tiles(i + 2):
                    front_project(i + 2)
                if i == -2:
                    ctx_part(0, 1)
                    ctx_part(0, 2)
                attention(NC * i + 2)
                if i == -1:
                    ctx_part(1, 0)
                    ctx_part(1, 1)
                if tiles(i + 1):
                    qk_transpose(i + 1)
                if tiles(i - 2):
                    cross_transpose(i - 2)
                if tiles(i - 3):
                    cross_scores(i - 3)
                if i == -1:
                    ctx_part(1, 2)
                attention(NC * i + 3)
                if tiles(i + 2):
                    latent_transpose(i + 2)
                if tiles(i - 2):
                    cross_project(i - 2)
                if tiles(i - 1):
                    out_transpose(i - 1)

            def cross_mix(q):
                pe.wait_ge(v_yh, q) if q else pe.wait_ge(v_at, 1)
                for h in range(XH):
                    last = mm(bank[0][:].rearrange("p (b h e) -> p b h e", b=2, h=XH)[:, :, h, :], aT[:, h, :],
                              cv_s[:, 2 * q:2 * q + 2, h, :], start=h == 0, stop=h == XH - 1, skip_group_check=True)
                last.then_inc(p_o, 1)

            def mix_transpose(q):
                pe.wait_ge(v_yh, q + 1)
                if q >= 1:
                    pe.wait_ge(a_ty, q)
                for b in range(2):
                    for k in range(KD):
                        last = tr(bank[2][:, (2 * k + b) * T:(2 * k + b + 1) * T], yh[:, b, k * 128:(k + 1) * 128], idf)
                last.then_inc(p_ty, 1)

            def cross_out(q):
                pe.wait_ge(g_z, q + 1)
                if q >= 1:
                    pe.wait_ge(v_x2, q)
                for b in range(2):
                    for k in range(KD):
                        last = mm(bank[3][:, b * D:(b + 1) * D], zT[:, k, b, :], wo_s[:, k, :], start=k == 0, stop=k == KD - 1)
                last.then_inc(p_xo, 1)

            def ffn_transpose(q):
                pe.wait_ge(v_xf, q + 1)
                if q >= 1:
                    pe.wait_ge(a_tf, q)
                for b in range(2):
                    for k in range(KD):
                        last = tr(bank[4][:, (2 * k + b) * T:(2 * k + b + 1) * T],
                                  x1_s[:, 2 * q + b, k * 128:(k + 1) * 128], idf)
                last.then_inc(p_tf, 1)

            def router(q):
                pe.wait_ge(a_tf, q + 1)
                for b in (2 * q, 2 * q + 1):
                    for k in range(KD):
                        last = mm(bank[5][:, b * E:(b + 1) * E], xfT[:, k, b, :], gate_s[:, k, :],
                                  start=k == 0, stop=k == KD - 1)
                last.then_inc(p_lg, 1)

            def shared_banks(b):
                return (6, 7) if b < 2 or b % 2 == 0 else (3, 4)

            def shared_up(b):
                pe.wait_ge(a_tf, b // 2 + 1)
                if b in (1, 2):
                    pe.wait_ge(v_sh, b)
                elif b >= 4:
                    pe.wait_ge(v_sh, b - 1)
                for m, n in enumerate(shared_banks(b)):
                    for k in range(KD):
                        last = mm(bank[n][:, 0:SI], xfT[:, k, b, :], sgu_s[:, k, m * SI:(m + 1) * SI],
                                  start=k == 0, stop=k == KD - 1)
                last.then_inc(p_sg, 1)

            def shared_transpose(b):
                pe.wait_ge(v_sh, b + 1)
                if b >= 1:
                    pe.wait_ge(v_sd, b)
                for k in range(3):
                    r = min(128, SI - k * 128)
                    last = tr(bank[1][0:r, k * T:(k + 1) * T], sh[:, b % 2, k * 128:k * 128 + r], idf)
                last.then_inc(p_sT, 1)

            def shared_down(b):
                pe.wait_ge(a_sT, b + 1)
                for k in range(3):
                    r = min(128, SI - k * 128)
                    last = mm(bank[1][:, 0:D], shT[0:r, b % 2, k, :], sdn_s[0:r, k, :], start=k == 0, stop=k == 2)
                last.then_inc(p_sd, 1)

            def count_pairs():
                pe.wait_ge(v_top, 1)
                pe.wait_ge(c_bf, 1)
                rank = bank[0][:, 0:B * E]
                for t in range(B - 1):
                    mm(rank[:, (t + 1) * E:].rearrange("p (t e) -> p t e", e=E), onesb[:],
                       mb[:, t:t + 1, :].to_broadcast([128, B - 1 - t, E]), start=t == 0, stop=False,
                       skip_group_check=True)
                mm(rank, trib, mb[:].rearrange("p t e -> p (t e)"), start=False, stop=True, skip_group_check=True)
                for t in range(B):
                    last = mm(bank[2][:, 0:E], onesb[:], mb[:, t, :], start=t == 0, stop=t == B - 1)
                last.then_inc(p_rk, 1)

            def slot_table():
                pe.wait_ge(v_hot, 1)
                for k in range(2):
                    for t in range(B):
                        last = mm(bank[5][:, k * BLOCKS:(k + 1) * BLOCKS], hot[:, k * B + t, :], num[:, k * B + t, :],
                                  start=t == 0, stop=t == B - 1)
                last.then_inc(p_tb, 1)

            pe.wait_ge(s_gate, 16)
            for j in range(PAIRS + 3):
                if j < PAIRS:
                    cross_mix(j)
                if 0 <= j - 3 < PAIRS:
                    router(j - 3)
                if 0 <= j - 2 < PAIRS:
                    cross_out(j - 2)
                if 0 <= j - 1 < PAIRS:
                    mix_transpose(j - 1)
                if j == 3:
                    pe.wait_ge(s_shw, 48)
                    shared_up(0)
                if j == 4:
                    shared_transpose(0)
                    shared_down(0)
                    shared_up(1)
                if j == 5:
                    shared_transpose(1)
                    shared_down(1)
                if 0 <= j - 2 < PAIRS:
                    ffn_transpose(j - 2)
            shared_up(2)
            for b in range(2, B):
                if b + 1 < B:
                    shared_up(b + 1)
                shared_transpose(b)
                if b == 4:
                    count_pairs()
                if b == 6:
                    slot_table()
                shared_down(b)

            pe.wait_ge(s_gu, 16 * 8)
            pe.wait_ge(s_dn, 16 * 4)

            def block_transpose(slot, nth, i):
                pe.wait_ge(d_bx[slot], 16 * nth + 16)
                if not (isinstance(i, int) and i == 0):
                    pe.wait_ge(v_bT, i)
                for k in range(KD):
                    last = tr(bank[0][:, k * T:(k + 1) * T], bx[:, slot, k * 128:(k + 1) * 128], idf)
                last.then_inc(p_bT, 1)

            def hidden_transpose(i, par):
                pe.wait_ge(v_h, i + 1)
                for k in range(2):
                    last = tr(bank[1][0:IH, k * T:(k + 1) * T], bh[:, par, k * IH:(k + 1) * IH], idf)
                last.then_inc(p_hT, 1)

            def expert_up(i, par, e):
                pe.wait_ge(v_bT, i + 1)
                for k in range(KD):
                    last = mm(bank[2 + par][:, 0:2 * I], bxT[:, par, k, :], gu_s[:, k, bass.ds(e, 1), :],
                              start=k == 0, stop=k == KD - 1)
                last.then_inc(p_gu, 1)

            def expert_down(i, par, e):
                pe.wait_ge(a_hT, i + 1)
                for k in range(2):
                    last = mm(bank[4 + par][:, 0:D], bhT[:, par, k, :], dn_s[:, k, bass.ds(e, 1), :],
                              start=k == 0, stop=k == 1)
                last.then_inc(p_dn, 1)

            def expert_of(i):
                return pe.value_load(bei[0:1, bass.ds(i, 1)], min_val=0, max_val=E - 1)

            def step(i, j, nth):
                par = (j + 1) % 2
                block_transpose((j + 2) % RB, nth + (j + 2) // RB, i + 1)
                hidden_transpose(i - 1, 1 - par)
                expert_up(i, par, expert_of(i))
                expert_down(i - 1, 1 - par, expert_of(i - 1))

            block_transpose(0, 0, 0)
            block_transpose(1, 0, 1)
            pe.wait_ge(v_blk, 1)
            expert_up(0, 0, expert_of(0))
            FULL = (BLOCKS - 2) // RB
            with pe.Fori(0, FULL) as nth:
                for j in range(RB):
                    step(nth * RB + (j + 1), j, nth)
            for i in range(RB * FULL + 1, BLOCKS - 1):
                step(i, i - 1 - RB * FULL, FULL)
            i = BLOCKS - 1
            hidden_transpose(i - 1, 1 - i % 2)
            expert_up(i, i % 2, expert_of(i))
            expert_down(i - 1, 1 - i % 2, expert_of(i - 1))
            hidden_transpose(i, i % 2)
            expert_down(i, i % 2, expert_of(i))

        @block.scalar
        def _(act):
            copy = lambda o, i: nc.scalar.activation(o, i, ACT.Copy)

            def exps(n):
                act.wait_ge(v_sb, n + 1)
                if n >= 2:
                    act.wait_ge(p_pt, n - 1)
                nc.scalar.activation(pr_s[:, n % 2, :, :], sc_s[:, n % 2, :, :], ACT.Exp, scale=DH ** -0.5).then_inc(a_exp, 1)

            def kv_out(b):
                act.wait_ge(p_kv, b + 1)
                if b >= 2:
                    act.wait_ge(p_t3, b - 1)
                if b >= 3:
                    act.wait_ge(p_pv, NC * (b - 2))
                copy(qk[:, b % 2, D:D + NOPE], bank[3][:, 0:NOPE])
                copy(v_s[:, b % 3, :, 0:DH], bank[3][:, NOPE:NOPE + D].rearrange("p (h d) -> p h d", h=H)).then_inc(a_kv, 1)

            def ot_out(b):
                act.wait_ge(p_t5, b + 1)
                if b >= 2:
                    act.wait_ge(p_wo, b - 1)
                copy(oT[:, b % 2, :, :].rearrange("p k t -> p (k t)"), bank[3][:, 0:D]).then_inc(a_ot, 1)

            def xT_out(b):
                act.wait_ge(p_t1, b + 1)
                if b >= 2:
                    act.wait_ge(p_m1, b - 1)
                copy(xT[:, b % 2, :, :].rearrange("p k t -> p (k t)"), bank[5][:, 0:D]).then_inc(a_xT, 1)

            def qkT_out(b):
                act.wait_ge(p_t3, b + 1)
                if b >= 2:
                    act.wait_ge(p_s, NC * (b - 1))
                    act.wait_ge(g_kbd, 2 * (b - 1))
                copy(qkT[:, b % 2, :, :].rearrange("p k t -> p (k t)"), bank[5][:, 0:4 * T]).then_inc(a_qkT, 1)

            def prT_out(n):
                act.wait_ge(p_pt, n + 1)
                if n >= 2:
                    act.wait_ge(p_pv, n - 1)
                copy(prT[:, n % 2, :, :].rearrange("p k t -> p (k t)"), bank[2][:]).then_inc(a_prT, 1)

            def xbT_out(b):
                act.wait_ge(p_bt, b + 1)
                if b >= 2:
                    act.wait_ge(p_bqw, b - 1)
                copy(xbT[:, b % 2, :, :].rearrange("p k t -> p (k t)"), bank[3][:, 0:D]).then_inc(a_bt, 1)

            def qw_out(b):
                act.wait_ge(p_bqw, b + 1)
                copy(qw_s[:, b, 0:XH, :].rearrange("p k t -> p (k t)"), bank[5][:, 0:XH * T])
                nc.scalar.activation(qw_s[:, b, XH:XH + KD, :].rearrange("p k t -> p (k t)"), bank[5][:, XH * T:],
                                     ACT.Relu).then_inc(a_qw, 1)

            def latents_out(b):
                act.wait_ge(p_t2, b + 1)
                if b >= 2:
                    act.wait_ge(p_q, b - 1)
                nc.scalar.activation(cqT[:, b % 2, :], bank[4][:, 0:T], ACT.Identity, scale=lnq_s[:, 0:1], bias=lnq_s[:, 1:2])
                for k in range(2):
                    last = nc.scalar.activation(ckvT[:, b % 2, k, :], bank[4][0:KPH, (k + 1) * T:(k + 2) * T],
                                                ACT.Identity, scale=lnkv_s[:, k, 0:1], bias=lnkv_s[:, k, 1:2])
                last.then_inc(a_lat, 1)

            def ctx_out(g):
                for h in range(XH):
                    act.wait_ge(p_ct, XH * g + h + 1)
                    if g:
                        act.wait_ge(p_cv, 2)
                    copy(cT[:, h, :, :].rearrange("p j t -> p (j t)"), bank[6 + h][:]).then_inc(a_ct, 1)
                for h in range(XH):
                    act.wait_ge(p_ck, XH * g + h + 1)
                    copy(ck_s[:, h, 4 * g:4 * g + 4, :].rearrange("p j t -> p (j t)"), bank[h][:]).then_inc(a_ck, 1)
                for j in range(2):
                    act.wait_ge(p_cv, 2 * g + j + 1)
                    copy(cv_s[:, 4 * g + 2 * j:4 * g + 2 * j + 2, :, :].rearrange("p j h t -> p (j h t)"),
                         bank[1 + j][:]).then_inc(a_cv, 1)

            tiles = lambda b: 0 <= b < B

            def attention(n):
                if 0 <= n - 2 < NC * B:
                    prT_out(n - 2)
                if 0 <= n < NC * B:
                    exps(n)

            act.wait_ge(s_lnv, 32)
            for i in range(-2, B + 3):
                attention(NC * i)
                if tiles(i + 1):
                    kv_out(i + 1)
                if tiles(i + 2):
                    xT_out(i + 2)
                if i == -2:
                    ctx_out(0)
                attention(NC * i + 1)
                attention(NC * i + 2)
                if i == -1:
                    ctx_out(1)
                if tiles(i + 1):
                    qkT_out(i + 1)
                if tiles(i - 2):
                    xbT_out(i - 2)
                attention(NC * i + 3)
                if tiles(i + 2):
                    latents_out(i + 2)
                if tiles(i - 2):
                    qw_out(i - 2)
                if tiles(i - 1):
                    ot_out(i - 1)

            def yT_out(q):
                act.wait_ge(p_ty, q + 1)
                if q >= 1:
                    act.wait_ge(g_z, q)
                for k in range(KD):
                    last = nc.scalar.activation(yT[:, k, :, :].rearrange("p b t -> p (b t)"), bank[2][:, 2 * k * T:2 * (k + 1) * T],
                                                ACT.Identity, scale=gn_s[:, k, 0:1], bias=gn_s[:, k, 1:2])
                last.then_inc(a_ty, 1)

            def xfT_out(q):
                act.wait_ge(p_tf, q + 1)
                copy(xfT[:, :, 2 * q:2 * q + 2, :], bank[4][:].rearrange("p (k b t) -> p k b t", k=KD, b=2)).then_inc(a_tf, 1)

            def shared_silu(b):
                act.wait_ge(p_sg, b + 1)
                if b >= 2:
                    act.wait_ge(v_sh, b - 1)
                n = 6 if b < 2 or b % 2 == 0 else 3
                nc.scalar.activation(sg[:, b % 2, :], bank[n][:, 0:SI], ACT.Silu).then_inc(a_sg, 1)

            def shT_out(b):
                act.wait_ge(p_sT, b + 1)
                if b >= 2:
                    act.wait_ge(p_sd, b - 1)
                copy(shT[:, b % 2, 0:2, :].rearrange("p k t -> p (k t)"), bank[1][:, 0:2 * T])
                copy(shT[0:SI - 256, b % 2, 2, :], bank[1][0:SI - 256, 2 * T:3 * T]).then_inc(a_sT, 1)

            for j in range(PAIRS + 2):
                if 0 <= j - 1 < PAIRS:
                    yT_out(j - 1)
                if j == 3:
                    shared_silu(0)
                if j == 4:
                    shT_out(0)
                    shared_silu(1)
                if j == 5:
                    shT_out(1)
                if 0 <= j - 2 < PAIRS:
                    xfT_out(j - 2)
            act.wait_ge(v_lg, 1)
            nc.scalar.activation(ex, lg, ACT.Exp).then_inc(a_re, 1)
            shared_silu(2)
            for b in range(2, B):
                if b + 1 < B:
                    shared_silu(b + 1)
                shT_out(b)

            def silu(i, par, first=False):
                act.wait_ge(p_gu, i + 1)
                if not first:
                    act.wait_ge(v_h, i - 1)
                nc.scalar.activation(bs[:, par, :], bank[2 + par][:, 0:I], ACT.Silu).then_inc(a_si, 1)

            def hT_out(i, par, first=False):
                act.wait_ge(p_hT, i + 1)
                if not first:
                    act.wait_ge(p_dn, i - 1)
                copy(bhT[:, par, :, :].rearrange("p k t -> p (k t)"), bank[1][0:IH, 0:2 * T]).then_inc(a_hT, 1)

            silu(0, 0, True)
            hT_out(0, 0, True)
            silu(1, 1, True)
            hT_out(1, 1, True)
            with act.Fori(2, BLOCKS - 1, 2) as i:
                silu(i, 0)
                hT_out(i, 0)
                silu(i + 1, 1)
                hT_out(i + 1, 1)
            silu(BLOCKS - 1, 0)
            hT_out(BLOCKS - 1, 0)
            for t in range(B):
                act.wait_ge(v_f1, 2 * t + 2)
                act.dma_start(out[t, :, :], x_s[:, t, :]).then_inc(d_out, 16)

        @block.vector
        def _(dve):
            V = nc.vector
            count = [0]

            def link(ins):
                count[0] += 1
                ins.then_inc(chain, 1)
                dve.wait_ge(chain, count[0])

            def variance(kind, b, src, eps, done):
                link(V.bn_stats(st[:, 0, :], src))
                link(V.bn_aggr(ag[:, kind, b % 2, :], st[:, 0, :]))
                V.tensor_scalar_add(ve[:, kind, b % 2, :], ag[:, kind, b % 2, 1:2], eps).then_inc(done, 1)

            def normalize(kind, b, o, src):
                return V.tensor_scalar(o, src, ag[:, kind, b % 2, 0:1], rs[:, kind, b % 2, :], ALU.subtract, ALU.mult)

            def x_variance(b):
                dve.wait_ge(s_x[xpart(b)], 16)
                variance(LX, b, x_s[:, b, :], LN_EPS, v_xv)

            def x_normalize(b):
                dve.wait_ge(g_x, b + 1)
                if b >= 2:
                    dve.wait_ge(p_t1, b - 1)
                normalize(LX, b, xh[:, b % 2, :], x_s[:, b, :]).then_inc(v_xh, 1)

            def max_subtract(n):
                s = bank[n % 2][:].rearrange("p (h k) -> p h k", h=CH)
                dve.wait_ge(p_s, n + 1)
                link(V.reduce_max(mx[:, n % 2, :], s, AX.X))
                if n >= 2:
                    dve.wait_ge(a_exp, n - 1)
                V.tensor_tensor(sc_s[:, n % 2, :, :], s, mx[:, n % 2, :].unsqueeze(2).to_broadcast([128, CH, T]),
                                ALU.subtract).then_inc(v_sb, 1)

            def rope(par, which, src, dst, done):
                t = rope_t[:, par, which, :]
                link(V.tensor_tensor(t, src, tab[:, C_ROPE:C_ROPE + 2 * ROPE], ALU.mult))
                V.tensor_tensor(dst, t[:, 0:ROPE], t[:, ROPE:2 * ROPE], ALU.add).then_inc(done, 1)

            def q_out(b):
                dve.wait_ge(p_q, b + 1)
                if b >= 2:
                    dve.wait_ge(p_t3, b - 1)
                link(V.tensor_copy(qk[:, b % 2, 0:NOPE], bank[4][:, 0:NOPE]))
                rope(b % 2, 0, bank[4][:, NOPE:NOPE + 2 * ROPE], qk[:, b % 2, NOPE:D], v_q)

            def latent_variance(b):
                dve.wait_ge(p_m1, b + 1)
                V.bn_stats(st[:, 0, :], bank[4][:, 0:QP])
                link(V.bn_stats(st[:, 1, :], bank[4][:, QP:QP + KP]))
                V.bn_aggr(ag2[:, b % 2, 0, :], st[:, 0, :])
                link(V.bn_aggr(ag2[:, b % 2, 1, :], st[:, 1, :]))
                V.tensor_scalar_add(ve2[:, b % 2, :], ag2[:, b % 2, :, 1], LN_EPS).then_inc(v_mv, 1)

            def latent_normalize(b):
                if b >= 2:
                    dve.wait_ge(p_t2, b - 1)
                    dve.wait_ge(p_t3, b - 1)
                dve.wait_ge(g_m, b + 1)
                for j, (lo, hi) in enumerate(((0, QP), (QP, QP + KP))):
                    V.tensor_scalar(lat[:, b % 2, lo:hi], bank[4][:, lo:hi], ag2[:, b % 2, j, 0:1],
                                    rs2[:, b % 2, j:j + 1], ALU.subtract, ALU.mult)
                rope(b % 2, 1, bank[4][:, QP + KP:MW], qk[:, b % 2, D + NOPE:2 * D], v_lat)

            def out_normalize(b):
                o = bank[6][:, 0:H * (DH + 1)].rearrange("p (h d) -> p h d", h=H)
                dve.wait_ge(p_pv, NC * (b + 1))
                link(V.reciprocal(rden[:, b % 2, :], o[:, :, DH]))
                if b >= 2:
                    dve.wait_ge(p_t5, b - 1)
                V.tensor_tensor(o_s[:, b % 2, :].rearrange("p (h d) -> p h d", h=H), o[:, :, 0:DH],
                                rden[:, b % 2, :].unsqueeze(2).to_broadcast([128, H, DH]), ALU.mult).then_inc(v_on, 1)

            def residual_attention(b):
                dve.wait_ge(p_wo, b + 1)
                V.tensor_tensor(x1_s[:, b, :], bank[3][:, 0:D], x_s[:, b, :], ALU.add).then_inc(v_x1, 1)
                dve.wait_ge(v_x1, b + 1)
                variance(LX1, b, x1_s[:, b, :], LN_EPS, v_x1v)

            def x1_normalize(b):
                dve.wait_ge(g_x1, b + 1)
                if b >= 2:
                    dve.wait_ge(p_bt, b - 1)
                normalize(LX1, b, xb[:, b % 2, :], x1_s[:, b, :]).then_inc(v_xb, 1)

            V.memset(onesb[:], 1.0).then_inc(c_bf, 1)
            x_variance(0)
            dve.wait_ge(s_tab, 16)
            x_normalize(0)
            tiles = lambda b: 0 <= b < B

            def chunk(n):
                if 0 <= n < NC * B:
                    max_subtract(n)

            for i in range(-2, B + 3):
                chunk(NC * i)
                if tiles(i + 1):
                    q_out(i + 1)
                chunk(NC * i + 1)
                if tiles(i - 2):
                    residual_attention(i - 2)
                    x1_normalize(i - 2)
                chunk(NC * i + 2)
                if tiles(i + 2):
                    latent_variance(i + 2)
                if 0 < i + 3 < B:
                    x_variance(i + 3)
                if tiles(i + 2):
                    latent_normalize(i + 2)
                if tiles(i - 1):
                    out_normalize(i - 1)
                chunk(NC * i + 3)
                if 0 < i + 3 < B:
                    x_normalize(i + 3)

            dve.wait_ge(p_sc, B)
            link(V.tensor_tensor(atmp, bank[7][:, 0:XH * T].rearrange("p (h t) -> p h t", h=XH),
                                 tab[:, C_DECAY:C_DECAY + XH * T].rearrange("p (h t) -> p h t", h=XH), ALU.mult))
            link(V.scalar_tensor_tensor(aT, atmp, -1.0, atmp, ALU.mult, ALU.max))
            V.tensor_scalar_max(aT, aT, 1.0).then_inc(v_at, 1)

            def variance_pair(kind, q, src, eps, done):
                V.bn_stats(st[:, 0, :], src[:, 0, :])
                link(V.bn_stats(st[:, 1, :], src[:, 1, :]))
                V.bn_aggr(agp[:, kind, q % 2, 0, :], st[:, 0, :])
                link(V.bn_aggr(agp[:, kind, q % 2, 1, :], st[:, 1, :]))
                V.tensor_scalar_add(vep[:, kind, q % 2, :], agp[:, kind, q % 2, :, 1], eps).then_inc(done, 1)

            def normalize_pair(kind, q, o, src):
                for b in range(2):
                    last = V.tensor_scalar(o[:, b, :], src[:, b, :], agp[:, kind, q % 2, b, 0:1],
                                           rsp[:, kind, q % 2, b:b + 1], ALU.subtract, ALU.mult)
                return last

            mixed = bank[0][:].rearrange("p (b d) -> p b d", b=2)

            def mix_variance(q):
                dve.wait_ge(p_o, q + 1)
                variance_pair(MIX, q, mixed, GN_EPS, v_ov)

            def mix_normalize(q):
                dve.wait_ge(g_o, q + 1)
                if q >= 1:
                    dve.wait_ge(p_ty, q)
                normalize_pair(MIX, q, yh[:], mixed).then_inc(v_yh, 1)

            def residual_cross(q):
                dve.wait_ge(p_xo, q + 1)
                V.tensor_tensor(x_s[:, 2 * q:2 * q + 2, :], bank[3][:].rearrange("p (b d) -> p b d", b=2),
                                x1_s[:, 2 * q:2 * q + 2, :], ALU.add).then_inc(v_x2, 1)
                dve.wait_ge(v_x2, q + 1)
                variance_pair(FFN, q, x_s[:, 2 * q:2 * q + 2, :], LN_EPS, v_x2v)

            def ffn_normalize(q):
                dve.wait_ge(g_x2, q + 1)
                normalize_pair(FFN, q, x1_s[:, 2 * q:2 * q + 2, :], x_s[:, 2 * q:2 * q + 2, :]).then_inc(v_xf, 1)

            def shared_mul(b):
                dve.wait_ge(a_sg, b + 1)
                if b >= 2:
                    dve.wait_ge(p_sT, b - 1)
                n = 7 if b < 2 or b % 2 == 0 else 4
                V.tensor_tensor(sh[:, b % 2, :], bank[n][:, 0:SI], sg[:, b % 2, :], ALU.mult).then_inc(v_sh, 1)

            def shared_add(b):
                dve.wait_ge(p_sd, b + 1)
                V.tensor_tensor(x_s[:, b, :], bank[1][:, 0:D], x_s[:, b, :], ALU.add).then_inc(v_sd, 1)

            for j in range(PAIRS + 2):
                if j < PAIRS:
                    mix_variance(j)
                if 0 <= j - 2 < PAIRS:
                    residual_cross(j - 2)
                if j < PAIRS:
                    mix_normalize(j)
                if 0 <= j - 2 < PAIRS:
                    ffn_normalize(j - 2)
                if j == 3:
                    shared_mul(0)
                if j == 4:
                    shared_add(0)
                    shared_mul(1)
                if j == 5:
                    shared_add(1)

            iota = tab[:, C_IOTA:C_IOTA + E].unsqueeze(1).to_broadcast([128, B, E])
            wide = lambda s: s.unsqueeze(2).to_broadcast([128, B, E])
            top_w, top_i = [s8[:, 0, :], s8[:, 1, :]], [s8[:, 2, :], s8[:, 3, :]]
            dve.wait_ge(p_lg, PAIRS)
            logits = bank[5][:, 0:B * E].rearrange("p (t e) -> p t e", e=E)
            link(V.reduce_max(s8[:, 4, :], logits, AX.X))
            V.tensor_tensor(lg, logits, wide(s8[:, 4, :]), ALU.subtract).then_inc(v_lg, 1)
            dve.wait_ge(a_re, 1)
            link(V.reduce_sum(s8[:, 5, :], ex, AX.X))
            link(V.reciprocal(s8[:, 6, :], s8[:, 5, :]))
            link(V.tensor_tensor(prob, ex, wide(s8[:, 6, :]), ALU.mult))

            def best(k):
                link(V.reduce_max(top_w[k], prob, AX.X))
                link(V.tensor_tensor(t128[:, 0], prob, wide(top_w[k]), ALU.is_lt))
                link(V.scalar_tensor_tensor(t128[:, 1], t128[:, 0], float(E), iota, ALU.mult, ALU.add))
                link(V.tensor_reduce(top_i[k], t128[:, 1], op=ALU.min, axis=AX.X))
                link(V.tensor_tensor(oh[:, k], iota, wide(top_i[k]), ALU.is_equal))

            shared_mul(2)
            best(0)
            shared_mul(3)
            link(V.scalar_tensor_tensor(prob, oh[:, 0], -2.0, prob, ALU.mult, ALU.add))
            best(1)
            V.tensor_tensor(mb[:], oh[:, 0], oh[:, 1], ALU.add).then_inc(v_top, 1)
            shared_add(2)
            shared_mul(4)
            shared_add(3)
            shared_mul(5)

            dve.wait_ge(p_rk, 1)
            dve.wait_ge(s_tabr, 16)
            c = cmp[:, :, 0:B]
            link(V.tensor_tensor(c, bank[2][:, 0:E].unsqueeze(2).to_broadcast([128, E, B]),
                                 tabr[:, R_THR:R_THR + B].unsqueeze(1).to_broadcast([128, E, B]), ALU.is_gt))
            link(V.reduce_sum(nb[:, 0, :], c, AX.X))
            link(V.tensor_tensor(cmp, nb[:, 0, :].unsqueeze(1).to_broadcast([128, E, E]),
                                 tabr[:, R_LOW:R_LOW + E * E].rearrange("p (a b) -> p a b", a=E), ALU.mult))
            link(V.reduce_sum(nb[:, 1, :], cmp, AX.X))
            link(V.tensor_scalar_mul(nb[:, 2, :], nb[:, 1, :], float(T)))
            link(V.tensor_tensor(t128[:, 0], bank[0][:, 0:B * E].rearrange("p (t e) -> p t e", e=E),
                                 nb[:, 2, :].unsqueeze(1).to_broadcast([128, B, E]), ALU.add))
            link(V.tensor_tensor(ohp, t128[:, 0:1].to_broadcast([128, 2, B, E]), oh, ALU.mult))
            link(V.reduce_sum(posf[:, 0, :], ohp.rearrange("p k t e -> p (k t) e"), AX.X))
            link(V.tensor_copy(posi[:, 0, :], posf[:, 0, :]))
            V.tensor_single_scalar(posi[:, 1, :], posi[:, 0, :], T - 1, op=ALU.bitwise_and)
            link(V.tensor_single_scalar(posi[:, 2, :], posi[:, 0, :], T.bit_length() - 1, op=ALU.logical_shift_right))
            link(V.tensor_copy(posf[:, 1:3, :], posi[:, 1:3, :]))
            shared_add(4)
            shared_mul(6)
            link(V.tensor_tensor(num, tabr[:, R_BLK:R_BLK + BLOCKS].unsqueeze(1).to_broadcast([128, 2 * B, BLOCKS]),
                                 posf[:, 2, :].unsqueeze(2).to_broadcast([128, 2 * B, BLOCKS]), ALU.is_equal))
            V.tensor_tensor(num.rearrange("p (k t) b -> p k t b", k=2), num.rearrange("p (k t) b -> p k t b", k=2),
                            tabr[:, R_TOK:R_TOK + B].unsqueeze(1).unsqueeze(3).to_broadcast([128, 2, B, BLOCKS]), ALU.mult)
            V.tensor_tensor(hot, tabr[:, R_SLOT:R_SLOT + T].unsqueeze(1).to_broadcast([128, 2 * B, T]),
                            posf[:, 1, :].unsqueeze(2).to_broadcast([128, 2 * B, T]), ALU.is_equal).then_inc(v_hot, 1)
            shared_add(5)
            shared_mul(7)
            link(V.tensor_tensor(bcmp, nb[0:1, 1, :].unsqueeze(1).to_broadcast([1, BLOCKS, E]),
                                 tabr[0:1, R_BLK:R_BLK + BLOCKS].unsqueeze(2).to_broadcast([1, BLOCKS, E]), ALU.is_le))
            link(V.reduce_sum(be[:, 0, :], bcmp, AX.X))
            V.tensor_scalar_add(bei[:], be[:, 0, :], -1.0).then_inc(v_blk, 1)
            dve.wait_ge(p_tb, 1)
            best_n, second_n = bank[5][:, 0:BLOCKS], bank[5][:, BLOCKS:2 * BLOCKS]
            link(V.tensor_copy(ids[:, 0, :], second_n))
            link(V.tensor_tensor(ids[:, 1, :], best_n, ids[:, 0, :], ALU.add))
            link(V.tensor_scalar(ids[:, 2, :], ids[:, 0, :], 0.0, float(B * T), ALU.is_gt, ALU.mult))
            V.tensor_scalar(idx[:, 0, :], ids[:, 1, :], -1.0, 0.0, ALU.add, ALU.max)
            link(V.scalar_tensor_tensor(ids[:, 3, :], ids[:, 1, :], 0.0, tabr[:, R_DUMMY:R_DUMMY + BLOCKS],
                                        ALU.is_equal, ALU.mult))
            link(V.tensor_tensor(ids[:, 3, :], ids[:, 3, :], ids[:, 2, :], ALU.add))
            V.scalar_tensor_tensor(idx[:, 1, :], ids[:, 3, :], -1.0, ids[:, 1, :], ALU.add, ALU.add).then_inc(v_idx, 1)
            shared_add(6)
            shared_add(7)

            def bT_out(i, par, first=False):
                dve.wait_ge(p_bT, i + 1)
                if not first:
                    dve.wait_ge(p_gu, i - 1)
                V.tensor_copy(bxT[:, par, :, :].rearrange("p k t -> p (k t)"), bank[0][:, 0:D]).then_inc(v_bT, 1)

            def h_mul(i, par, first=False):
                dve.wait_ge(a_si, i + 1)
                if not first:
                    dve.wait_ge(p_hT, i - 1)
                V.tensor_tensor(bh[:, par, :], bank[2 + par][:, I:2 * I], bs[:, par, :], ALU.mult).then_inc(v_h, 1)

            def y_out(i, par, slot, nth):
                dve.wait_ge(p_dn, i + 1)
                if not (isinstance(i, int) and i < RB):
                    dve.wait_ge(d_by[slot], 16 * nth)
                V.tensor_copy(by[:, slot, :], bank[4 + par][:, 0:D]).then_inc(v_y, 1)

            bT_out(0, 0, True)
            bT_out(1, 1, True)
            h_mul(0, 0, True)
            bT_out(2, 0)
            h_mul(1, 1, True)
            y_out(0, 0, 0, 0)
            for i in range(2, RB + 1):
                bT_out(i + 1, (i + 1) % 2)
                h_mul(i, i % 2)
                y_out(i - 1, (i - 1) % 2, i - 1, 0)
            FULL = (BLOCKS - 2 - RB) // RB
            with dve.Fori(0, FULL) as n:
                for j in range(RB):
                    i = n * RB + (j + RB + 1)
                    bT_out(i + 1, j % 2)
                    h_mul(i, (j + 1) % 2)
                    y_out(i - 1, j % 2, j, n + 1)
            for i in range(RB * (FULL + 1) + 1, BLOCKS + 1):
                if i + 1 < BLOCKS:
                    bT_out(i + 1, (i + 1) % 2)
                if i < BLOCKS:
                    h_mul(i, i % 2)
                y_out(i - 1, (i - 1) % 2, (i - 1) % RB, (i - 1) // RB)

            for t in range(B):
                for k in range(2):
                    if k == 0:
                        dve.wait_ge(d_g[t % 4], 16 * (t // 4 + 1))
                    else:
                        dve.wait_ge(v_f1, 2 * t + 1)
                    V.scalar_tensor_tensor(x_s[:, t, :], yg[:, t % 4, k, :], top_w[k][:, t:t + 1], x_s[:, t, :],
                                           ALU.mult, ALU.add).then_inc(v_f1, 1)


def kernel(**inputs):
    import numpy as _np
    import concourse.bacc as _bacc
    from concourse import mybir as _mybir
    from concourse.bass_utils import run_bass_kernel_spmd as _run

    g = {k: _np.asarray(v) for k, v in inputs.items()}

    def swapped(w):
        return w.reshape(w.shape[0], -1, 2, DH // 2)[:, :, ::-1, :].reshape(w.shape)

    a = "L0_attn_"
    arrays = {
        "x": g["x"],
        "ctx_in": g["ctx_2048"],
        "table": constants(),
        "table_b": bf16_constants(),
        "table_r": routing_constants(),
        "w_m": _np.concatenate([g[a + "W_dq"], g[a + "W_dkv"], g[a + "W_kr"], swapped(g[a + "W_kr"])], 1),
        "w_q": _np.concatenate([g[a + "W_uq"], g[a + "W_qr"], swapped(g[a + "W_qr"])], 1),
        "w_kv": g[a + "W_ukv"],
        "w_out": g[a + "W_o"].T,
        "ln_q": _np.stack([g[a + "q_ln_w"], g[a + "q_ln_b"]], 1),
        "ln_kv": _np.stack([g[a + "kv_ln_w"], g[a + "kv_ln_b"]], 1),
        "wh": g["L0_xattn_Wh"],
        "wg": g["L0_xattn_wg_w"],
        "wo": g["L0_xattn_wo_w"],
        "gn": _np.stack([g["L0_xattn_gn_gamma"], g["L0_xattn_gn_beta"]], 1),
        "gate": g["L0_ffn_gate_w"].T,
        "w_gu": g["L0_ffn_w_gate_up"],
        "w_dn": g["L0_ffn_w_down"],
        "s_gu_d": g["L0_ffn_shared_gate_up"],
        "s_dn_d": g["L0_ffn_shared_down"],
    }
    nc = _bacc.Bacc("TRN2", target_bir_lowering=False, num_devices=1)
    feed, args = {}, []
    for name, v in arrays.items():
        v = _np.ascontiguousarray(v)
        feed[f"in_{name}"] = v
        args.append(nc.dram_tensor(f"in_{name}", v.shape, _mybir.dt.from_np(v.dtype), kind="ExternalInput").ap())
    args.append(nc.dram_tensor("out_0", (B, T, D), _mybir.dt.float32, kind="ExternalOutput").ap())
    decoder_layer(nc, *args)
    r = _run(nc, [feed], core_ids=[0])
    return r.results[0]["out_0"]
```

```python
import numpy as np
import concourse.bass as bass
from concourse import mybir
from contextlib import ExitStack

T = 128
B = 8
D = 256
KD = D // 128
H, DH = 16, 16
HN = 14
NOPE = HN * DH
ROPE = (H - HN) * DH
QP = D // 2
KP = 2 * D // 3
KPH = KP // 2
MW = QP + KP + 2 * ROPE
QW = D + ROPE
CH = 4
NC = H // CH
HD = 128
XH = D // HD
E = 16
I = 176
IH = I // 2
SI = 2 * I
SLOTS = 2 * B * T
BLOCKS = (SLOTS + E * (T - 1)) // T
LN_EPS, GN_EPS = 1e-5, 1e-3
MASKED = -1e30

DUMMY = SLOTS
RB = 4
PAIRS = B // 2
EARLY = 6

C_ID, C_ROPE, C_HEAD, C_DECAY = 0, 128, 128 + 4 * DH, 128 + 4 * DH + 8
C_IOTA = C_DECAY + XH * T
C_N = C_IOTA + E
R_THR, R_LOW, R_BLK, R_SLOT, R_TOK, R_DUMMY = (int(v) for v in np.cumsum([0, B, E * E, BLOCKS, T, 2 * B]))
R_N = R_DUMMY + BLOCKS


def constants():
    c = np.zeros((128, C_N), np.float32)
    p = np.arange(128)
    c[:, C_ID:C_ID + 128] = np.eye(128)
    freqs = (1.0 / 10000.0 ** (np.arange(0, DH, 2, dtype=np.float32) / DH)).astype(np.float32)
    ang = p.astype(np.float32)[:, None] * freqs[None, :]
    cos, sin = np.cos(ang), np.sin(ang)
    c[:, C_ROPE:C_ROPE + 4 * DH] = np.concatenate([cos, cos, cos, cos, -sin, sin, -sin, sin], 1)
    c[:, C_HEAD:C_HEAD + 8] = p[:, None] // DH == np.arange(8)[None, :]
    for h in range(XH):
        expo = (p[None, :] - p[:, None]).astype(np.float64)
        decay = np.where(expo <= 0, (1.0 - 2.0 ** (-5.0 - h)) ** expo, 0.0)
        decay = decay / np.sqrt(decay.sum(-1))[None, :] / np.sqrt(float(HD))
        c[:, C_DECAY + h * T:C_DECAY + (h + 1) * T] = decay.T
    c[:, C_IOTA:C_IOTA + E] = np.arange(E)
    return c


def routing_constants():
    c = np.zeros((128, R_N), np.float32)
    p = np.arange(128)[:, None]
    c[:, R_THR:R_THR + B] = 128.0 * np.arange(B)
    c[:, R_LOW:R_LOW + E * E] = (np.arange(E)[None, :] < np.arange(E)[:, None]).reshape(1, -1)
    c[:, R_BLK:R_BLK + BLOCKS] = np.arange(BLOCKS)
    c[:, R_SLOT:R_SLOT + T] = np.arange(T)
    c[:, R_TOK:R_TOK + B] = T * np.arange(B)
    c[:, R_TOK + B:R_TOK + 2 * B] = p + 1
    c[:, R_DUMMY:R_DUMMY + BLOCKS] = DUMMY + T * np.arange(BLOCKS) + p + 1
    return c


def bf16_constants():
    p = np.arange(128)
    c = np.concatenate([np.where(p[None, :] <= p[:, None], 0.0, MASKED), p[:, None] < p[None, :]], 1)
    return c.astype(mybir.dt.np(mybir.dt.bfloat16))


def decoder_layer(nc, x, ctx_in, table, table_b, table_r, w_m, w_q, w_kv, w_out, ln_q, ln_kv, wh, wg, wo, gn,
                  gate, w_gu, w_dn, s_gu_d, s_dn_d, out):
    f32, bf16, i32 = mybir.dt.float32, mybir.dt.bfloat16, mybir.dt.int32
    ALU, ACT, AX = mybir.AluOpType, mybir.ActivationFunctionType, mybir.AxisListType

    ctx = ExitStack()
    with ctx:
        def sb(name, shape, dt=f32):
            return ctx.enter_context(nc.sbuf_tensor(name, shape, dt))

        def sem(name):
            return ctx.enter_context(nc.semaphore(name))

        ffn_in = nc.dram_tensor("ffn_in", [B * T, D], f32).ap()
        expert_out = nc.dram_tensor("expert_out", [DUMMY + BLOCKS * T, D], f32).ap()

        tab = sb("tab", [128, C_N])
        wm_s = sb("wm_s", [128, KD, MW])
        idf = tab[:, C_ID:C_ID + 128]
        tabr = wm_s[:].rearrange("p k n -> p (k n)")[:, 0:R_N]
        tabb = sb("tabb", [128, 2 * 128], bf16)
        maskb, trib = (tabb[:, i * 128:(i + 1) * 128] for i in range(2))
        onesb = sb("onesb", [128, 128], bf16)
        halfpow = sb("halfpow", [128, 2])
        wq_s = sb("wq_s", [128, QW])
        wkv_s = sb("wkv_s", [KPH, 2, NOPE + D])
        wout_s = sb("wout_s", [128, KD, D])
        lnq_s = sb("lnq_s", [128, 2])
        lnkv_s = sb("lnkv_s", [KPH, 2, 2])
        wh_s = sb("wh_s", [128, XH, HD])
        wg_s = sb("wg_s", [128, KD, D])
        wo_s = sb("wo_s", [128, KD, D])
        gn_s = sb("gn_s", [128, KD, 2])
        gate_s = sb("gate_s", [128, KD, E])
        gu_s = sb("gu_s", [128, KD, E, 2 * I])
        dn_s = sb("dn_s", [IH, 2, E, D])
        sgu_s = sb("sgu_s", [128, KD, 2 * SI])
        x_s = sb("x_s", [128, B, D])
        x1_s = sb("x1_s", [128, B, D])
        qx_s = sb("qx_s", [128, B, 4, T])
        ck_s = sb("ck_s", [128, XH, B, T])
        cv_s = sb("cv_s", [128, B, XH, HD])
        kbd = sb("kbd", [128, 2, 2, 8, T])
        xh = sb("xh", [128, 2, D])
        xT = sb("xT", [128, 2, KD, T])
        lat = sb("lat", [128, 2, QP + KP])
        cqT = sb("cqT", [128, 2, T])
        ckvT = sb("ckvT", [KPH, 2, 2, T])
        qk = sb("qk", [128, 2, 2 * D])
        rope_t = sb("rope_t", [128, 2, 2, 2 * ROPE])
        v_s = sb("v_s", [128, 3, H, DH + 1])
        qkT = sb("qkT", [128, 2, 4, T])
        mx = sb("mx", [128, 2, CH])
        sc_s = sb("sc_s", [128, 2, CH, T])
        pr_s = sb("pr_s", [128, 2, CH, T])
        prT = sb("prT", [128, 2, CH, T])
        rden = sb("rden", [128, 2, H])
        o_s = sb("o_s", [128, 2, D])
        oT = sb("oT", [128, 2, KD, T])
        xb = sb("xb", [128, 2, D])
        bxT = sb("bxT", [128, 2, KD, T])
        cs = qx_s[:].rearrange("p b k t -> p (b k t)")[:, 0:B * D].rearrange("p (b d) -> p b d", b=B)
        cT = pr_s[:].rearrange("p r h t -> p (r h t)").rearrange("p (h j t) -> p h j t", h=XH, j=4)
        st = sb("st", [128, 2, 6])
        ag = sb("ag", [128, 2, 2, 2])
        ve = sb("ve", [128, 2, 2, 1])
        rs = sb("rs", [128, 2, 2, 1])
        agp = sb("agp", [128, 2, 2, 2, 2])
        vep = sb("vep", [128, 2, 2, 2])
        rsp = sb("rsp", [128, 2, 2, 2])
        ag2 = sb("ag2", [128, 2, 2, 2])
        ve2 = sb("ve2", [128, 2, 2])
        rs2 = sb("rs2", [128, 2, 2])
        LX, LX1 = range(2)
        MIX, FFN = range(2)

        bank = [ctx.enter_context(nc.psum_tensor(f"bank{i}", [128, 512], f32)) for i in range(8)]

        NX = 3
        XPARTS = [(0, 1), (1, 3), (3, 8)]
        ld_x = [sem(f"ld_x{i}") for i in range(NX)]
        (ld_table, ld_table_b, ld_w_m, ld_w_q, ld_w_kv, ld_ln, ld_w_out, ld_ctx0, ld_ctx1, ld_wh,
         ld_wg_wo, ld_gate, ld_shared, ld_gate_up, ld_down) = [sem(n) for n in (
            "ld_table ld_table_b ld_w_m ld_w_q ld_w_kv ld_ln ld_w_out ld_ctx0 ld_ctx1 ld_wh ld_wg_wo ld_gate "
            "ld_shared ld_gate_up ld_down").split()]
        ld_table_r, ld_identity = sem("ld_table_r"), sem("ld_identity")
        dve_block_hot, pool_block_numbers = sem("dve_block_hot"), sem("pool_block_numbers")
        set_ones, set_pool = sem("set_ones"), sem("set_pool")
        (pe_x_T, pe_latents, pe_latents_T, pe_keys_values, pe_queries, pe_qk_T, pe_scores, pe_probs_T,
         pe_weighed, pe_attn_T, pe_attn_out, pe_x1_T, pe_cross_queries, pe_cross_scores) = [sem(n) for n in (
            "pe_x_T pe_latents pe_latents_T pe_keys_values pe_queries pe_qk_T pe_scores pe_probs_T pe_weighed "
            "pe_attn_T pe_attn_out pe_x1_T pe_cross_queries pe_cross_scores").split()]
        pe_gates, act_gates = sem("pe_gates"), sem("act_gates")
        pe_ctx_T, pe_ctx_keys, pe_ctx_values = sem("pe_ctx_T"), sem("pe_ctx_keys"), sem("pe_ctx_values")
        chain = sem("chain")
        (dve_x_var, dve_x_normed, dve_queries, dve_masked, dve_row_max, dve_x1, dve_x1_var,
         dve_x1_normed, dve_latents_var, dve_latents_normed, dve_attn_normed) = [sem(n) for n in (
            "dve_x_var dve_x_normed dve_queries dve_masked dve_row_max dve_x1 dve_x1_var dve_x1_normed "
            "dve_latents_var dve_latents_normed dve_attn_normed").split()]
        (act_exp, act_keys_values, act_attn_T, act_x_T, act_qk_T, act_probs_T, act_x1_T,
         act_cross_queries, act_latents, act_ctx_T, act_ctx_keys, act_ctx_values) = [sem(n) for n in (
            "act_exp act_keys_values act_attn_T act_x_T act_qk_T act_probs_T act_x1_T act_cross_queries "
            "act_latents act_ctx_T act_ctx_keys act_ctx_values").split()]
        (pool_x_rstd, pool_latents_rstd, pool_x1_rstd, pool_keys_spread) = [sem(n) for n in (
            "pool_x_rstd pool_latents_rstd pool_x1_rstd pool_keys_spread").split()]
        (dve_decayed, pe_mix, dve_mix_var, pool_mix_rstd, dve_mix_normed, pe_mix_T, act_mix_T,
         pool_gated, pe_cross_out, dve_x2_var, pool_x2_rstd, dve_ffn_in, pe_ffn_in_T, act_ffn_in_T,
         pe_logits) = [sem(n) for n in (
            "dve_decayed pe_mix dve_mix_var pool_mix_rstd dve_mix_normed pe_mix_T act_mix_T pool_gated "
            "pe_cross_out dve_x2_var pool_x2_rstd dve_ffn_in pe_ffn_in_T act_ffn_in_T pe_logits").split()]
        act_x2, pe_shared_up = sem("act_x2"), sem("pe_shared_up")
        (dve_logits, act_router_exp, dve_top2, pe_counts, dve_block_experts) = [sem(n) for n in (
            "dve_logits act_router_exp dve_top2 pe_counts dve_block_experts").split()]
        dve_slot_hot, pe_slot_table, dve_rows, dma_ffn_in = [sem(n) for n in "dve_slot_hot pe_slot_table dve_rows dma_ffn_in".split()]
        (pe_shared_gate, act_shared_silu, dve_shared_hidden, pe_shared_T, act_shared_T, pe_shared_down,
         dve_shared_added) = [sem(n) for n in (
            "pe_shared_gate act_shared_silu dve_shared_hidden pe_shared_T act_shared_T pe_shared_down "
            "dve_shared_added").split()]
        dma_gathered = [sem(f"dma_gathered{i}") for i in range(RB)]
        dma_scattered = [sem(f"dma_scattered{i}") for i in range(RB)]
        (pe_block_T, dve_block_T, pe_expert_up, act_expert_silu, dve_hidden, pe_hidden_T, act_hidden_T,
         pe_expert_down, dve_expert_out) = [sem(n) for n in (
            "pe_block_T dve_block_T pe_expert_up act_expert_silu dve_hidden pe_hidden_T act_hidden_T "
            "pe_expert_down dve_expert_out").split()]
        dma_token_outputs = [sem(f"dma_token_outputs{i}") for i in range(B)]
        dve_first_sum, dve_second_sum, dma_out = sem("dve_first_sum"), sem("dve_second_sum"), sem("dma_out")

        def carve(t, cols):
            flat, at = t
            t[1] = at + cols
            return flat[:, at:at + cols]

        scr = [sc_s[:].rearrange("p r h t -> p (r h t)"), 0]
        prr = [pr_s[:].rearrange("p r h t -> p (r h t)"), 0]
        ptr = [prT[:].rearrange("p r h t -> p (r h t)"), 0]
        qtr = [qkT[:].rearrange("p r h t -> p (r h t)"), 0]
        qkr = [qk[:].rearrange("p r t -> p (r t)"), 0]
        aT = carve(scr, XH * T).rearrange("p (h t) -> p h t", h=XH)
        atmp = carve(scr, XH * T).rearrange("p (h t) -> p h t", h=XH)
        yh = [xh, xb]
        yT = [xT, bxT]
        zT = [oT, prr[0][:, 0:KD * 2 * T].rearrange("p (k b t) -> p k b t", k=KD, b=2)]
        mix_bank = [0, 6, 7, 1]
        gate_bank = [4, 4, 2, 5]
        cross_bank = [3, 0]
        xfT = ck_s
        lg = carve(qtr, B * E).rearrange("p (t e) -> p t e", t=B)
        ex = carve(qtr, B * E).rearrange("p (t e) -> p t e", t=B)
        prob = carve(qtr, B * E).rearrange("p (t e) -> p t e", t=B)
        s8 = sb("s8", [128, 8, B])
        oh = carve(qtr, 2 * B * E).rearrange("p (k t e) -> p k t e", k=2, t=B)
        t128 = carve(qtr, 2 * B * E).rearrange("p (k t e) -> p k t e", k=2, t=B)
        ohp = carve(qkr, 2 * B * E).rearrange("p (k t e) -> p k t e", k=2, t=B)
        mb = sb("mb", [128, B, E], bf16)
        cmp = carve(qkr, E * E).rearrange("p (a b) -> p a b", a=E)
        nb = sb("nb", [128, 3, E])
        posi = sb("posi", [128, 3, 2 * B], i32)
        posf = sb("posf", [128, 3, 2 * B])
        bcmp = carve(qkr, BLOCKS * E)[0:1, :].rearrange("p (a b) -> p a b", a=BLOCKS)
        be = sb("be", [1, 2, BLOCKS])
        bei = sb("bei", [1, BLOCKS], i32)
        shared_bank = [(6, 7), (3, 1)]
        spare = [kbd[:].rearrange("p a g h t -> p (a g h t)"), 0]
        sg = carve(spare, 2 * SI).rearrange("p (r n) -> p r n", r=2)
        sh = carve(spare, 2 * SI).rearrange("p (r n) -> p r n", r=2)
        shT = carve(spare, 6 * T).rearrange("p (r k t) -> p r k t", r=2, k=3)
        sdn_s = carve(spare, 3 * D).rearrange("p (k n) -> p k n", k=3)
        by = carve(spare, RB * D).rearrange("p (r n) -> p r n", r=RB)
        qxr = [qx_s[:].rearrange("p b k t -> p (b k t)"), 0]
        hot = carve(qxr, B * T).bitcast(bf16).rearrange("p (n t) -> p n t", n=2 * B)
        num = carve(qxr, 2 * B * BLOCKS).rearrange("p (n b) -> p n b", n=2 * B)
        num_b = carve(qxr, 2 * B * BLOCKS).bitcast(bf16).rearrange("p (f n b) -> p f n b", f=2, n=2 * B)
        bx = carve(qxr, RB * D).rearrange("p (r n) -> p r n", r=RB)
        yg = [half.rearrange("p (r k d) -> p r k d", r=B // 2, k=2) for half in
              (cv_s[:].rearrange("p b h e -> p (b h e)"), gu_s[:].rearrange("p k e n -> p (k e n)")[:, 0:B * D])]
        yg = [yg[t // (B // 2)][:, t % (B // 2)] for t in range(B)]
        bs = carve(prr, 2 * I).rearrange("p (r n) -> p r n", r=2)
        bh = carve(prr, 2 * I).rearrange("p (r n) -> p r n", r=2)
        bhT = carve(ptr, 4 * T)[0:IH, :].rearrange("p (r k t) -> p r k t", r=2, k=2)
        idx = ptr[0][:, ptr[1]:].bitcast(i32)[:, 0:2 * BLOCKS].rearrange("p (k b) -> p k b", k=2)
        ids = ptr[0][:, ptr[1] + 64:ptr[1] + 64 + 4 * BLOCKS].rearrange("p (k b) -> p k b", k=4)

        def xpart(b):
            return [i for i, (lo, hi) in enumerate(XPARTS) if lo <= b < hi][0]

        block = ctx.enter_context(nc.Block())

        @block.sync
        def _(sp):
            xv = x.rearrange("b p d -> p b d")
            cv = ctx_in.rearrange("b p d -> p b d")
            sp.dma_start(x_s[:, 0:1, :], xv[:, 0:1, :]).then_inc(ld_x[0], 16)
            sp.dma_start(tab[:, C_ID:C_ID + 128], table[:, C_ID:C_ID + 128]).then_inc(ld_identity, 16)
            sp.dma_start(wm_s[:], w_m.rearrange("(k p) n -> p k n", p=128)).then_inc(ld_w_m, 16)
            sp.dma_start(cs[:, 0:4, :], cv[:, 0:4, :]).then_inc(ld_ctx0, 16)
            sp.dma_start(wh_s[:], wh.rearrange("h p n -> p h n")).then_inc(ld_wh, 16)
            sp.dma_start(tab[:, C_ROPE:], table[:, C_ROPE:]).then_inc(ld_table, 16)
            sp.dma_start(x_s[:, 1:3, :], xv[:, 1:3, :]).then_inc(ld_x[1], 16)
            sp.dma_start(wq_s[:], w_q).then_inc(ld_w_q, 16)
            sp.dma_start(tabb[:], table_b).then_inc(ld_table_b, 16)
            sp.dma_start(wkv_s[:], w_kv.rearrange("(k p) n -> p k n", p=KPH)).then_inc(ld_w_kv, 16)
            sp.dma_start(lnq_s[:], ln_q).then_inc(ld_ln, 16)
            sp.dma_start(lnkv_s[:], ln_kv.rearrange("(k p) n -> p k n", p=KPH)).then_inc(ld_ln, 16)
            sp.dma_start(x_s[:, 3:8, :], xv[:, 3:8, :]).then_inc(ld_x[2], 16)
            sp.dma_start(cs[:, 4:8, :], cv[:, 4:8, :]).then_inc(ld_ctx1, 16)
            sp.dma_start(wout_s[:], w_out.rearrange("(k p) n -> p k n", p=128)).then_inc(ld_w_out, 16)
            sp.dma_start(wg_s[:], wg.rearrange("(k p) n -> p k n", p=128)).then_inc(ld_wg_wo, 16)
            sp.dma_start(wo_s[:], wo.rearrange("(k p) n -> p k n", p=128)).then_inc(ld_wg_wo, 16)
            sp.dma_start(gn_s[:], gn.rearrange("(k p) n -> p k n", p=128)).then_inc(ld_wg_wo, 16)
            sp.dma_start(gate_s[:], gate.rearrange("(k p) n -> p k n", p=128)).then_inc(ld_gate, 16)
            sp.dma_start(sgu_s[:], s_gu_d.rearrange("(k p) n -> p k n", p=128)).then_inc(ld_shared, 16)
            for k in range(KD):
                for e in range(0, E, 4):
                    sp.dma_start(gu_s[:, k, e:e + 4, :],
                                 w_gu[e:e + 4, k * 128:(k + 1) * 128, :].rearrange("e p n -> p e n")).then_inc(ld_gate_up, 16)
            for k in range(2):
                for e in range(0, E, 8):
                    sp.dma_start(dn_s[:, k, e:e + 8, :],
                                 w_dn[e:e + 8, k * IH:(k + 1) * IH, :].rearrange("e p n -> p e n")).then_inc(ld_down, 16)
            sp.wait_ge(pe_latents, B)
            sp.dma_start(tabr, table_r).then_inc(ld_table_r, 16)
            sp.wait_ge(pe_scores, NC * B)
            sp.dma_start(sdn_s[:, 0:2, :], s_dn_d[0:256, :].rearrange("(k p) n -> p k n", p=128)).then_inc(ld_shared, 16)
            sp.dma_start(sdn_s[0:SI - 256, 2, :], s_dn_d[256:SI, :]).then_inc(ld_shared, 16)
            for q in range(PAIRS):
                sp.wait_ge(dve_ffn_in, q + 1)
                sp.dma_start(ffn_in[2 * q * T:2 * (q + 1) * T, :].rearrange("(b p) d -> p b d", b=2),
                             x1_s[:, 2 * q:2 * q + 2, :]).then_inc(dma_ffn_in, 16)
            for r in range(RB):
                sp.wait_ge(dma_scattered[r], 16 * len(range(r, BLOCKS, RB)))
            for t in range(B):
                sp.dma_start(yg[t],
                             expert_out[0:SLOTS, :].rearrange("(k b p) d -> b p k d", k=2, b=B)[t]).then_inc(dma_token_outputs[t], 16)
            sp.wait_ge(dma_out, 16 * B)

        @block.gpsimd
        def _(pool):
            nc.gpsimd.memset(halfpow[:], -0.5).then_inc(set_pool, 1)
            nc.gpsimd.memset(v_s[:, :, :, DH:DH + 1], 1.0).then_inc(set_pool, 1)
            pool.wait_ge(set_pool, 2)

            def rsqrt(kind, b, ready, done):
                pool.wait_ge(ready, b + 1)
                nc.gpsimd.tensor_tensor(rs[:, kind, b % 2, :], ve[:, kind, b % 2, :], halfpow[:, 0:1],
                                        ALU.pow).then_inc(done, 1)

            def rsqrt_latent(b):
                pool.wait_ge(dve_latents_var, b + 1)
                nc.gpsimd.tensor_tensor(rs2[:, b % 2, :], ve2[:, b % 2, :], halfpow[:], ALU.pow).then_inc(pool_latents_rstd, 1)

            def expand(b, g):
                pool.wait_ge(act_qk_T, b + 1)
                if b >= 2:
                    pool.wait_ge(pe_scores, NC * (b - 2) + 2 * (g + 1))
                nc.gpsimd.tensor_tensor(
                    kbd[:, b % 2, g, :, :],
                    qkT[:, b % 2, 2 + g, :].unsqueeze(1).to_broadcast([128, 8, T]),
                    tab[:, C_HEAD:C_HEAD + 8].unsqueeze(2).to_broadcast([128, 8, T]), ALU.mult).then_inc(pool_keys_spread, 1)

            rsqrt(LX, 0, dve_x_var, pool_x_rstd)
            pool.wait_ge(ld_table, 16)
            tiles = lambda b: 0 <= b < B
            for i in range(-2, B + 2):
                if tiles(i - 2):
                    rsqrt(LX1, i - 2, dve_x1_var, pool_x1_rstd)
                if tiles(i + 2):
                    rsqrt_latent(i + 2)
                if tiles(i + 1):
                    expand(i + 1, 0)
                if 0 < i + 3 < B:
                    rsqrt(LX, i + 3, dve_x_var, pool_x_rstd)
                if tiles(i + 1):
                    expand(i + 1, 1)
            def rsqrt_pair(kind, q, ready, done):
                pool.wait_ge(ready, q + 1)
                nc.gpsimd.tensor_tensor(rsp[:, kind, q % 2, :], vep[:, kind, q % 2, :], halfpow[:], ALU.pow).then_inc(done, 1)

            def gate_mix(q):
                pool.wait_ge(act_gates, q + 1)
                pool.wait_ge(act_mix_T, q + 1)
                if q >= 2:
                    pool.wait_ge(pe_cross_out, q - 1)
                nc.gpsimd.tensor_tensor(zT[q % 2][:], qx_s[:, 2 * q:2 * q + 2, 0:KD, :].rearrange("p b k t -> p k b t"),
                                        yT[q % 2][:], ALU.mult).then_inc(pool_gated, 1)

            rsqrt_pair(MIX, 0, dve_mix_var, pool_mix_rstd)
            rsqrt_pair(MIX, 1, dve_mix_var, pool_mix_rstd)
            gate_mix(0)
            rsqrt_pair(MIX, 2, dve_mix_var, pool_mix_rstd)
            rsqrt_pair(MIX, 3, dve_mix_var, pool_mix_rstd)
            gate_mix(1)
            gate_mix(2)
            rsqrt_pair(FFN, 0, dve_x2_var, pool_x2_rstd)
            gate_mix(3)
            rsqrt_pair(FFN, 1, dve_x2_var, pool_x2_rstd)
            rsqrt_pair(FFN, 2, dve_x2_var, pool_x2_rstd)
            rsqrt_pair(FFN, 3, dve_x2_var, pool_x2_rstd)

            pool.wait_ge(dve_block_hot, 1)
            for f in range(2):
                last = nc.gpsimd.tensor_tensor(
                    num_b[:, f].rearrange("p (k t) b -> p k t b", k=2), num.rearrange("p (k t) b -> p k t b", k=2),
                    tabr[:, R_TOK + f * B:R_TOK + (f + 1) * B].unsqueeze(1).unsqueeze(3).to_broadcast([128, 2, B, BLOCKS]),
                    ALU.mult)
            last.then_inc(pool_block_numbers, 1)

            LAG = RB + 3
            pool.wait_ge(dma_ffn_in, 16 * PAIRS)
            pool.wait_ge(dve_rows, 1)
            for i in range(BLOCKS + LAG):
                if i < BLOCKS:
                    if i >= RB:
                        pool.wait_ge(pe_block_T, i - RB + 1)
                    pool.indirect_dma_start(bx[:, i % RB, :], None, ffn_in[:],
                                            bass.IndirectOffsetOnAxis(ap=idx[:, 0, i:i + 1], axis=0)).then_inc(dma_gathered[i % RB], 16)
                k = i - LAG
                if k >= 0:
                    pool.wait_ge(dve_expert_out, k + 1)
                    pool.indirect_dma_start(expert_out[:], bass.IndirectOffsetOnAxis(ap=idx[:, 1, k:k + 1], axis=0),
                                            by[:, k % RB, :], None).then_inc(dma_scattered[k % RB], 16)

        @block.tensor
        def _(pe):
            mm, tr = nc.tensor.matmul, nc.tensor.transpose

            def front_transpose(b):
                pe.wait_ge(dve_x_normed, b + 1)
                if b >= 5:
                    pe.wait_ge(act_cross_queries, b - 4)
                for k in range(KD):
                    last = tr(bank[5][:, k * T:(k + 1) * T], xh[:, b % 2, k * 128:(k + 1) * 128], idf)
                last.then_inc(pe_x_T, 1)

            def front_project(b):
                pe.wait_ge(act_x_T, b + 1)
                if b >= 1:
                    pe.wait_ge(dve_queries, b)
                for k in range(KD):
                    last = mm(bank[4][:, 0:MW], xT[:, b % 2, k, :], wm_s[:, k, :], start=k == 0, stop=k == KD - 1)
                last.then_inc(pe_latents, 1)

            def latent_transpose(b):
                pe.wait_ge(dve_latents_normed, b + 1)
                tr(bank[4][:, 0:T], lat[:, b % 2, 0:QP], idf)
                for k in range(2):
                    last = tr(bank[4][0:KPH, (k + 1) * T:(k + 2) * T],
                              lat[:, b % 2, QP + k * KPH:QP + (k + 1) * KPH], idf)
                last.then_inc(pe_latents_T, 1)

            def keys_values(b):
                pe.wait_ge(act_latents, b + 1)
                if b >= 3:
                    pe.wait_ge(act_attn_T, b - 2)
                for k in range(2):
                    last = mm(bank[3][:, 0:NOPE + D], ckvT[:, b % 2, k, :], wkv_s[:, k, :], start=k == 0, stop=k == 1)
                last.then_inc(pe_keys_values, 1)
                mm(bank[4][:, 0:QW], cqT[:, b % 2, :], wq_s[:], start=True, stop=True).then_inc(pe_queries, 1)

            def qk_transpose(b):
                pe.wait_ge(dve_queries, b + 1)
                pe.wait_ge(act_keys_values, b + 1)
                pe.wait_ge(act_x_T, min(b + 2, B))
                for k in range(4):
                    last = tr(bank[5][:, k * T:(k + 1) * T], qk[:, b % 2, k * 128:(k + 1) * 128], idf)
                last.then_inc(pe_qk_T, 1)

            def scores(n):
                b, c = n // NC, n % NC
                g = c // 2
                if c == 0:
                    pe.wait_ge(act_qk_T, b + 1)
                if c % 2 == 0:
                    pe.wait_ge(pool_keys_spread, 2 * b + g + 1)
                if n >= 2:
                    pe.wait_ge(dve_masked, n - 1)
                h0 = (c % 2) * CH
                o = bank[n % 2][:].rearrange("p (h k) -> p h k", h=CH)
                mm(o, qkT[:, b % 2, g, :], kbd[:, b % 2, g, h0:h0 + CH, :], start=True, stop=True).then_inc(pe_scores, 1)

            def prob_transpose(n):
                pe.wait_ge(act_exp, n + 1)
                if n >= 1:
                    pe.wait_ge(act_probs_T, n)
                for h in range(CH):
                    last = tr(bank[2][:, h * T:(h + 1) * T], pr_s[:, n % 2, h, :], idf)
                last.then_inc(pe_probs_T, 1)

            def weigh_values(n):
                b, c = n // NC, n % NC
                pe.wait_ge(act_probs_T, n + 1)
                if c == 0 and b >= 1:
                    pe.wait_ge(dve_attn_normed, b)
                for h in range(CH):
                    hh = c * CH + h
                    last = mm(bank[6][:, hh * (DH + 1):(hh + 1) * (DH + 1)], prT[:, n % 2, h, :],
                              v_s[:, b % 3, hh, :], start=True, stop=True)
                last.then_inc(pe_weighed, 1)

            def out_bank(b):
                return bank[3] if b < B - 1 else bank[0]

            def out_transpose(b):
                pe.wait_ge(dve_attn_normed, b + 1)
                if 1 <= b < B - 1:
                    pe.wait_ge(act_x1_T, b)
                if b == B - 1:
                    pe.wait_ge(dve_masked, NC * B)
                for k in range(KD):
                    last = tr(out_bank(b)[:, k * T:(k + 1) * T], o_s[:, b % 2, k * 128:(k + 1) * 128], idf)
                last.then_inc(pe_attn_T, 1)

            def out_project(b):
                pe.wait_ge(act_attn_T, b + 1)
                pe.wait_ge(act_keys_values, min(b + 4, B))
                for k in range(KD):
                    last = mm(out_bank(b)[:, 0:D], oT[:, b % 2, k, :], wout_s[:, k, :], start=k == 0, stop=k == KD - 1)
                last.then_inc(pe_attn_out, 1)

            def cross_transpose(b):
                pe.wait_ge(dve_x1_normed, b + 1)
                for k in range(KD):
                    last = tr(out_bank(b)[:, k * T:(k + 1) * T], xb[:, b % 2, k * 128:(k + 1) * 128], idf)
                last.then_inc(pe_x1_T, 1)

            def cross_queries(b):
                pe.wait_ge(act_x1_T, b + 1)
                pe.wait_ge(act_qk_T, min(b + 4, B))
                if b == B - 1:
                    pe.wait_ge(dve_masked, NC * B)
                for h in range(XH):
                    last = mm(bank[5 if b < B - 1 else 1][:, h * T:(h + 1) * T], wh_s[:, h, :], qx_s[:, b, XH + h, :],
                              start=True, stop=True)
                last.then_inc(pe_cross_queries, 1)

            def cross_scores(b):
                pe.wait_ge(act_cross_queries, b + 1)
                for h in range(XH):
                    last = mm(bank[7][:, h * T:(h + 1) * T], ck_s[:, h, b, :], qx_s[:, b, h, :],
                              start=b == 0 and h == 0, stop=b == B - 1, skip_group_check=True)
                last.then_inc(pe_cross_scores, 1)

            def ctx_part(g, step):
                if step == 0:
                    pe.wait_ge((ld_ctx0, ld_ctx1)[g], 16)
                    for h in range(XH):
                        for j in range(4):
                            last = tr(bank[6 + h][:, j * T:(j + 1) * T], cs[:, 4 * g + j, h * HD:(h + 1) * HD], idf)
                        last.then_inc(pe_ctx_T, 1)
                if step == 1:
                    pe.wait_ge(ld_wh, 16)
                    for h in range(XH):
                        pe.wait_ge(act_ctx_T, XH * g + h + 1)
                        if g:
                            pe.wait_ge(act_ctx_values, 2)
                        mm(bank[h][:], wh_s[:, h, :], cT[:, h, :, :], start=True, stop=True).then_inc(pe_ctx_keys, 1)
                if step == 2:
                    pe.wait_ge(act_ctx_keys, XH * (g + 1))
                    for j in range(4):
                        for h in range(XH):
                            last = mm(bank[1 + j // 2][:, (j % 2) * D + h * HD:(j % 2) * D + (h + 1) * HD],
                                      cT[:, h, j, :], wh_s[:, h, :], start=True, stop=True)
                        if j % 2:
                            last.then_inc(pe_ctx_values, 1)

            def gates(q, m):
                if q < 2 and m == 0:
                    pe.wait_ge(act_gates, 1) if q else pe.wait_ge(dve_queries, B)
                if q == 3 and m == 0:
                    pe.wait_ge(act_cross_queries, B - 1)
                for k in range(KD):
                    last = mm(bank[gate_bank[q]][:, 2 * m * T:2 * (m + 1) * T], wg_s[:, k, m * 128:(m + 1) * 128],
                              qx_s[:, 2 * q:2 * q + 2, XH + k, :], start=k == 0, stop=k == KD - 1)
                if m == KD - 1:
                    last.then_inc(pe_gates, 1)

            def cross_residual(q):
                if q == 0:
                    pe.wait_ge(act_x1_T, B - 1)
                if q >= 2:
                    pe.wait_ge(act_x2, q - 1)
                mm(bank[cross_bank[q % 2]][:], idf, x1_s[:, 2 * q:2 * q + 2, :].rearrange("p b d -> p (b d)"),
                   start=True, stop=False, skip_group_check=True)

            tiles = lambda b: 0 <= b < B

            def attention(n):
                if 0 <= n < NC * B:
                    scores(n)
                if 0 <= n - 2 < NC * B:
                    prob_transpose(n - 2)
                if 0 <= n - 3 < NC * B:
                    weigh_values(n - 3)

            pe.wait_ge(ld_identity, 16)
            front_transpose(0)
            pe.wait_ge(ld_w_m, 16)
            front_project(0)
            ctx_part(0, 0)
            ctx_part(0, 1)
            latent_transpose(0)
            ctx_part(0, 2)
            pe.wait_ge(ld_w_q, 16)
            pe.wait_ge(ld_w_kv, 16)
            front_transpose(1)
            keys_values(0)
            ctx_part(1, 0)
            front_project(1)
            qk_transpose(0)
            ctx_part(1, 1)
            latent_transpose(1)
            ctx_part(1, 2)
            pe.wait_ge(ld_table_b, 16)
            pe.wait_ge(act_ctx_keys, 4)
            for i in range(B):
                if i == 2:
                    pe.wait_ge(ld_w_out, 16)
                    pe.wait_ge(ld_wg_wo, 48)
                attention(NC * i)
                if tiles(i + 1):
                    keys_values(i + 1)
                if tiles(i + 2):
                    front_transpose(i + 2)
                if i == 0:
                    pe.wait_ge(act_ctx_values, 4)
                attention(NC * i + 1)
                if tiles(i - 2):
                    out_project(i - 2)
                if tiles(i + 2):
                    front_project(i + 2)
                attention(NC * i + 2)
                if tiles(i + 1):
                    qk_transpose(i + 1)
                if tiles(i - 2):
                    cross_transpose(i - 2)
                if tiles(i - 3):
                    cross_scores(i - 3)
                if i == B - 2:
                    gates(0, 0)
                attention(NC * i + 3)
                if i == B - 2:
                    gates(0, 1)
                if i == B - 1:
                    gates(1, 0)
                if tiles(i - 1):
                    out_transpose(i - 1)
                if tiles(i + 2):
                    latent_transpose(i + 2)
                if tiles(i - 2):
                    cross_queries(i - 2)
            out_project(B - 2)
            attention(NC * B)
            attention(NC * B + 1)
            attention(NC * B + 2)
            cross_scores(B - 3)
            cross_transpose(B - 2)
            gates(1, 1)
            out_transpose(B - 1)
            cross_queries(B - 2)
            out_project(B - 1)
            cross_scores(B - 2)
            gates(2, 0)
            gates(2, 1)
            cross_transpose(B - 1)
            cross_queries(B - 1)
            gates(3, 0)
            cross_scores(B - 1)
            cross_residual(0)

            def cross_mix(q):
                pe.wait_ge(dve_decayed, 1)
                o = bank[mix_bank[q]][:].rearrange("p (b h e) -> p b h e", b=2, h=XH)
                for h in range(XH):
                    last = mm(o[:, :, h, :], aT[:, h, :], cv_s[:, 2 * q:2 * q + 2, h, :],
                              start=h == 0, stop=h == XH - 1, skip_group_check=True)
                last.then_inc(pe_mix, 1)

            def mix_transpose(q):
                pe.wait_ge(dve_mix_normed, q + 1)
                pe.wait_ge(act_mix_T, q) if q else pe.wait_ge(act_gates, 3)
                for b in range(2):
                    for k in range(KD):
                        last = tr(bank[2][:, (2 * k + b) * T:(2 * k + b + 1) * T],
                                  yh[q % 2][:, b, k * 128:(k + 1) * 128], idf)
                last.then_inc(pe_mix_T, 1)

            def cross_out(q):
                pe.wait_ge(pool_gated, q + 1)
                for b in range(2):
                    for k in range(KD):
                        last = mm(bank[cross_bank[q % 2]][:, b * D:(b + 1) * D], zT[q % 2][:, k, b, :], wo_s[:, k, :],
                                  start=False, stop=b == 1 and k == KD - 1, skip_group_check=True)
                last.then_inc(pe_cross_out, 1)

            def ffn_transpose(q):
                pe.wait_ge(dve_ffn_in, q + 1)
                if q >= 1:
                    pe.wait_ge(act_ffn_in_T, q)
                for b in range(2):
                    for k in range(KD):
                        last = tr(bank[4][:, (2 * k + b) * T:(2 * k + b + 1) * T],
                                  x1_s[:, 2 * q + b, k * 128:(k + 1) * 128], idf)
                last.then_inc(pe_ffn_in_T, 1)

            def router(q):
                pe.wait_ge(act_ffn_in_T, q + 1)
                for b in (2 * q, 2 * q + 1):
                    for k in range(KD):
                        last = mm(bank[5][:, b * E:(b + 1) * E], xfT[:, k, b, :], gate_s[:, k, :],
                                  start=k == 0, stop=k == KD - 1)
                last.then_inc(pe_logits, 1)

            def shared_gate(b):
                pe.wait_ge(act_ffn_in_T, b // 2 + 1)
                pe.wait_ge(dve_shared_hidden, b - 1) if b >= 2 else pe.wait_ge(act_x2, (b + 1) * PAIRS // 2)
                for k in range(KD):
                    last = mm(bank[shared_bank[b % 2][0]][:, 0:SI], xfT[:, k, b, :], sgu_s[:, k, 0:SI],
                              start=k == 0, stop=k == KD - 1)
                last.then_inc(pe_shared_gate, 1)

            def shared_up(b):
                for k in range(KD):
                    last = mm(bank[shared_bank[b % 2][1]][:, 0:SI], xfT[:, k, b, :], sgu_s[:, k, SI:2 * SI],
                              start=k == 0, stop=k == KD - 1)
                last.then_inc(pe_shared_up, 1)

            def shared_transpose(b):
                pe.wait_ge(dve_shared_hidden, b + 1)
                pe.wait_ge(act_shared_T, b) if b else pe.wait_ge(act_ffn_in_T, PAIRS)
                for k in range(3):
                    r = min(128, SI - k * 128)
                    last = tr(bank[4][0:r, k * T:(k + 1) * T], sh[:, b % 2, k * 128:k * 128 + r], idf)
                last.then_inc(pe_shared_T, 1)

            def shared_down(b):
                pe.wait_ge(act_shared_T, b + 1)
                if b >= 1:
                    pe.wait_ge(dve_shared_added, b)
                for k in range(3):
                    r = min(128, SI - k * 128)
                    last = mm(bank[0][:, 0:D], shT[0:r, b % 2, k, :], sdn_s[0:r, k, :], start=k == 0, stop=k == 2)
                last.then_inc(pe_shared_down, 1)

            def count_pairs():
                pe.wait_ge(dve_top2, 1)
                pe.wait_ge(set_ones, 1)
                rank = bank[2][:, 0:B * E]
                for t in range(B - 1):
                    mm(rank[:, (t + 1) * E:].rearrange("p (t e) -> p t e", e=E), onesb[:],
                       mb[:, t:t + 1, :].to_broadcast([128, B - 1 - t, E]), start=t == 0, stop=False,
                       skip_group_check=True)
                mm(rank, trib, mb[:].rearrange("p t e -> p (t e)"), start=False, stop=True, skip_group_check=True)
                for t in range(B):
                    last = mm(bank[2][:, B * E:(B + 1) * E], onesb[:], mb[:, t, :], start=t == 0, stop=t == B - 1)
                last.then_inc(pe_counts, 1)

            def slot_table():
                pe.wait_ge(dve_slot_hot, 1)
                pe.wait_ge(pool_block_numbers, 1)
                for k in range(2):
                    for t in range(B):
                        for f in range(2):
                            last = mm(bank[5][:, k * BLOCKS:(k + 1) * BLOCKS], hot[:, k * B + t, :],
                                      num_b[:, f, k * B + t, :], start=t == 0 and f == 0, stop=t == B - 1 and f == 1)
                last.then_inc(pe_slot_table, 1)

            def block_transpose(slot, nth, i):
                pe.wait_ge(dma_gathered[slot], 16 * nth + 16)
                if not (isinstance(i, int) and i < 2):
                    pe.wait_ge(dve_block_T, i - 1)
                for k in range(KD):
                    last = tr(bank[6 + slot % 2][:, k * T:(k + 1) * T], bx[:, slot, k * 128:(k + 1) * 128], idf)
                last.then_inc(pe_block_T, 1)

            def hidden_transpose(i, par):
                pe.wait_ge(dve_hidden, i + 1)
                if not (isinstance(i, int) and i == 0):
                    pe.wait_ge(act_hidden_T, i)
                for k in range(2):
                    last = tr(bank[1][0:IH, k * T:(k + 1) * T], bh[:, par, k * IH:(k + 1) * IH], idf)
                last.then_inc(pe_hidden_T, 1)

            def expert_up(i, par, e):
                pe.wait_ge(dve_block_T, i + 1)
                if not (isinstance(i, int) and i < 2):
                    pe.wait_ge(dve_hidden, i - 1)
                for k in range(KD):
                    last = mm(bank[2 + par][:, 0:2 * I], bxT[:, par, k, :], gu_s[:, k, bass.ds(e, 1), :],
                              start=k == 0, stop=k == KD - 1)
                last.then_inc(pe_expert_up, 1)

            def expert_down(i, par, e):
                pe.wait_ge(act_hidden_T, i + 1)
                for k in range(2):
                    last = mm(bank[4 + par][:, 0:D], bhT[:, par, k, :], dn_s[:, k, bass.ds(e, 1), :],
                              start=k == 0, stop=k == 1)
                last.then_inc(pe_expert_down, 1)

            expert_reg = [pe.alloc_register(f"expert{j}") for j in range(RB)]

            def read_expert(i, slot):
                pe.reg_load(expert_reg[slot], bei[0:1, bass.ds(i, 1)])

            def expert(slot):
                return pe.snap(expert_reg[slot], min_val=0, max_val=E - 1)

            def step(i, j, nth):
                par = j % 2
                block_transpose((j + 3) % RB, nth + (j + 3) // RB, i + 1)
                expert_up(i, par, expert((j + 2) % RB))
                read_expert(i + 1, (j + 3) % RB)
                hidden_transpose(i - 1, 1 - par)
                expert_down(i - 2, par, expert(j % RB))

            pe.wait_ge(ld_gate, 16)
            for q in range(PAIRS):
                cross_mix(q)
            gates(3, 1)
            mix_transpose(0)
            cross_residual(1)
            mix_transpose(1)
            cross_out(0)
            mix_transpose(2)
            cross_out(1)
            mix_transpose(3)
            cross_residual(2)
            cross_out(2)
            pe.wait_ge(act_gates, PAIRS)
            ffn_transpose(0)
            cross_residual(3)
            cross_out(3)
            pe.wait_ge(ld_shared, 48)
            shared_gate(0)
            ffn_transpose(1)
            router(0)
            shared_up(0)
            ffn_transpose(2)
            router(1)
            ffn_transpose(3)
            shared_gate(1)
            router(2)
            router(3)
            for b in range(EARLY):
                shared_transpose(b)
                if b + 1 < EARLY:
                    shared_up(b + 1)
                if b == 1:
                    count_pairs()
                if b == EARLY - 1:
                    pe.wait_ge(dve_block_experts, 1)
                    read_expert(0, 0)
                    read_expert(1, 1)
                shared_down(b)
                if b == 3:
                    slot_table()
                if b + 2 < EARLY:
                    shared_gate(b + 2)
            read_expert(2, 2)
            block_transpose(0, 0, 0)
            block_transpose(1, 0, 1)
            pe.wait_ge(ld_gate_up, 16 * 8)
            pe.wait_ge(ld_down, 16 * 4)
            expert_up(0, 0, expert(0))
            block_transpose(2, 0, 2)
            expert_up(1, 1, expert(1))
            hidden_transpose(0, 0)
            FULL = (BLOCKS - 3) // RB
            with pe.Fori(0, FULL) as nth:
                for j in range(RB):
                    step(nth * RB + (j + 2), j, nth)
            for i in range(RB * FULL + 2, BLOCKS - 1):
                step(i, i - 2 - RB * FULL, FULL)
            i = BLOCKS - 1
            expert_up(i, i % 2, expert(i % RB))
            hidden_transpose(i - 1, 1 - i % 2)
            expert_down(i - 2, i % 2, expert((i - 2) % RB))
            hidden_transpose(i, i % 2)
            expert_down(i - 1, 1 - i % 2, expert((i - 1) % RB))
            pe.wait_ge(dve_expert_out, i - 1)
            expert_down(i, i % 2, expert(i % RB))

            shared_gate(EARLY)
            shared_up(EARLY)
            for b in range(EARLY, B):
                if b + 1 < B:
                    shared_gate(b + 1)
                pe.wait_ge(dve_expert_out, BLOCKS)
                shared_transpose(b)
                if b + 1 < B:
                    shared_up(b + 1)
                shared_down(b)

        @block.scalar
        def _(act):
            copy = lambda o, i: nc.scalar.activation(o, i, ACT.Copy)

            def exps(n):
                act.wait_ge(dve_row_max, n + 1)
                if n >= 2:
                    act.wait_ge(pe_probs_T, n - 1)
                for h in range(CH):
                    last = nc.scalar.activation(pr_s[:, n % 2, h, :], sc_s[:, n % 2, h, :], ACT.Exp,
                                                bias=mx[:, n % 2, h:h + 1])
                last.then_inc(act_exp, 1)

            def kv_out(b):
                act.wait_ge(pe_keys_values, b + 1)
                if b >= 2:
                    act.wait_ge(pe_qk_T, b - 1)
                if b >= 3:
                    act.wait_ge(pe_weighed, NC * (b - 2))
                copy(qk[:, b % 2, D:D + NOPE], bank[3][:, 0:NOPE])
                copy(v_s[:, b % 3, :, 0:DH], bank[3][:, NOPE:NOPE + D].rearrange("p (h d) -> p h d", h=H)).then_inc(act_keys_values, 1)

            def ot_out(b):
                act.wait_ge(pe_attn_T, b + 1)
                if b >= 2:
                    act.wait_ge(pe_attn_out, b - 1)
                copy(oT[:, b % 2, :, :].rearrange("p k t -> p (k t)"), bank[3 if b < B - 1 else 0][:, 0:D]).then_inc(act_attn_T, 1)

            def xT_out(b):
                act.wait_ge(pe_x_T, b + 1)
                if b >= 2:
                    act.wait_ge(pe_latents, b - 1)
                copy(xT[:, b % 2, :, :].rearrange("p k t -> p (k t)"), bank[5][:, 0:D]).then_inc(act_x_T, 1)

            def qkT_out(b):
                act.wait_ge(pe_qk_T, b + 1)
                if b >= 2:
                    act.wait_ge(pe_scores, NC * (b - 1))
                    act.wait_ge(pool_keys_spread, 2 * (b - 1))
                copy(qkT[:, b % 2, :, :].rearrange("p k t -> p (k t)"), bank[5][:, 0:4 * T]).then_inc(act_qk_T, 1)

            def prT_out(n):
                act.wait_ge(pe_probs_T, n + 1)
                if n >= 2:
                    act.wait_ge(pe_weighed, n - 1)
                copy(prT[:, n % 2, :, :].rearrange("p k t -> p (k t)"), bank[2][:]).then_inc(act_probs_T, 1)

            def x1T_out(b):
                act.wait_ge(pe_x1_T, b + 1)
                copy(qx_s[:, b, XH:XH + KD, :].rearrange("p k t -> p (k t)"),
                     bank[3 if b < B - 1 else 0][:, 0:D]).then_inc(act_x1_T, 1)

            def queries_out(b):
                act.wait_ge(pe_cross_queries, b + 1)
                copy(qx_s[:, b, 0:XH, :].rearrange("p k t -> p (k t)"),
                     bank[5 if b < B - 1 else 1][:, 0:XH * T]).then_inc(act_cross_queries, 1)

            def gates_out(q):
                act.wait_ge(pe_gates, q + 1)
                act.wait_ge(pe_cross_scores, 2 * (q + 1))
                nc.scalar.activation(qx_s[:, 2 * q:2 * q + 2, 0:KD, :], bank[gate_bank[q]][:].rearrange("p (k b t) -> p b k t", k=KD, b=2),
                                     ACT.Relu).then_inc(act_gates, 1)

            def latents_out(b):
                act.wait_ge(pe_latents_T, b + 1)
                if b >= 2:
                    act.wait_ge(pe_queries, b - 1)
                nc.scalar.activation(cqT[:, b % 2, :], bank[4][:, 0:T], ACT.Identity, scale=lnq_s[:, 0:1], bias=lnq_s[:, 1:2])
                for k in range(2):
                    last = nc.scalar.activation(ckvT[:, b % 2, k, :], bank[4][0:KPH, (k + 1) * T:(k + 2) * T],
                                                ACT.Identity, scale=lnkv_s[:, k, 0:1], bias=lnkv_s[:, k, 1:2])
                last.then_inc(act_latents, 1)

            def ctx_out(g, step):
                if step == 0:
                    for h in range(XH):
                        act.wait_ge(pe_ctx_T, XH * g + h + 1)
                        if g:
                            act.wait_ge(pe_ctx_values, 2)
                        copy(cT[:, h, :, :].rearrange("p j t -> p (j t)"), bank[6 + h][:]).then_inc(act_ctx_T, 1)
                if step == 1:
                    for h in range(XH):
                        act.wait_ge(pe_ctx_keys, XH * g + h + 1)
                        copy(ck_s[:, h, 4 * g:4 * g + 4, :].rearrange("p j t -> p (j t)"), bank[h][:]).then_inc(act_ctx_keys, 1)
                if step == 2:
                    for j in range(2):
                        act.wait_ge(pe_ctx_values, 2 * g + j + 1)
                        copy(cv_s[:, 4 * g + 2 * j:4 * g + 2 * j + 2, :, :].rearrange("p j h t -> p (j h t)"),
                             bank[1 + j][:]).then_inc(act_ctx_values, 1)

            tiles = lambda b: 0 <= b < B

            def attention(n):
                if 0 <= n - 2 < NC * B:
                    prT_out(n - 2)
                if 0 <= n < NC * B:
                    exps(n)

            xT_out(0)
            ctx_out(0, 0)
            ctx_out(0, 1)
            act.wait_ge(ld_ln, 32)
            latents_out(0)
            ctx_out(0, 2)
            xT_out(1)
            kv_out(0)
            ctx_out(1, 0)
            qkT_out(0)
            ctx_out(1, 1)
            latents_out(1)
            ctx_out(1, 2)
            for i in range(B):
                attention(NC * i)
                if tiles(i + 1):
                    kv_out(i + 1)
                if tiles(i + 2):
                    xT_out(i + 2)
                attention(NC * i + 1)
                attention(NC * i + 2)
                if tiles(i + 1):
                    qkT_out(i + 1)
                if tiles(i - 2):
                    x1T_out(i - 2)
                if i >= 0:
                    prT_out(NC * i + 1)
                if tiles(i - 1):
                    ot_out(i - 1)
                if tiles(i + 2):
                    latents_out(i + 2)
                exps(NC * i + 3)
                if i == B - 2:
                    gates_out(0)
                if tiles(i - 2):
                    queries_out(i - 2)
            attention(NC * B)
            attention(NC * B + 1)
            x1T_out(B - 2)
            gates_out(1)
            ot_out(B - 1)
            queries_out(B - 2)
            gates_out(2)
            x1T_out(B - 1)
            queries_out(B - 1)
            gates_out(3)

            def yT_out(q):
                act.wait_ge(pe_mix_T, q + 1)
                if q >= 2:
                    act.wait_ge(pool_gated, q - 1)
                for k in range(KD):
                    last = nc.scalar.activation(yT[q % 2][:, k, :, :].rearrange("p b t -> p (b t)"),
                                                bank[2][:, 2 * k * T:2 * (k + 1) * T],
                                                ACT.Identity, scale=gn_s[:, k, 0:1], bias=gn_s[:, k, 1:2])
                last.then_inc(act_mix_T, 1)

            def xfT_out(q):
                act.wait_ge(pe_ffn_in_T, q + 1)
                copy(xfT[:, :, 2 * q:2 * q + 2, :], bank[4][:].rearrange("p (k b t) -> p k b t", k=KD, b=2)).then_inc(act_ffn_in_T, 1)

            def x2_out(q):
                act.wait_ge(pe_cross_out, q + 1)
                copy(x_s[:, 2 * q:2 * q + 2, :].rearrange("p b d -> p (b d)"), bank[cross_bank[q % 2]][:]).then_inc(act_x2, 1)

            def shared_silu(b):
                act.wait_ge(pe_shared_gate, b + 1)
                if b >= 2:
                    act.wait_ge(dve_shared_hidden, b - 1)
                nc.scalar.activation(sg[:, b % 2, :], bank[shared_bank[b % 2][0]][:, 0:SI], ACT.Silu).then_inc(act_shared_silu, 1)

            def shT_out(b):
                act.wait_ge(pe_shared_T, b + 1)
                if b >= 2:
                    act.wait_ge(pe_shared_down, b - 1)
                copy(shT[:, b % 2, 0:2, :].rearrange("p k t -> p (k t)"), bank[4][:, 0:2 * T])
                copy(shT[0:SI - 256, b % 2, 2, :], bank[4][0:SI - 256, 2 * T:3 * T]).then_inc(act_shared_T, 1)

            yT_out(0)
            yT_out(1)
            x2_out(0)
            yT_out(2)
            x2_out(1)
            yT_out(3)
            x2_out(2)
            xfT_out(0)
            x2_out(3)
            xfT_out(1)
            shared_silu(0)
            xfT_out(2)
            xfT_out(3)
            act.wait_ge(dve_logits, 1)
            nc.scalar.activation(ex, lg, ACT.Exp).then_inc(act_router_exp, 1)
            shT_out(0)
            shared_silu(1)
            for b in range(EARLY):
                if b >= 1:
                    shT_out(b)
                if b + 2 < EARLY:
                    shared_silu(b + 2)

            def silu(i, par, first=False):
                act.wait_ge(pe_expert_up, i + 1)
                if not first:
                    act.wait_ge(dve_hidden, i - 1)
                nc.scalar.activation(bs[:, par, :], bank[2 + par][:, 0:I], ACT.Silu).then_inc(act_expert_silu, 1)

            def hT_out(i, par, first=False):
                act.wait_ge(pe_hidden_T, i + 1)
                if not first:
                    act.wait_ge(pe_expert_down, i - 1)
                copy(bhT[:, par, :, :].rearrange("p k t -> p (k t)"), bank[1][0:IH, 0:2 * T]).then_inc(act_hidden_T, 1)

            silu(0, 0, True)
            hT_out(0, 0, True)
            silu(1, 1, True)
            hT_out(1, 1, True)
            with act.Fori(2, BLOCKS - 1, 2) as i:
                silu(i, 0)
                hT_out(i, 0)
                silu(i + 1, 1)
                hT_out(i + 1, 1)
            silu(BLOCKS - 1, 0)
            hT_out(BLOCKS - 1, 0)
            shared_silu(EARLY)
            for b in range(EARLY, B):
                if b + 1 < B:
                    shared_silu(b + 1)
                shT_out(b)
            for t in range(B):
                act.wait_ge(dve_second_sum, t + 1)
                act.dma_start(out[t, :, :], x_s[:, t, :]).then_inc(dma_out, 16)

        @block.vector
        def _(dve):
            V = nc.vector
            count = [0]

            def link(ins):
                count[0] += 1
                ins.then_inc(chain, 1)
                dve.wait_ge(chain, count[0])

            def variance(kind, b, src, eps, done):
                link(V.bn_stats(st[:, 0, :], src))
                link(V.bn_aggr(ag[:, kind, b % 2, :], st[:, 0, :]))
                V.tensor_scalar_add(ve[:, kind, b % 2, :], ag[:, kind, b % 2, 1:2], eps).then_inc(done, 1)

            def normalize(kind, b, o, src):
                return V.tensor_scalar(o, src, ag[:, kind, b % 2, 0:1], rs[:, kind, b % 2, :], ALU.subtract, ALU.mult)

            def x_variance(b):
                dve.wait_ge(ld_x[xpart(b)], 16)
                variance(LX, b, x_s[:, b, :], LN_EPS, dve_x_var)

            def x_normalize(b):
                dve.wait_ge(pool_x_rstd, b + 1)
                if b >= 2:
                    dve.wait_ge(pe_x_T, b - 1)
                normalize(LX, b, xh[:, b % 2, :], x_s[:, b, :]).then_inc(dve_x_normed, 1)

            def mask_max(n):
                s = bank[n % 2][:].rearrange("p (h k) -> p h k", h=CH)
                dve.wait_ge(pe_scores, n + 1)
                if n >= 2:
                    dve.wait_ge(act_exp, n - 1)
                V.scalar_tensor_tensor(sc_s[:, n % 2, :, :], s, DH ** -0.5, maskb.unsqueeze(1).to_broadcast([128, CH, T]),
                                       ALU.mult, ALU.add).then_inc(dve_masked, 1)
                dve.wait_ge(dve_masked, n + 1)
                V.tensor_reduce(mx[:, n % 2, :], sc_s[:, n % 2, :, :], op=ALU.max, axis=AX.X, negate=True).then_inc(dve_row_max, 1)

            def rope(par, which, src, dst, done):
                t = rope_t[:, par, which, :]
                link(V.tensor_tensor(t, src, tab[:, C_ROPE:C_ROPE + 2 * ROPE], ALU.mult))
                V.tensor_tensor(dst, t[:, 0:ROPE], t[:, ROPE:2 * ROPE], ALU.add).then_inc(done, 1)

            def q_out(b):
                dve.wait_ge(pe_queries, b + 1)
                if b >= 2:
                    dve.wait_ge(pe_qk_T, b - 1)
                link(V.tensor_copy(qk[:, b % 2, 0:NOPE], bank[4][:, 0:NOPE]))
                rope(b % 2, 0, bank[4][:, NOPE:NOPE + 2 * ROPE], qk[:, b % 2, NOPE:D], dve_queries)

            def latent_variance(b):
                dve.wait_ge(pe_latents, b + 1)
                V.bn_stats(st[:, 0, :], bank[4][:, 0:QP])
                link(V.bn_stats(st[:, 1, :], bank[4][:, QP:QP + KP]))
                V.bn_aggr(ag2[:, b % 2, 0, :], st[:, 0, :])
                link(V.bn_aggr(ag2[:, b % 2, 1, :], st[:, 1, :]))
                V.tensor_scalar_add(ve2[:, b % 2, :], ag2[:, b % 2, :, 1], LN_EPS).then_inc(dve_latents_var, 1)

            def latent_normalize(b):
                if b >= 2:
                    dve.wait_ge(pe_latents_T, b - 1)
                    dve.wait_ge(pe_qk_T, b - 1)
                dve.wait_ge(pool_latents_rstd, b + 1)
                for j, (lo, hi) in enumerate(((0, QP), (QP, QP + KP))):
                    V.tensor_scalar(lat[:, b % 2, lo:hi], bank[4][:, lo:hi], ag2[:, b % 2, j, 0:1],
                                    rs2[:, b % 2, j:j + 1], ALU.subtract, ALU.mult)
                rope(b % 2, 1, bank[4][:, QP + KP:MW], qk[:, b % 2, D + NOPE:2 * D], dve_latents_normed)

            def out_normalize(b):
                o = bank[6][:, 0:H * (DH + 1)].rearrange("p (h d) -> p h d", h=H)
                dve.wait_ge(pe_weighed, NC * (b + 1))
                link(V.reciprocal(rden[:, b % 2, :], o[:, :, DH]))
                if b >= 2:
                    dve.wait_ge(pe_attn_T, b - 1)
                V.tensor_tensor(o_s[:, b % 2, :].rearrange("p (h d) -> p h d", h=H), o[:, :, 0:DH],
                                rden[:, b % 2, :].unsqueeze(2).to_broadcast([128, H, DH]), ALU.mult).then_inc(dve_attn_normed, 1)

            def residual_attention(b):
                dve.wait_ge(pe_attn_out, b + 1)
                V.tensor_tensor(x1_s[:, b, :], bank[3 if b < B - 1 else 0][:, 0:D], x_s[:, b, :], ALU.add).then_inc(dve_x1, 1)
                dve.wait_ge(dve_x1, b + 1)
                variance(LX1, b, x1_s[:, b, :], LN_EPS, dve_x1_var)

            def x1_normalize(b):
                dve.wait_ge(pool_x1_rstd, b + 1)
                if b >= 2:
                    dve.wait_ge(pe_x1_T, b - 1)
                normalize(LX1, b, xb[:, b % 2, :], x1_s[:, b, :]).then_inc(dve_x1_normed, 1)

            V.memset(onesb[:], 1.0).then_inc(set_ones, 1)
            x_variance(0)
            x_normalize(0)
            dve.wait_ge(ld_table, 16)
            dve.wait_ge(ld_table_b, 16)
            tiles = lambda b: 0 <= b < B

            def chunk(n):
                if 0 <= n < NC * B:
                    mask_max(n)

            for i in range(-2, B):
                chunk(NC * i)
                if 0 < i + 2 < B:
                    x_normalize(i + 2)
                if tiles(i + 1):
                    q_out(i + 1)
                chunk(NC * i + 1)
                if tiles(i - 2):
                    residual_attention(i - 2)
                    x1_normalize(i - 2)
                chunk(NC * i + 2)
                if tiles(i + 2):
                    latent_variance(i + 2)
                if tiles(i - 1):
                    out_normalize(i - 1)
                if tiles(i + 2):
                    latent_normalize(i + 2)
                chunk(NC * i + 3)
                if 0 < i + 3 < B:
                    x_variance(i + 3)
            residual_attention(B - 2)
            x1_normalize(B - 2)
            out_normalize(B - 1)
            residual_attention(B - 1)
            x1_normalize(B - 1)

            dve.wait_ge(pe_cross_scores, B)
            link(V.tensor_tensor(atmp, bank[7][:, 0:XH * T].rearrange("p (h t) -> p h t", h=XH),
                                 tab[:, C_DECAY:C_DECAY + XH * T].rearrange("p (h t) -> p h t", h=XH), ALU.mult))
            link(V.scalar_tensor_tensor(aT, atmp, -1.0, atmp, ALU.mult, ALU.max))
            V.tensor_scalar_max(aT, aT, 1.0).then_inc(dve_decayed, 1)

            def variance_pair(kind, q, src, eps, done):
                V.bn_stats(st[:, 0, :], src[:, 0, :])
                link(V.bn_stats(st[:, 1, :], src[:, 1, :]))
                V.bn_aggr(agp[:, kind, q % 2, 0, :], st[:, 0, :])
                link(V.bn_aggr(agp[:, kind, q % 2, 1, :], st[:, 1, :]))
                V.tensor_scalar_add(vep[:, kind, q % 2, :], agp[:, kind, q % 2, :, 1], eps).then_inc(done, 1)

            def normalize_pair(kind, q, o, src):
                for b in range(2):
                    last = V.tensor_scalar(o[:, b, :], src[:, b, :], agp[:, kind, q % 2, b, 0:1],
                                           rsp[:, kind, q % 2, b:b + 1], ALU.subtract, ALU.mult)
                return last

            mixed = lambda q: bank[mix_bank[q]][:].rearrange("p (b d) -> p b d", b=2)

            def mix_variance(q):
                dve.wait_ge(pe_mix, q + 1)
                if q >= 2:
                    dve.wait_ge(dve_mix_normed, q - 1)
                variance_pair(MIX, q, mixed(q), GN_EPS, dve_mix_var)

            def mix_normalize(q):
                dve.wait_ge(pool_mix_rstd, q + 1)
                if q >= 2:
                    dve.wait_ge(pe_mix_T, q - 1)
                normalize_pair(MIX, q, yh[q % 2][:], mixed(q)).then_inc(dve_mix_normed, 1)

            def ffn_variance(q):
                dve.wait_ge(act_x2, q + 1)
                if q >= 2:
                    dve.wait_ge(dve_ffn_in, q - 1)
                variance_pair(FFN, q, x_s[:, 2 * q:2 * q + 2, :], LN_EPS, dve_x2_var)

            def ffn_normalize(q):
                dve.wait_ge(pool_x2_rstd, q + 1)
                normalize_pair(FFN, q, x1_s[:, 2 * q:2 * q + 2, :], x_s[:, 2 * q:2 * q + 2, :]).then_inc(dve_ffn_in, 1)

            def shared_mul(b):
                dve.wait_ge(act_shared_silu, b + 1)
                dve.wait_ge(pe_shared_up, b + 1)
                if b >= 2:
                    dve.wait_ge(pe_shared_T, b - 1)
                V.tensor_tensor(sh[:, b % 2, :], bank[shared_bank[b % 2][1]][:, 0:SI], sg[:, b % 2, :],
                                ALU.mult).then_inc(dve_shared_hidden, 1)

            def shared_add(b):
                dve.wait_ge(pe_shared_down, b + 1)
                V.tensor_tensor(x_s[:, b, :], bank[0][:, 0:D], x_s[:, b, :], ALU.add).then_inc(dve_shared_added, 1)

            mix_variance(0)
            mix_variance(1)
            mix_normalize(0)
            mix_normalize(1)
            mix_variance(2)
            mix_variance(3)
            mix_normalize(2)
            mix_normalize(3)
            ffn_variance(0)
            ffn_variance(1)
            ffn_normalize(0)
            ffn_variance(2)
            ffn_normalize(1)
            ffn_variance(3)
            ffn_normalize(2)
            ffn_normalize(3)

            iota = tab[:, C_IOTA:C_IOTA + E].unsqueeze(1).to_broadcast([128, B, E])
            wide = lambda s: s.unsqueeze(2).to_broadcast([128, B, E])
            top_w, top_i = [s8[:, 0, :], s8[:, 1, :]], [s8[:, 2, :], s8[:, 3, :]]
            shared_mul(0)
            dve.wait_ge(pe_logits, PAIRS)
            logits = bank[5][:, 0:B * E].rearrange("p (t e) -> p t e", e=E)
            link(V.reduce_max(s8[:, 4, :], logits, AX.X))
            V.tensor_tensor(lg, logits, wide(s8[:, 4, :]), ALU.subtract).then_inc(dve_logits, 1)
            dve.wait_ge(act_router_exp, 1)
            link(V.reduce_sum(s8[:, 5, :], ex, AX.X))
            link(V.reciprocal(s8[:, 6, :], s8[:, 5, :]))
            link(V.tensor_tensor(prob, ex, wide(s8[:, 6, :]), ALU.mult))

            def best(k):
                link(V.reduce_max(top_w[k], prob, AX.X))
                link(V.tensor_tensor(t128[:, 0], prob, wide(top_w[k]), ALU.is_lt))
                link(V.scalar_tensor_tensor(t128[:, 1], t128[:, 0], float(E), iota, ALU.mult, ALU.add))
                link(V.tensor_reduce(top_i[k], t128[:, 1], op=ALU.min, axis=AX.X))
                link(V.tensor_tensor(oh[:, k], iota, wide(top_i[k]), ALU.is_equal))

            best(0)
            shared_mul(1)
            link(V.scalar_tensor_tensor(prob, oh[:, 0], -2.0, prob, ALU.mult, ALU.add))
            best(1)
            V.tensor_tensor(mb[:], oh[:, 0], oh[:, 1], ALU.add).then_inc(dve_top2, 1)
            shared_add(0)
            shared_mul(2)

            dve.wait_ge(pe_counts, 1)
            dve.wait_ge(ld_table_r, 16)
            c = cmp[:, :, 0:B]
            link(V.tensor_tensor(c, bank[2][:, B * E:(B + 1) * E].unsqueeze(2).to_broadcast([128, E, B]),
                                 tabr[:, R_THR:R_THR + B].unsqueeze(1).to_broadcast([128, E, B]), ALU.is_gt))
            link(V.reduce_sum(nb[:, 0, :], c, AX.X))
            link(V.tensor_tensor(cmp, nb[:, 0, :].unsqueeze(1).to_broadcast([128, E, E]),
                                 tabr[:, R_LOW:R_LOW + E * E].rearrange("p (a b) -> p a b", a=E), ALU.mult))
            link(V.reduce_sum(nb[:, 1, :], cmp, AX.X))
            link(V.tensor_scalar_mul(nb[:, 2, :], nb[:, 1, :], float(T)))
            shared_add(1)
            link(V.tensor_tensor(t128[:, 0], bank[2][:, 0:B * E].rearrange("p (t e) -> p t e", e=E),
                                 nb[:, 2, :].unsqueeze(1).to_broadcast([128, B, E]), ALU.add))
            link(V.tensor_tensor(ohp, t128[:, 0:1].to_broadcast([128, 2, B, E]), oh, ALU.mult))
            link(V.reduce_sum(posf[:, 0, :], ohp.rearrange("p k t e -> p (k t) e"), AX.X))
            link(V.tensor_copy(posi[:, 0, :], posf[:, 0, :]))
            V.tensor_single_scalar(posi[:, 1, :], posi[:, 0, :], T - 1, op=ALU.bitwise_and)
            link(V.tensor_single_scalar(posi[:, 2, :], posi[:, 0, :], T.bit_length() - 1, op=ALU.logical_shift_right))
            link(V.tensor_copy(posf[:, 1:3, :], posi[:, 1:3, :]))
            shared_mul(3)
            shared_add(2)
            V.tensor_tensor(num, tabr[:, R_BLK:R_BLK + BLOCKS].unsqueeze(1).to_broadcast([128, 2 * B, BLOCKS]),
                                 posf[:, 2, :].unsqueeze(2).to_broadcast([128, 2 * B, BLOCKS]), ALU.is_equal).then_inc(dve_block_hot, 1)
            V.tensor_tensor(hot, tabr[:, R_SLOT:R_SLOT + T].unsqueeze(1).to_broadcast([128, 2 * B, T]),
                            posf[:, 1, :].unsqueeze(2).to_broadcast([128, 2 * B, T]), ALU.is_equal).then_inc(dve_slot_hot, 1)
            shared_mul(4)
            shared_add(3)
            link(V.tensor_tensor(bcmp, nb[0:1, 1, :].unsqueeze(1).to_broadcast([1, BLOCKS, E]),
                                 tabr[0:1, R_BLK:R_BLK + BLOCKS].unsqueeze(2).to_broadcast([1, BLOCKS, E]), ALU.is_le))
            link(V.reduce_sum(be[:, 0, :], bcmp, AX.X))
            V.tensor_scalar_add(bei[:], be[:, 0, :], -1.0).then_inc(dve_block_experts, 1)
            dve.wait_ge(pe_slot_table, 1)
            best_n, second_n = bank[5][:, 0:BLOCKS], bank[5][:, BLOCKS:2 * BLOCKS]
            link(V.tensor_copy(ids[:, 0, :], second_n))
            link(V.tensor_tensor(ids[:, 1, :], best_n, ids[:, 0, :], ALU.add))
            link(V.tensor_scalar(ids[:, 2, :], ids[:, 0, :], 0.0, float(B * T), ALU.is_gt, ALU.mult))
            V.tensor_scalar(idx[:, 0, :], ids[:, 1, :], -1.0, 0.0, ALU.add, ALU.max)
            link(V.scalar_tensor_tensor(ids[:, 3, :], ids[:, 1, :], 0.0, tabr[:, R_DUMMY:R_DUMMY + BLOCKS],
                                        ALU.is_equal, ALU.mult))
            link(V.tensor_tensor(ids[:, 3, :], ids[:, 3, :], ids[:, 2, :], ALU.add))
            V.scalar_tensor_tensor(idx[:, 1, :], ids[:, 3, :], -1.0, ids[:, 1, :], ALU.add, ALU.add).then_inc(dve_rows, 1)
            shared_mul(5)
            shared_add(4)
            shared_add(5)

            def bT_out(i, par, first=False):
                dve.wait_ge(pe_block_T, i + 1)
                if not first:
                    dve.wait_ge(pe_expert_up, i - 1)
                V.tensor_copy(bxT[:, par, :, :].rearrange("p k t -> p (k t)"), bank[6 + par][:, 0:D]).then_inc(dve_block_T, 1)

            def h_mul(i, par, first=False):
                dve.wait_ge(act_expert_silu, i + 1)
                if not first:
                    dve.wait_ge(pe_hidden_T, i - 1)
                V.tensor_tensor(bh[:, par, :], bank[2 + par][:, I:2 * I], bs[:, par, :], ALU.mult).then_inc(dve_hidden, 1)

            def y_out(i, par, slot, nth):
                dve.wait_ge(pe_expert_down, i + 1)
                if not (isinstance(i, int) and i < RB):
                    dve.wait_ge(dma_scattered[slot], 16 * nth)
                V.tensor_copy(by[:, slot, :], bank[4 + par][:, 0:D]).then_inc(dve_expert_out, 1)

            bT_out(0, 0, True)
            bT_out(1, 1, True)
            h_mul(0, 0, True)
            bT_out(2, 0)
            h_mul(1, 1, True)
            for i in range(2, RB + 2):
                bT_out(i + 1, (i + 1) % 2)
                y_out(i - 2, i % 2, i - 2, 0)
                h_mul(i, i % 2)
            FULL = (BLOCKS - 3 - RB) // RB
            with dve.Fori(0, FULL) as n:
                for j in range(RB):
                    i = n * RB + (j + RB + 2)
                    bT_out(i + 1, (j + 1) % 2)
                    y_out(i - 2, j % 2, j, n + 1)
                    h_mul(i, j % 2)
            for i in range(RB * (FULL + 1) + 2, BLOCKS + 2):
                if i + 1 < BLOCKS:
                    bT_out(i + 1, (i + 1) % 2)
                if i < BLOCKS:
                    h_mul(i, i % 2)
                y_out(i - 2, i % 2, (i - 2) % RB, (i - 2) // RB)

            shared_mul(EARLY)
            shared_mul(EARLY + 1)

            for t in range(0, B, 2):
                if t == 2:
                    shared_add(EARLY)
                if t == EARLY:
                    shared_add(EARLY + 1)
                    dve.wait_ge(dve_shared_added, B)
                for k in range(2):
                    for u in (t, t + 1):
                        dve.wait_ge(dve_first_sum, u + 1) if k else dve.wait_ge(dma_token_outputs[u], 16)
                        V.scalar_tensor_tensor(x_s[:, u, :], yg[u][:, k, :], top_w[k][:, u:u + 1], x_s[:, u, :],
                                               ALU.mult, ALU.add).then_inc(dve_second_sum if k else dve_first_sum, 1)


def kernel(**inputs):
    import numpy as _np
    import concourse.bacc as _bacc
    from concourse import mybir as _mybir
    from concourse.bass_utils import run_bass_kernel_spmd as _run

    g = {k: _np.asarray(v) for k, v in inputs.items()}

    def swapped(w):
        return w.reshape(w.shape[0], -1, 2, DH // 2)[:, :, ::-1, :].reshape(w.shape)

    a = "L0_attn_"
    arrays = {
        "x": g["x"],
        "ctx_in": g["ctx_2048"],
        "table": constants(),
        "table_b": bf16_constants(),
        "table_r": routing_constants(),
        "w_m": _np.concatenate([g[a + "W_dq"], g[a + "W_dkv"], g[a + "W_kr"], swapped(g[a + "W_kr"])], 1),
        "w_q": _np.concatenate([g[a + "W_uq"], g[a + "W_qr"], swapped(g[a + "W_qr"])], 1),
        "w_kv": g[a + "W_ukv"],
        "w_out": g[a + "W_o"].T,
        "ln_q": _np.stack([g[a + "q_ln_w"], g[a + "q_ln_b"]], 1),
        "ln_kv": _np.stack([g[a + "kv_ln_w"], g[a + "kv_ln_b"]], 1),
        "wh": g["L0_xattn_Wh"],
        "wg": g["L0_xattn_wg_w"],
        "wo": g["L0_xattn_wo_w"],
        "gn": _np.stack([g["L0_xattn_gn_gamma"], g["L0_xattn_gn_beta"]], 1),
        "gate": g["L0_ffn_gate_w"].T,
        "w_gu": g["L0_ffn_w_gate_up"],
        "w_dn": g["L0_ffn_w_down"],
        "s_gu_d": g["L0_ffn_shared_gate_up"],
        "s_dn_d": g["L0_ffn_shared_down"],
    }
    nc = _bacc.Bacc("TRN2", target_bir_lowering=False, num_devices=1)
    feed, args = {}, []
    for name, v in arrays.items():
        v = _np.ascontiguousarray(v)
        feed[f"in_{name}"] = v
        args.append(nc.dram_tensor(f"in_{name}", v.shape, _mybir.dt.from_np(v.dtype), kind="ExternalInput").ap())
    args.append(nc.dram_tensor("out_0", (B, T, D), _mybir.dt.float32, kind="ExternalOutput").ap())
    decoder_layer(nc, *args)
    r = _run(nc, [feed], core_ids=[0])
    return r.results[0]["out_0"]
```
